# Optimizing a Trainium2 kernel written in Bass

```python
import numpy as np
import jax
import jax.numpy as jnp

def _softmax(x, axis=-1):
    return jax.nn.softmax(x, axis=axis)

def _gelu(x):
    return jax.nn.gelu(x, approximate=True)

def _silu(x):
    return jax.nn.silu(x)

def _sigmoid(x):
    return jax.nn.sigmoid(x)

def _layernorm(x, axis=-1, eps=1e-05):
    m = jnp.mean(x, axis=axis, keepdims=True)
    v = jnp.var(x, axis=axis, keepdims=True)
    return (x - m) / jnp.sqrt(v + eps)

def _scatter_add(tgt, idx, src, axis=0):
    return tgt.at[idx].add(src)

def _segment_sum(src, seg, n):
    return jax.ops.segment_sum(src, seg, n)
kernel_name = 'mk_prb_d2_jaxref_r4_11d51d'

def setup_inputs(seed: int=0):
    np.random.seed(seed)
    _w = jnp.asarray

    def _L0_attn_setup():
        import jax, jax.numpy as jnp
        import numpy as np
        DIM_Q = 256
        DIM_K = 256
        DIM_V = 256
        OUT_DIM = 256
        B, N = (4, 512)

        def _layer_norm(h, gamma, beta, eps=1e-05):
            mu = jnp.mean(h, axis=-1, keepdims=True)
            var = jnp.mean(jnp.square(h - mu), axis=-1, keepdims=True)
            return (h - mu) * jax.lax.rsqrt(var + eps) * gamma + beta
        key = jax.random.key(seed)
        ks = jax.random.split(key, 8)
        s_in = 1.0 / np.sqrt(DIM_Q)
        s_v = 1.0 / np.sqrt(DIM_V)
        return {'x': jax.random.normal(ks[0], (B, N, DIM_Q), dtype=jnp.float32), 'Wq': jax.random.normal(ks[1], (DIM_Q, DIM_K), dtype=jnp.float32) * s_in, 'Wk': jax.random.normal(ks[2], (DIM_Q, DIM_K), dtype=jnp.float32) * s_in, 'Wv': jax.random.normal(ks[3], (DIM_Q, DIM_V), dtype=jnp.float32) * s_in, 'Wfc': jax.random.normal(ks[4], (DIM_V, OUT_DIM), dtype=jnp.float32) * s_v, 'bfc': jax.random.normal(ks[5], (OUT_DIM,), dtype=jnp.float32) * 0.02, 'gamma': jnp.ones((DIM_V,), dtype=jnp.float32), 'beta': jnp.zeros((DIM_V,), dtype=jnp.float32)}
    _L0_attn_in = _L0_attn_setup()

    def _L0_ffn_setup():
        import jax, jax.numpy as jnp
        import numpy as np
        HIDDEN = 256
        INTER = 1024
        key = jax.random.key(seed)
        k1, k2, k3, k4, k5 = jax.random.split(key, 5)
        hidden_states = jax.random.normal(k1, (4, 512, HIDDEN), dtype=jnp.float32)
        W1 = jax.random.normal(k2, (HIDDEN, INTER), dtype=jnp.float32) * (1.0 / np.sqrt(HIDDEN))
        b1 = jax.random.normal(k3, (INTER,), dtype=jnp.float32) * 0.02
        W2 = jax.random.normal(k4, (INTER, HIDDEN), dtype=jnp.float32) * (1.0 / np.sqrt(INTER))
        b2 = jax.random.normal(k5, (HIDDEN,), dtype=jnp.float32) * 0.02
        return {'hidden_states': hidden_states, 'W1': W1, 'b1': b1, 'W2': W2, 'b2': b2}
    _L0_ffn_in = _L0_ffn_setup()

    def _L1_attn_setup():
        import jax, jax.numpy as jnp
        import numpy as np
        GROUP = 64
        MAX_REL = 32

        def _silu(x):
            return x * jax.nn.sigmoid(x)

        def _ln(x, w, b, eps=1e-05):
            m = x.mean(-1, keepdims=True)
            v = ((x - m) ** 2).mean(-1, keepdims=True)
            return (x - m) / jnp.sqrt(v + eps) * w + b

        def _rope(x):
            n, d = (x.shape[-2], x.shape[-1])
            half = d // 2
            pos = jnp.arange(n, dtype=x.dtype)
            inv_freq = 10000.0 ** (-jnp.arange(half, dtype=x.dtype) / half)
            sinusoid = pos[:, None] * inv_freq[None, :]
            sin, cos = (jnp.sin(sinusoid), jnp.cos(sinusoid))
            x1, x2 = (x[..., :half], x[..., half:])
            return jnp.concatenate([x1 * cos - x2 * sin, x2 * cos + x1 * sin], axis=-1)
        key = jax.random.key(seed)
        ks = jax.random.split(key, 8)
        B, N, D, QK, H = (4, 1024, 256, 64, 512)
        s = 0.02
        return {'x': jax.random.normal(ks[0], (B, N, D), dtype=jnp.float32), 'ln1_w': jnp.ones((D,), jnp.float32), 'ln1_b': jnp.zeros((D,), jnp.float32), 'Wqk': jax.random.normal(ks[1], (QK, D), jnp.float32) * s, 'bqk': jnp.zeros((QK,), jnp.float32), 'Wv': jax.random.normal(ks[2], (H, D), jnp.float32) * s, 'bv': jnp.zeros((H,), jnp.float32), 'Wg': jax.random.normal(ks[3], (H, D), jnp.float32) * s, 'bg': jnp.zeros((H,), jnp.float32), 'Wo': jax.random.normal(ks[4], (D, H), jnp.float32) * s, 'bo': jnp.zeros((D,), jnp.float32), 'ln2_w': jnp.ones((D,), jnp.float32), 'ln2_b': jnp.zeros((D,), jnp.float32), 'gamma': jax.random.normal(ks[5], (4, QK), jnp.float32) * 0.02, 'beta': jnp.zeros((4, QK), jnp.float32), 'pos_emb': jax.random.normal(ks[6], (2 * MAX_REL + 1,), jnp.float32)}
    _L1_attn_in = _L1_attn_setup()

    def _L1_ffn_setup():
        import jax, jax.numpy as jnp
        import numpy as np
        DIM = 256
        HID = 512
        E = 8
        K = 2
        R = 16
        B_, S_ = (2, 256)

        def _lora_in(xf, W, b, A, B):
            base = jnp.einsum('td,ehd->teh', xf, W)
            low = jnp.einsum('ter,ehr->teh', jnp.einsum('td,erd->ter', xf, A), B)
            return base + low + b

        def _lora_out(g, W, b, A, B):
            base = jnp.einsum('teh,edh->ted', g, W)
            low = jnp.einsum('ter,edr->ted', jnp.einsum('teh,erh->ter', g, A), B)
            return base + low + b
        key = jax.random.key(seed)
        ks = jax.random.split(key, 14)
        n = lambda k, shape, scale: jax.random.normal(k, shape, jnp.float32) * scale
        inp = {'x': jax.random.normal(ks[0], (B_, S_, DIM), jnp.float32), 'Wg': n(ks[1], (E, DIM), DIM ** (-0.5)), 'W1': n(ks[2], (E, HID, DIM), DIM ** (-0.5)), 'b1': jnp.zeros((E, HID), jnp.float32), 'A1': n(ks[3], (E, R, DIM), DIM ** (-0.5)), 'B1': n(ks[4], (E, HID, R), 0.01), 'W2': n(ks[5], (E, DIM, HID), HID ** (-0.5)), 'b2': jnp.zeros((E, DIM), jnp.float32), 'A2': n(ks[6], (E, R, HID), HID ** (-0.5)), 'B2': n(ks[7], (E, DIM, R), 0.01), 'W3': n(ks[8], (E, HID, DIM), DIM ** (-0.5)), 'b3': jnp.zeros((E, HID), jnp.float32), 'A3': n(ks[9], (E, R, DIM), DIM ** (-0.5)), 'B3': n(ks[10], (E, HID, R), 0.01)}
        return inp
    _L1_ffn_in = _L1_ffn_setup()
    _d = {'L0_attn_x': _L0_attn_in['x'], 'L0_attn_Wq': _L0_attn_in['Wq'], 'L0_attn_Wk': _L0_attn_in['Wk'], 'L0_attn_Wv': _L0_attn_in['Wv'], 'L0_attn_Wfc': _L0_attn_in['Wfc'], 'L0_attn_bfc': _L0_attn_in['bfc'], 'L0_attn_gamma': _L0_attn_in['gamma'], 'L0_attn_beta': _L0_attn_in['beta'], 'L0_ffn_W1': _L0_ffn_in['W1'], 'L0_ffn_b1': _L0_ffn_in['b1'], 'L0_ffn_W2': _L0_ffn_in['W2'], 'L0_ffn_b2': _L0_ffn_in['b2'], 'L1_attn_ln1_w': _L1_attn_in['ln1_w'], 'L1_attn_ln1_b': _L1_attn_in['ln1_b'], 'L1_attn_Wqk': _L1_attn_in['Wqk'], 'L1_attn_bqk': _L1_attn_in['bqk'], 'L1_attn_Wv': _L1_attn_in['Wv'], 'L1_attn_bv': _L1_attn_in['bv'], 'L1_attn_Wg': _L1_attn_in['Wg'], 'L1_attn_bg': _L1_attn_in['bg'], 'L1_attn_Wo': _L1_attn_in['Wo'], 'L1_attn_bo': _L1_attn_in['bo'], 'L1_attn_ln2_w': _L1_attn_in['ln2_w'], 'L1_attn_ln2_b': _L1_attn_in['ln2_b'], 'L1_attn_gamma': _L1_attn_in['gamma'], 'L1_attn_beta': _L1_attn_in['beta'], 'L1_attn_pos_emb': _L1_attn_in['pos_emb'], 'L1_ffn_Wg': _L1_ffn_in['Wg'], 'L1_ffn_W1': _L1_ffn_in['W1'], 'L1_ffn_b1': _L1_ffn_in['b1'], 'L1_ffn_A1': _L1_ffn_in['A1'], 'L1_ffn_B1': _L1_ffn_in['B1'], 'L1_ffn_W2': _L1_ffn_in['W2'], 'L1_ffn_b2': _L1_ffn_in['b2'], 'L1_ffn_A2': _L1_ffn_in['A2'], 'L1_ffn_B2': _L1_ffn_in['B2'], 'L1_ffn_W3': _L1_ffn_in['W3'], 'L1_ffn_b3': _L1_ffn_in['b3'], 'L1_ffn_A3': _L1_ffn_in['A3'], 'L1_ffn_B3': _L1_ffn_in['B3']}
    _x0 = _d['L0_attn_x']
    _d['L0_attn_x'] = jax.random.normal(jax.random.fold_in(jax.random.key(seed), 1), (4, 1024, 256), dtype=_x0.dtype)
    del _x0
    return _d

def reference(L0_attn_x, L0_attn_Wq, L0_attn_Wk, L0_attn_Wv, L0_attn_Wfc, L0_attn_bfc, L0_attn_gamma, L0_attn_beta, L0_ffn_W1, L0_ffn_b1, L0_ffn_W2, L0_ffn_b2, L1_attn_ln1_w, L1_attn_ln1_b, L1_attn_Wqk, L1_attn_bqk, L1_attn_Wv, L1_attn_bv, L1_attn_Wg, L1_attn_bg, L1_attn_Wo, L1_attn_bo, L1_attn_ln2_w, L1_attn_ln2_b, L1_attn_gamma, L1_attn_beta, L1_attn_pos_emb, L1_ffn_Wg, L1_ffn_W1, L1_ffn_b1, L1_ffn_A1, L1_ffn_B1, L1_ffn_W2, L1_ffn_b2, L1_ffn_A2, L1_ffn_B2, L1_ffn_W3, L1_ffn_b3, L1_ffn_A3, L1_ffn_B3):

    def _L0_attn_ref(x, Wq, Wk, Wv, Wfc, bfc, gamma, beta):
        import jax, jax.numpy as jnp
        import numpy as np
        DIM_Q = 256
        DIM_K = 256
        DIM_V = 256
        OUT_DIM = 256
        B, N = (4, 512)

        def _layer_norm(h, gamma, beta, eps=1e-05):
            mu = jnp.mean(h, axis=-1, keepdims=True)
            var = jnp.mean(jnp.square(h - mu), axis=-1, keepdims=True)
            return (h - mu) * jax.lax.rsqrt(var + eps) * gamma + beta
        q = jnp.einsum('bnd,dk->bnk', x, Wq)
        k = jnp.einsum('bnd,dk->bnk', x, Wk)
        v = jnp.einsum('bnd,dv->bnv', x, Wv)
        scale = 1.0 / np.sqrt(DIM_K)
        scores = jnp.einsum('bnk,bmk->bnm', q, k) * scale
        n = x.shape[1]
        causal = jnp.tril(jnp.ones((n, n), dtype=bool))
        scores = jnp.where(causal, scores, -jnp.inf)
        att = jax.nn.softmax(scores, axis=-1)
        out = jnp.einsum('bnm,bmv->bnv', att, v)
        out = _layer_norm(out + v, gamma, beta)
        return jnp.einsum('bnv,vo->bno', out, Wfc) + bfc

    def _L0_ffn_ref(hidden_states, W1, b1, W2, b2):
        import jax, jax.numpy as jnp
        import numpy as np
        HIDDEN = 256
        INTER = 1024
        h = jax.nn.relu(jnp.einsum('bsh,hi->bsi', hidden_states, W1) + b1)
        return jnp.einsum('bsi,ih->bsh', h, W2) + b2

    def _L1_attn_ref(x, ln1_w, ln1_b, Wqk, bqk, Wv, bv, Wg, bg, Wo, bo, ln2_w, ln2_b, gamma, beta, pos_emb):
        import jax, jax.numpy as jnp
        import numpy as np
        GROUP = 64
        MAX_REL = 32

        def _silu(x):
            return x * jax.nn.sigmoid(x)

        def _ln(x, w, b, eps=1e-05):
            m = x.mean(-1, keepdims=True)
            v = ((x - m) ** 2).mean(-1, keepdims=True)
            return (x - m) / jnp.sqrt(v + eps) * w + b

        def _rope(x):
            n, d = (x.shape[-2], x.shape[-1])
            half = d // 2
            pos = jnp.arange(n, dtype=x.dtype)
            inv_freq = 10000.0 ** (-jnp.arange(half, dtype=x.dtype) / half)
            sinusoid = pos[:, None] * inv_freq[None, :]
            sin, cos = (jnp.sin(sinusoid), jnp.cos(sinusoid))
            x1, x2 = (x[..., :half], x[..., half:])
            return jnp.concatenate([x1 * cos - x2 * sin, x2 * cos + x1 * sin], axis=-1)
        b, n, d = x.shape
        G = GROUP
        x = _ln(x, ln1_w, ln1_b)
        qk = _silu(x @ Wqk.T + bqk)
        v = _silu(x @ Wv.T + bv)
        heads = qk[..., None, :] * gamma + beta
        quad_q, lin_q, quad_k, lin_k = (heads[..., i, :] for i in range(4))
        quad_q, lin_q, quad_k, lin_k = map(_rope, (quad_q, lin_q, quad_k, lin_k))
        g = n // G
        rs = lambda t: t.reshape(b, g, G, t.shape[-1])
        qq, lq, qkk, lk, vg = map(rs, (quad_q, lin_q, quad_k, lin_k, v))
        idx = jnp.arange(G)
        dist = jnp.clip(jnp.abs(idx[:, None] - idx[None, :]), 0, MAX_REL)
        bias = pos_emb[dist]
        quad_att = jnp.einsum('bgid,bgjd->bgij', qq, qkk) / G + bias
        attn = jax.nn.relu(quad_att) ** 2
        quad_out = jnp.einsum('bgij,bgje->bgie', attn, vg)
        lin_kv = jnp.einsum('bgnd,bgne->bde', lk, vg) / n
        lin_out = jnp.einsum('bgnd,bde->bgne', lq, lin_kv)
        qo = quad_out.reshape(b, n, -1)
        lo = lin_out.reshape(b, n, -1)
        gate = _silu(x @ Wg.T + bg)
        out = gate * (qo + lo)
        out = out @ Wo.T + bo
        return _ln(out, ln2_w, ln2_b)

    def _L1_ffn_ref(x, Wg, W1, b1, A1, B1, W2, b2, A2, B2, W3, b3, A3, B3):
        import jax, jax.numpy as jnp
        import numpy as np
        DIM = 256
        HID = 512
        E = 8
        K = 2
        R = 16
        B_, S_ = (2, 256)

        def _lora_in(xf, W, b, A, B):
            base = jnp.einsum('td,ehd->teh', xf, W)
            low = jnp.einsum('ter,ehr->teh', jnp.einsum('td,erd->ter', xf, A), B)
            return base + low + b

        def _lora_out(g, W, b, A, B):
            base = jnp.einsum('teh,edh->ted', g, W)
            low = jnp.einsum('ter,edr->ted', jnp.einsum('teh,erh->ter', g, A), B)
            return base + low + b
        orig_shape = x.shape
        xf = x.reshape(-1, x.shape[-1])
        scores = jax.nn.softmax(xf @ Wg.T, axis=-1)
        expert_weights, expert_indices = jax.lax.top_k(scores, K)
        expert_weights = expert_weights / expert_weights.sum(-1, keepdims=True)
        gates = (jax.nn.one_hot(expert_indices, E, dtype=xf.dtype) * expert_weights[..., None]).sum(axis=1)
        h1 = _lora_in(xf, W1, b1, A1, B1)
        h3 = _lora_in(xf, W3, b3, A3, B3)
        g = jax.nn.silu(h1) * h3
        y_e = _lora_out(g, W2, b2, A2, B2)
        y = jnp.einsum('te,ted->td', gates, y_e)
        return y.reshape(orig_shape)
    x = L0_attn_x
    xn = _layernorm(x, axis=-1)
    x = x + _L0_attn_ref(xn, L0_attn_Wq, L0_attn_Wk, L0_attn_Wv, L0_attn_Wfc, L0_attn_bfc, L0_attn_gamma, L0_attn_beta) + _L0_ffn_ref(xn, L0_ffn_W1, L0_ffn_b1, L0_ffn_W2, L0_ffn_b2)
    xn = _layernorm(x, axis=-1)
    x = x + _L1_attn_ref(xn, L1_attn_ln1_w, L1_attn_ln1_b, L1_attn_Wqk, L1_attn_bqk, L1_attn_Wv, L1_attn_bv, L1_attn_Wg, L1_attn_bg, L1_attn_Wo, L1_attn_bo, L1_attn_ln2_w, L1_attn_ln2_b, L1_attn_gamma, L1_attn_beta, L1_attn_pos_emb) + _L1_ffn_ref(xn, L1_ffn_Wg, L1_ffn_W1, L1_ffn_b1, L1_ffn_A1, L1_ffn_B1, L1_ffn_W2, L1_ffn_b2, L1_ffn_A2, L1_ffn_B2, L1_ffn_W3, L1_ffn_b3, L1_ffn_A3, L1_ffn_B3)
    return x

_drawn_inputs = setup_inputs


def setup_inputs(seed=0):
    import zlib

    import numpy as np

    out = dict(_drawn_inputs(seed))
    spreads = {'L0_attn_gamma': (1.0, 0.2),
     'L0_attn_beta': (0.0, 0.1),
     'L1_attn_ln1_w': (1.0, 0.2),
     'L1_attn_ln1_b': (0.0, 0.1),
     'L1_attn_bqk': (0.0, 2.0),
     'L1_attn_bv': (0.0, 0.1),
     'L1_attn_bg': (0.0, 0.1),
     'L1_attn_bo': (0.0, 0.8),
     'L1_attn_ln2_w': (1.0, 0.2),
     'L1_attn_ln2_b': (0.0, 0.275),
     'L1_attn_beta': (0.0, 2.0),
     'L1_ffn_b1': (0.0, 0.328),
     'L1_ffn_b2': (0.0, 0.368),
     'L1_ffn_b3': (0.0, 0.352)}
    factors = {'L0_ffn_b1': 3.359,
     'L1_attn_Wqk': 48.499,
     'L1_attn_gamma': 45.801,
     'L1_ffn_A1': 5.904,
     'L1_ffn_B1': 5.857,
     'L1_ffn_A2': 6.156,
     'L1_ffn_B2': 6.155,
     'L1_ffn_A3': 6.221,
     'L1_ffn_B3': 6.161,
     'L1_attn_pos_emb': 6.132}
    for name, (base, spread) in spreads.items():
        noise = np.random.default_rng([zlib.crc32(name.encode()), seed]).standard_normal(out[name].shape)
        drawn = base * np.exp(spread * noise) if base else spread * noise
        out[name] = jnp.asarray(drawn.astype(out[name].dtype))
    for name, factor in factors.items():
        out[name] = (out[name] * factor).astype(out[name].dtype)
    return out
```

```python
import numpy as np
import concourse.bass as bass
from concourse import mybir
from contextlib import ExitStack

F32 = mybir.dt.float32
I32 = mybir.dt.int32
F32R = mybir.dt.float32r
ALU = mybir.AluOpType
ACT = mybir.ActivationFunctionType
AX = mybir.AxisListType

P = 128
BATCH, SEQ, DIM = 4, 1024, 256
TOKENS = BATCH * SEQ
TPB = SEQ // P
TILES = TOKENS // P
DC = DIM // P
INTER = 1024
IC = INTER // P
E, HID, R, TOPK = 8, 512, 16, 2
HC = HID // P
EXPERT = 3 * DC * HID
BIASES = 2 * HID + DIM
PIECE = 32
STACK = 3 * PIECE
QK, H1, GROUP, MAXREL = 64, 512, 64, 32
EC = H1 // P
SLOTS_T = TOKENS * TOPK // P + E
SLOTS = SLOTS_T * P
EPS = 1e-5
MASKED = -3.0e38


ROWS1 = {}
ROWS1_N = 0
for _name, _length in (("L1_attn_bv", H1), ("L1_attn_bqk", QK), ("L1_attn_bo", DIM), ("L1_attn_ln2_w", DIM),
                       ("L1_attn_ln2_b", DIM), ("L1_attn_gamma", 4 * QK), ("L1_attn_beta", 4 * QK)):
    ROWS1[_name] = (ROWS1_N, _length)
    ROWS1_N += _length


def units_of_batch():
    order = [("XT", t) for t in range(4)] + [("PT", n) for n in range(4)]
    order += [("VV", n) for n in range(4)] + [("S", 0)]
    for i in range(TPB):
        if i < 2:
            first = [("W1", 4 * i + n) for n in range(2)]
            second = [("W1", 4 * i + n) for n in range(2, 4)]
        elif i < 4:
            first, second = [("W2", 2 * (i - 2))], [("W2", 2 * (i - 2) + 1)]
        else:
            first, second = [("W1", 2 * i)], [("W1", 2 * i + 1)]
        if i < 6:
            first = [("ET", i)] + first
            second = second + [("EP", 2 * i), ("EP", 2 * i + 1)]
        if i + 1 < TPB:
            order.append(("S", i + 1))
        order += first + [("TP", i)]
        if i:
            order.append(("LT", i - 1))
        order += second + [("AV", i)]
        if i:
            order.append(("FC", i - 1))
    order += [("W2", 4), ("W2", 5), ("LT", TPB - 1), ("W2", 6), ("W2", 7), ("FC", TPB - 1)]
    return order


def hold(engine, passed, semaphore, value):
    engine.wait_ge(semaphore, value)
    engine.sem_inc(passed, 1)


def t_uses(unit):
    kind, n = unit
    if kind == "TP":
        return n // 4 + 1
    return 1 if kind in ("XT", "LT", "ET") else 0


def g_uses(unit):
    return 1 if unit[0] in ("PT", "VV", "AV", "FC", "W1", "W2", "EP") else 0


def numbered(order, uses):
    at, out = 0, {}
    for u in order:
        out[u] = at
        at += uses(u)
    return out, at


def build(nc, io, out):
    ctx = ExitStack()
    dram = {}

    def sb(name, shape, dt=F32, at=ctx):
        return at.enter_context(nc.sbuf_tensor(name, shape, dt))

    def sem(name):
        return ctx.enter_context(nc.semaphore(name))

    with ctx:
        bank = [ctx.enter_context(nc.psum_tensor(f"bank{i}", [P, 512], F32)) for i in range(4, 8)]
        wide = [ctx.enter_context(nc.psum_tensor(f"wide{i}", [P, 1024], F32)) for i in range(2)]
        psum = {"T": bank[0:2], "G": bank[2:4], "S": wide}
        keep = {
            "ident": sb("ident", [P, P]),
            "r2": sb("r2", [P, TILES]),
            "r2i": sb("r2i", [P, TILES]),
        }
        scr = {
            "x1": nc.dram_tensor("x1_scratch", [TOKENS, DIM], F32).ap(),
            "xn1": nc.dram_tensor("xn1_scratch", [TOKENS, DIM], F32).ap(),
            "x2": nc.dram_tensor("x2_scratch", [TOKENS // 2, DIM], F32).ap(),
            "xs": nc.dram_tensor("slot_rows_scratch", [SLOTS, DIM], F32).ap(),
            "ys": nc.dram_tensor("slot_results_scratch", [SLOTS, DIM], F32).ap(),
            "experts": nc.dram_tensor("experts_scratch", [E, P, 2, EXPERT], F32).ap(),
        }
        layer0(nc, io, keep, scr, psum, out)
        keep.update({
            "wv1": sb("wv1", [P, DC, H1]), "wg1": sb("wg1", [P, DC, H1]), "wqk1": sb("wqk1", [P, DC, QK]),
            "wo1": sb("wo1", [P, EC, DIM]), "rout": sb("router", [P, DC, E]),
            "cols1": sb("cols1", [P, 8]),
            "rows1": sb("rows1", [P, ROWS1_N]),
            "same": sb("same_group", [P, P]), "bias": sb("distance_bias", [P, P]),
            "rope": sb("rope", [P, 2, TPB, QK]),
            "gates": sb("gates", [P, TOPK, TILES]), "slot": sb("slot", [P, TOPK, TILES], I32),
            "tile_expert": sb("tile_expert", [P, SLOTS_T + 8], I32),
            "expert_end": sb("expert_end", [P, E], I32),
        })
        route(nc, io, keep, scr, psum)
        with ExitStack() as held:
            keep["experts"] = sb("expert_ring", [P, 2, 2, EXPERT], F32R, held)
            keep["expert_bias"] = sb("expert_bias", [P, 2, BIASES], F32, held)
            keep["expert_in"] = [held.enter_context(nc.semaphore(f"expert_in{i}")) for i in range(2)]
            attention(nc, io, keep, scr, psum, 0, out)
            moe(nc, io, keep, scr, psum)
        attention(nc, io, keep, scr, psum, 2, out)


VN = 47


def layer0(nc, io, keep, scr, psum, out):
    ctx = ExitStack()

    def sb(name, shape, dt=F32):
        return ctx.enter_context(nc.sbuf_tensor(name, shape, dt))

    def sem(name):
        return ctx.enter_context(nc.semaphore(name))

    ORDER = units_of_batch()
    T_AT, T_N = numbered(ORDER, t_uses)
    G_AT, G_N = numbered(ORDER, g_uses)
    assert T_N % 2 == 0 and G_N % 2 == 0
    T, G, S = psum["T"], psum["G"], psum["S"]
    ident = keep["ident"]

    with ctx:
        wv = sb("wv", [P, DC, DIM])
        wfc = sb("wfc", [P, DC, DIM])
        w1 = sb("w1", [P, DC, INTER])
        w2 = sb("w2", [P, IC, DIM])
        wqk = sb("wqk_product", [P, DC, DIM])
        cols = sb("cols", [P, 12])
        crow = sb("crow", [P, DIM])
        mask = sb("mask", [P, P])
        zero = sb("zero", [P, DIM // 2])
        xb = sb("xb", [P, 2, TPB, DIM])
        xp = sb("xp", [P, 2, SEQ])
        xnT = sb("xnT", [P, DC, SEQ])
        pT = sb("pT", [P, DC, SEQ])
        v = sb("v", [P, TPB, DIM])
        prT = sb("prT", [P, 2, TPB, P])
        hT = sb("hT", [P, IC, 512])
        res = sb("res", [P, DIM])
        lnT = sb("lnT", [P, DIM])
        raw = sb("raw", [P, 2, 2 * HID])
        rawA = sb("rawA", [P, 2, HID])
        rawB = sb("rawB", [P, 2, HC, R])
        highB = sb("highB", [P, HC, R], F32R)
        partsB = sb("partsB", [P, 2, HC, STACK])
        partsA = sb("partsA", [P, 2, HID], F32R)
        partsBT = sb("partsBT", [P, HID], F32R)
        folds = sb("folded_matrices", [P, 2, 2, 2 * HID], F32R)
        st = sb("st", [P, TPB, 6])
        mv = sb("mv", [P, TPB, 2])
        ve = sb("ve", [P, TPB])
        rs = sb("rs", [P, TPB])
        sta = sb("sta", [P, 2, 6])
        mva = sb("mva", [P, 2, 2])
        vea = sb("vea", [P, 2])
        rsa = sb("rsa", [P, 2])
        st1 = sb("st1", [P, TPB, 6])
        mv1 = sb("mv1", [P, TPB, 2])
        ve1 = sb("ve1", [P, TPB])
        rs1 = sb("rs1", [P, TPB])
        varn = sb("varn", [P, TPB])
        half = sb("half", [P, TPB])
        mx = sb("mx", [P, 2])
        nmx = sb("nmx", [P, 2])
        rsum = sb("rsum", [P, 2])
        rinv = sb("rinv", [P, 2])

        prob = xp
        wq, wk = pT[:, :, 0:DIM], pT[:, :, DIM:2 * DIM]
        rows = v

        xn = xp[:].rearrange("p a (t d) -> p (a t) d", d=DIM)
        xn1 = pT[:].rearrange("p a (t d) -> p (a t) d", d=DIM)

        attn_w_in, ffn_w_in, const_in = sem("attn_weights_in"), sem("ffn_weights_in"), sem("consts_in")
        x_in, x1_stored, xn1_stored = sem("x_in"), sem("x1_stored"), sem("xn1_stored")
        matrix_in = [sem(f"matrix_in{i}") for i in range(2)]
        matrix_out = [sem(f"matrix_out{i}") for i in range(2)]
        factors_ready, high_ready = sem("factors_ready"), sem("matrix_high_ready")
        p_step, p_held = sem("gpsimd_step"), sem("gpsimd_held")
        wT_done, wT_copied = sem("wqk_transposed"), sem("wqk_transposes_copied")
        pre_done, wqk_copied, folded, beta_spread = (sem("pre_products_done"), sem("wqk_product_copied"),
                                                     sem("biases_and_gamma_folded"), sem("beta_spread"))
        half_ready, zeroed = sem("half_ready"), sem("slots_zeroed")
        t_done, t_taken = sem("transposes_done"), sem("transposes_taken")
        g_done = [sem(f"product_done{i}") for i in range(2)]
        g_taken = [sem(f"product_taken{i}") for i in range(2)]
        s_done, max_ready, probs_ready = sem("scores_done"), sem("max_ready"), sem("probs_ready")
        var_ready, rstd_ready, xn_ready, bias_added = (sem("var_ready"), sem("rstd_ready"), sem("xn_ready"),
                                                       sem("bias_added"))
        avar_ready, arstd_ready, ln_ready = sem("attn_var_ready"), sem("attn_rstd_ready"), sem("attn_normalised")
        var1_ready, rstd1_ready, xn1_ready = sem("var1_ready"), sem("rstd1_ready"), sem("xn1_ready")
        varn_ready, r2_ready = sem("xn1_var_ready"), sem("r2_ready")
        v_step = sem("vector_step")
        v_held = sem("vector_held")

        block = ctx.enter_context(nc.Block())
        x_b = io["L0_attn_x"].rearrange("b (t p) d -> b p t d", p=P)
        x1_b = scr["x1"].rearrange("(b t p) d -> b p t d", p=P, t=TPB)
        xn1_b = scr["xn1"].rearrange("(b t p) d -> b p t d", p=P, t=TPB)

        def taken_t(b, u, k=0):
            return T_N * b + T_AT[u] + k + 1 + 2

        def taken_g(b, u):
            n = G_AT[u]
            return g_taken[n % 2], (G_N // 2) * b + n // 2 + 1 + 1

        @block.sync
        def _(sp):
            def load_matrix(b, j):
                e, m = 2 * b + j // 3, j % 3
                name = ("1", "3", "2")[m]
                k = DC if m == 2 else HC
                arrived = matrix_in[j % 2]
                sp.dma_start(raw[:, j % 2, :].rearrange("p (c n) -> p c n", c=k),
                             io["L1_ffn_W" + name][bass.ds(e, 1)].rearrange("e (c p) n -> p (e c) n", p=P)
                             ).then_inc(arrived, 16)
                for part in range(3):
                    sp.dma_start(rawA[PIECE * part:PIECE * part + R, j % 2, 0:DIM if m < 2 else HID],
                                 io["L1_ffn_A" + name][bass.ds(e, 1)].rearrange("e r n -> (e r) n")).then_inc(arrived, 16)
                sp.dma_start(rawB[:, j % 2, 0:k, :],
                             io["L1_ffn_B" + name][bass.ds(e, 1)].rearrange("e (c p) r -> p (e c) r", p=P)
                             ).then_inc(arrived, 16)

            def store_matrix(b, j):
                e, m = 2 * b + j // 3, j % 3
                sp.wait_ge(*taken_g(b, ("EP", 2 * j + 1)))
                sp.dma_start(scr["experts"][bass.ds(e, 1), :, :, 2 * HID * m:2 * HID * (m + 1)].rearrange("e p h n -> (e p) h n"),
                             folds[:, j % 2, :, :].bitcast(F32)).then_inc(matrix_out[j % 2], 16)

            sp.dma_start(ident[:], io["ident"]).then_inc(attn_w_in, 16)
            sp.dma_start(wq, io["L0_attn_Wq"].rearrange("(c p) k -> p c k", p=P)).then_inc(attn_w_in, 16)
            sp.dma_start(wk, io["L0_attn_Wk"].rearrange("(c p) k -> p c k", p=P)).then_inc(attn_w_in, 16)
            sp.dma_start(xb[:, 0, :, :], x_b[0]).then_inc(x_in, 16)
            sp.dma_start(wv[:], io["L0_attn_Wv"].rearrange("(c p) k -> p c k", p=P)).then_inc(const_in, 16)
            sp.dma_start(wfc[:], io["L0_attn_Wfc"].rearrange("(c p) k -> p c k", p=P)).then_inc(const_in, 16)
            sp.dma_start(cols[:], io["cols0"]).then_inc(const_in, 16)
            sp.dma_start(rows[:, 0, :], io["L0_attn_bfc"].to_broadcast([P, DIM])).then_inc(const_in, 16)
            sp.dma_start(rows[:, 1, :], io["L0_ffn_b2"].to_broadcast([P, DIM])).then_inc(const_in, 16)
            sp.dma_start(mask[:], io["causal"]).then_inc(const_in, 16)
            sp.dma_start(w1[:], io["L0_ffn_W1"].rearrange("(c p) k -> p c k", p=P)).then_inc(ffn_w_in, 16)
            sp.dma_start(w2[:], io["L0_ffn_W2"].rearrange("(c p) k -> p c k", p=P)).then_inc(ffn_w_in, 16)
            def store(b):
                sp.wait_ge(var1_ready, b + 1)
                sp.dma_start(x1_b[bass.ds(b, 1)].rearrange("o p t d -> p (o t) d"),
                             xb[:, bass.ds(b % 2, 1), :, :].rearrange("p o t d -> p (o t) d")).then_inc(x1_stored, 16)
                sp.wait_ge(xn1_ready, TPB * b + TPB)
                sp.dma_start(xn1_b[bass.ds(b, 1)].rearrange("o p t d -> p (o t) d"), xn1).then_inc(xn1_stored, 16)

            sp.sem_inc(x1_stored, 16)
            sp.sem_inc(xn1_stored, 16)
            for k in range(2):
                sp.sem_inc(matrix_out[k], 16)
            sp.wait_ge(half_ready, 4)
            load_matrix(0, 0)
            load_matrix(0, 1)
            sp.dma_start(scr["xs"].rearrange("(p s) (k d) -> p (s k) d", p=P, k=2),
                         zero[:].unsqueeze(1).to_broadcast([P, 2 * SLOTS_T, DIM // 2])).then_inc(zeroed, 16)
            with sp.Fori(0, BATCH - 1) as b:
                sp.wait_ge(x1_stored, 16 * b + 16)
                sp.dma_start(xb[:, bass.ds((b + 1) % 2, 1), :, :].rearrange("p o t d -> p (o t) d"),
                             x_b[bass.ds(b + 1, 1)].rearrange("o p t d -> p (o t) d")).then_inc(x_in, 16)
                for j in range(6):
                    store_matrix(b, j)
                    load_matrix(b, j + 2)
                store(b)
            for j in range(6):
                store_matrix(BATCH - 1, j)
                if j < 4:
                    load_matrix(BATCH - 1, j + 2)
            store(BATCH - 1)
            for k in range(2):
                sp.wait_ge(matrix_out[k], 16 * (3 * BATCH + 1))
            sp.wait_ge(zeroed, 16)
            sp.wait_ge(x1_stored, 16 * BATCH + 16)
            sp.wait_ge(xn1_stored, 16 * BATCH + 16)

        @block.gpsimd
        def _(pool):
            nc.gpsimd.memset(half[:], -0.5).then_inc(half_ready, 1)
            nc.gpsimd.memset(zero[:], 0.0).then_inc(half_ready, 1)
            nc.gpsimd.memset(rawA[:], 0.0).then_inc(half_ready, 1)
            nc.gpsimd.memset(partsB[:], 0.0).then_inc(half_ready, 1)
            pool.wait_ge(half_ready, 4)
            pool.wait_ge(folded, 1)
            ready = [0]

            def factors(b, j):
                def own(ins):
                    ready[0] += 1
                    ins.then_inc(p_step, 1)
                    hold(pool, p_held, p_step, 18 * b + ready[0])

                i, k, w = j % 2, DC if j % 3 == 2 else HC, HID if j % 3 == 2 else DIM
                hold(pool, p_held, matrix_in[i], 80 * (3 * b + j // 2 + 1))
                nc.gpsimd.tensor_copy(partsA[:, i, 0:w], rawA[:, i, 0:w])
                own(nc.gpsimd.tensor_copy(highB[:, 0:k, :], rawB[:, i, 0:k, :]))
                pieces = partsB[:, i, 0:k, :].rearrange("p c (s w) -> p c s w", w=PIECE)
                nc.gpsimd.tensor_copy(pieces[:, :, 0:2, 0:R], highB[:, 0:k, :].unsqueeze(2).to_broadcast([P, k, 2, R]))
                own(nc.gpsimd.tensor_tensor(pieces[:, :, 2, 0:R], rawB[:, i, 0:k, :], highB[:, 0:k, :], ALU.subtract))
                low = slice(PIECE, 2 * PIECE)
                own(nc.gpsimd.tensor_tensor(partsA[low, i, 0:w], rawA[low, i, 0:w], partsA[low, i, 0:w], ALU.subtract))
                pool.sem_inc(factors_ready, 1)

            with pool.Fori(0, BATCH) as b:
                pool.wait_ge(var_ready, b + 1)
                nc.gpsimd.tensor_tensor(rs[:], ve[:], half[:], ALU.pow).then_inc(rstd_ready, 1)
                ready[0] = 0
                factors(b, 0)
                factors(b, 1)
                for t in range(TPB):
                    pool.wait_ge(xn_ready, TPB * b + t + 1)
                    xs = xb[:, bass.ds(b % 2, 1), t, :].rearrange("p o d -> p (o d)")
                    nc.gpsimd.tensor_tensor(xs, xs, crow[:], ALU.add).then_inc(bias_added, 1)
                for i in range(TPB):
                    pool.wait_ge(avar_ready, TPB * b + i + 1)
                    nc.gpsimd.tensor_tensor(rsa[:, i % 2:i % 2 + 1], vea[:, i % 2:i % 2 + 1], half[:, 0:1],
                                            ALU.pow).then_inc(arstd_ready, 1)
                    if i + 2 < 6:
                        factors(b, i + 2)
                pool.wait_ge(var1_ready, b + 1)
                nc.gpsimd.tensor_tensor(rs1[:], ve1[:], half[:], ALU.pow).then_inc(rstd1_ready, 1)
                pool.wait_ge(varn_ready, b + 1)
                nc.gpsimd.tensor_tensor(keep["r2"][:, bass.ds(TPB * b, TPB)], varn[:], half[:],
                                        ALU.pow).then_inc(r2_ready, 1)

        @block.tensor
        def _(pe):
            mm = nc.tensor.matmul
            pe.wait_ge(attn_w_in, 48)
            for n, w in enumerate((wq, wk)):
                for kc in range(DC):
                    for c in range(DC):
                        last = nc.tensor.transpose(S[n][:, (kc * DC + c) * P:(kc * DC + c + 1) * P],
                                                   w[:, c, kc * P:(kc + 1) * P], ident[:])
                last.then_inc(wT_done, 1)
            pe.wait_ge(wT_copied, 2)
            for c in range(DC):
                for kc in range(DC):
                    last = mm(G[0][:, c * DIM:(c + 1) * DIM], hT[:, kc, c * P:(c + 1) * P], hT[:, 2 + kc, 0:DIM],
                              start=(kc == 0), stop=(kc == DC - 1))
            last.then_inc(pre_done, 1)
            pe.wait_ge(beta_spread, 1)
            for c in range(DC):
                last = mm(G[1][:, 0:DIM], hT[:, 4 + c, 0:P], wfc[:, c, :], start=(c == 0), stop=(c == DC - 1))
            last.then_inc(pre_done, 1)
            pe.wait_ge(wqk_copied, 1)
            pe.wait_ge(folded, 2)
            pe.wait_ge(ffn_w_in, 32)

            with pe.Fori(0, BATCH) as b:
                def t_bank(u, k=0):
                    n = T_AT[u] + k
                    pe.wait_ge(t_taken, T_N * b + n + 1)
                    return T[n % 2]

                def g_bank(u):
                    n = G_AT[u]
                    pe.wait_ge(g_taken[n % 2], (G_N // 2) * b + n // 2 + 1)
                    return G[n % 2], g_done[n % 2]

                for u in ORDER:
                    kind, n = u
                    if kind == "XT":
                        pe.wait_ge(xn_ready, TPB * b + 2 * n + 2)
                        o = t_bank(u)
                        for c in range(DC):
                            for t in range(2):
                                last = nc.tensor.transpose(o[:, (2 * c + t) * P:(2 * c + t + 1) * P],
                                                           xn[:, 2 * n + t, c * P:(c + 1) * P], ident[:])
                        last.then_inc(t_done, 1)
                    elif kind == "PT":
                        c2, h = n // 2, n % 2
                        if n == 0:
                            pe.wait_ge(t_taken, taken_t(b, ("XT", 3)))
                        o, done = g_bank(u)
                        for c in range(DC):
                            last = mm(o[:], wqk[:, c, c2 * P:(c2 + 1) * P], xnT[:, c, h * 512:(h + 1) * 512],
                                      start=(c == 0), stop=(c == DC - 1))
                        last.then_inc(done, 1)
                    elif kind == "VV":
                        o, done = g_bank(u)
                        for t in range(2):
                            for c in range(DC):
                                last = mm(o[:, t * DIM:(t + 1) * DIM], xnT[:, c, (2 * n + t) * P:(2 * n + t + 1) * P],
                                          wv[:, c, :], start=(c == 0), stop=(c == DC - 1))
                        last.then_inc(done, 1)
                    elif kind == "S":
                        pe.wait_ge(probs_ready, TPB * b + n + 1)
                        if n == 0:
                            pe.wait_ge(*taken_g(b, ("PT", 3)))
                        keys = (n + 1) * P
                        for k0 in range(0, keys, 512):
                            k1 = min(keys, k0 + 512)
                            for c in range(DC):
                                last = mm(S[n % 2][:, k0:k1], pT[:, c, n * P:(n + 1) * P], xnT[:, c, k0:k1],
                                          start=(c == 0), stop=(c == DC - 1))
                        last.then_inc(s_done, 1)
                    elif kind == "TP":
                        pe.wait_ge(probs_ready, TPB * b + n + 1 + 2)
                        for k in range(n // 4 + 1):
                            o = t_bank(u, k)
                            for m in range(4 * k, min(n + 1, 4 * k + 4)):
                                last = nc.tensor.transpose(o[:, (m % 4) * P:(m % 4 + 1) * P],
                                                           prob[:, n % 2, m * P:(m + 1) * P], ident[:])
                            last.then_inc(t_done, 1)
                    elif kind == "AV":
                        pe.wait_ge(t_taken, taken_t(b, ("TP", n), n // 4))
                        if n == 0:
                            pe.wait_ge(*taken_g(b, ("VV", 3)))
                        o, done = g_bank(u)
                        for m in range(n + 1):
                            last = mm(o[:, 0:DIM], prT[:, n % 2, m, :], v[:, m, :], start=(m == 0), stop=(m == n))
                        last.then_inc(done, 1)
                    elif kind == "LT":
                        pe.wait_ge(ln_ready, TPB * b + n + 1)
                        o = t_bank(u)
                        for c in range(DC):
                            last = nc.tensor.transpose(o[:, c * P:(c + 1) * P], res[:, c * P:(c + 1) * P], ident[:])
                        last.then_inc(t_done, 1)
                    elif kind == "FC":
                        pe.wait_ge(t_taken, taken_t(b, ("LT", n)))
                        o, done = g_bank(u)
                        for c in range(DC):
                            last = mm(o[:, 0:DIM], lnT[:, c * P:(c + 1) * P], wfc[:, c, :],
                                      start=(c == 0), stop=(c == DC - 1))
                        last.then_inc(done, 1)
                    elif kind == "W1":
                        h, i = n // IC, n % IC
                        o, done = g_bank(u)
                        for c in range(DC):
                            last = mm(o[:], w1[:, c, i * P:(i + 1) * P], xnT[:, c, h * 512:(h + 1) * 512],
                                      start=(c == 0), stop=(c == DC - 1))
                        last.then_inc(done, 1)
                    elif kind == "W2":
                        h, t = n // 4, n % 4
                        pe.wait_ge(*taken_g(b, ("W1", IC * h + IC - 1)))
                        o, done = g_bank(u)
                        for i in range(IC):
                            last = mm(o[:, 0:DIM], hT[:, i, t * P:(t + 1) * P], w2[:, i, :],
                                      start=(i == 0), stop=(i == IC - 1))
                        last.then_inc(done, 1)
                    elif kind == "ET":
                        m = n % 3
                        pe.wait_ge(factors_ready, 6 * b + n + 1)
                        o = t_bank(u)
                        for c in range(DC if m == 2 else HC):
                            last = nc.tensor.transpose(o[0:STACK, c * P:(c + 1) * P], partsB[:, n % 2, c, :], ident[:])
                        last.then_inc(t_done, 1)
                    elif kind == "EP":
                        j, c = n // 2, n % 2
                        A, BT = partsA[0:STACK, j % 2, :], partsBT[0:STACK, :]
                        if c == 0:
                            pe.wait_ge(t_taken, taken_t(b, ("ET", j)))
                        o, done = g_bank(u)
                        def fold(out, a, bt, parts):
                            mm(out, a, bt, start=True, stop=False)
                            for h, part in enumerate(parts):
                                ins = mm(out[:, h * P:(h + 1) * P], part, ident[:], start=False, stop=(h == len(parts) - 1))
                            return ins

                        if j % 3 < 2:
                            last = fold(o[:], A[:, c * P:(c + 1) * P], BT,
                                        [raw[:, j % 2, h * DIM + c * P:h * DIM + (c + 1) * P] for h in range(HC)])
                        else:
                            for h in (2 * c, 2 * c + 1):
                                last = fold(o[:, h % 2 * DIM:(h % 2 + 1) * DIM], A[:, h * P:(h + 1) * P], BT[:, 0:DIM],
                                            [raw[:, j % 2, d * HID + h * P:d * HID + (h + 1) * P] for d in range(DC)])
                        last.then_inc(done, 1)

        @block.scalar
        def _(act):
            def copy(o, i):
                return nc.scalar.activation(o, i, ACT.Copy)

            for n in range(2):
                act.wait_ge(wT_done, n + 1)
                copy(hT[:, 2 * n:2 * n + 2, 0:DIM], S[n][:, 0:512].rearrange("p (k d) -> p k d", k=DC)).then_inc(wT_copied, 1)
            act.wait_ge(pre_done, 1)
            copy(wqk[:].rearrange("p c d -> p (c d)"), G[0][:]).then_inc(wqk_copied, 1)
            act.sem_inc(t_taken, 2)
            act.sem_inc(probs_ready, 2)
            act.sem_inc(g_taken[0], 1)
            act.sem_inc(g_taken[1], 1)
            act.wait_ge(const_in, 96)
            with act.Fori(0, BATCH) as b:
                def t_full(u, k=0):
                    n = T_AT[u] + k
                    act.wait_ge(t_done, T_N * b + n + 1)
                    return T[n % 2]

                def g_full(u):
                    n = G_AT[u]
                    act.wait_ge(g_done[n % 2], (G_N // 2) * b + n // 2 + 1)
                    return G[n % 2], g_taken[n % 2]

                def exp(i):
                    act.wait_ge(max_ready, TPB * b + i + 1)
                    nc.scalar.activation(prob[:, i % 2, 0:(i + 1) * P], S[i % 2][:, 0:(i + 1) * P], ACT.Exp,
                                         bias=nmx[:, i % 2:i % 2 + 1], scale=1.0 / 16.0,
                                         accum_out=rsum[:, i % 2:i % 2 + 1]).then_inc(probs_ready, 1)

                for u in ORDER:
                    kind, n = u
                    if kind == "XT":
                        o = t_full(u)
                        copy(xnT[:, :, 2 * n * P:(2 * n + 2) * P],
                             o[:].rearrange("p (c t) -> p c t", c=DC)).then_inc(t_taken, 1)
                    elif kind == "PT":
                        o, taken = g_full(u)
                        if n == 0:
                            act.wait_ge(xn1_stored, 16 * b + 16)
                        copy(pT[:, n // 2, (n % 2) * 512:(n % 2 + 1) * 512], o[:]).then_inc(taken, 1)
                    elif kind == "S" and n == 0:
                        exp(0)
                    elif kind == "TP":
                        for k in range(n // 4 + 1):
                            o = t_full(u, k)
                            m0, m1 = 4 * k, min(n + 1, 4 * k + 4)
                            copy(prT[:, n % 2, m0:m1, :].rearrange("p m q -> p (m q)"),
                                 o[:, 0:(m1 - m0) * P]).then_inc(t_taken, 1)
                        if n == 0:
                            exp(1)
                    elif kind == "LT":
                        o = t_full(u)
                        copy(lnT[:], o[:, 0:DIM]).then_inc(t_taken, 1)
                        if n + 2 < TPB:
                            exp(n + 2)
                    elif kind == "W1":
                        o, taken = g_full(u)
                        nc.scalar.activation(hT[:, n % IC, :], o[:], ACT.Relu,
                                             bias=cols[:, 4 + n % IC:5 + n % IC]).then_inc(taken, 1)
                    elif kind == "ET":
                        o = t_full(u)
                        w = DIM if n % 3 == 2 else HID
                        copy(partsBT[0:STACK, 0:w], o[0:STACK, 0:w]).then_inc(t_taken, 1)
                    elif kind == "EP":
                        o, _ = g_full(u)
                        if n % 2 == 0:
                            act.wait_ge(matrix_out[n // 2 % 2], 16 * (3 * b + n // 4 + 1))
                        copy(folds[:, n // 2 % 2, 0, (n % 2) * 512:(n % 2 + 1) * 512], o[:]).then_inc(high_ready, 1)

        @block.vector
        def _(dve):
            steps = [0]

            def own(ins, b=None):
                steps[0] += 1
                ins.then_inc(v_step, 1)
                hold(dve, v_held, v_step, steps[0] if b is None else VPRE + VN * b + steps[0])

            dve.wait_ge(const_in, 96)
            dve.wait_ge(attn_w_in, 48)
            for c in range(DC):
                last = nc.vector.tensor_scalar(hT[:, 4 + c, 0:P], ident[:], 0.0, cols[:, 2 + c:3 + c], ALU.mult, ALU.add)
            last.then_inc(beta_spread, 1)
            own(nc.vector.tensor_tensor(crow[:], rows[:, 0, :], rows[:, 1, :], ALU.add))
            dve.wait_ge(pre_done, 2)
            nc.vector.tensor_tensor(crow[:], crow[:], G[1][:, 0:DIM], ALU.add).then_inc(folded, 1)
            for c in range(DC):
                last = nc.vector.tensor_scalar(wfc[:, c, :], wfc[:, c, :], cols[:, c:c + 1], None, ALU.mult)
            last.then_inc(folded, 1)
            VPRE = steps[0]

            with dve.Fori(0, BATCH) as b:
                steps[0] = 0

                def g_full(u):
                    n = G_AT[u]
                    dve.wait_ge(g_done[n % 2], (G_N // 2) * b + n // 2 + 1)
                    return G[n % 2], g_taken[n % 2]

                def x_tile(t):
                    return xb[:, bass.ds(b % 2, 1), t, :].rearrange("p o d -> p (o d)")

                hold(dve, v_held, x_in, 16 * b + 16)
                for t in range(TPB):
                    last = nc.vector.bn_stats(st[:, t, :], x_tile(t))
                own(last, b)
                for t in range(TPB):
                    last = nc.vector.bn_aggr(mv[:, t, :], st[:, t, :])
                own(last, b)
                nc.vector.tensor_scalar(ve[:], mv[:, :, 1], EPS, None, ALU.add).then_inc(var_ready, 1)
                dve.wait_ge(rstd_ready, b + 1)
                for t in range(TPB):
                    nc.vector.tensor_scalar(xn[:, t, :], x_tile(t), mv[:, t, 0:1], rs[:, t:t + 1],
                                            ALU.subtract, ALU.mult).then_inc(xn_ready, 1)
                for u in ORDER:
                    kind, n = u
                    if kind == "VV":
                        o, taken = g_full(u)
                        nc.vector.tensor_copy(v[:, 2 * n:2 * n + 2, :].rearrange("p t d -> p (t d)"), o[:]).then_inc(taken, 1)
                    elif kind == "S":
                        i = n % 2
                        dve.wait_ge(s_done, TPB * b + n + 1)
                        diag = S[i][:, n * P:(n + 1) * P]
                        own(nc.vector.tensor_tensor(diag, diag, mask[:], ALU.add), b)
                        own(nc.vector.reduce_max(mx[:, i:i + 1], S[i][:, 0:(n + 1) * P], AX.X), b)
                        nc.vector.tensor_scalar(nmx[:, i:i + 1], mx[:, i:i + 1], -1.0 / 16.0, None,
                                                ALU.mult).then_inc(max_ready, 1)
                    elif kind == "AV":
                        i = n % 2
                        o, taken = g_full(u)
                        own(nc.vector.reciprocal(rinv[:, i:i + 1], rsum[:, i:i + 1]), b)
                        nc.vector.scalar_tensor_tensor(out=res[:], in0=o[:, 0:DIM], scalar=rinv[:, i:i + 1],
                                                       in1=v[:, n, :], op0=ALU.mult, op1=ALU.add).then_inc(taken, 1)
                        hold(dve, v_held, *taken_g(b, u))
                        own(nc.vector.bn_stats(sta[:, i, :], res[:]), b)
                        own(nc.vector.bn_aggr(mva[:, i, :], sta[:, i, :]), b)
                        nc.vector.tensor_scalar(vea[:, i:i + 1], mva[:, i, 1:2], EPS, None, ALU.add).then_inc(avar_ready, 1)
                        dve.wait_ge(arstd_ready, TPB * b + n + 1)
                        nc.vector.tensor_scalar(res[:], res[:], mva[:, i, 0:1], rsa[:, i:i + 1],
                                                ALU.subtract, ALU.mult).then_inc(ln_ready, 1)
                    elif kind in ("W2", "FC"):
                        o, taken = g_full(u)
                        other = ("FC" if kind == "W2" else "W2", n)
                        second = ORDER.index(other) < ORDER.index(u)
                        if second:
                            dve.wait_ge(*taken_g(b, other))
                        else:
                            dve.wait_ge(bias_added, TPB * b + n + 1)
                        nc.vector.tensor_tensor(x_tile(n), x_tile(n), o[:, 0:DIM], ALU.add).then_inc(taken, 1)
                        if second:
                            hold(dve, v_held, *taken_g(b, u))
                            last = nc.vector.bn_stats(st1[:, n, :], x_tile(n))
                    elif kind == "EP":
                        o, taken = g_full(u)
                        dve.wait_ge(high_ready, 12 * b + n + 1)
                        at = slice((n % 2) * 512, (n % 2 + 1) * 512)
                        nc.vector.tensor_tensor(folds[:, n // 2 % 2, 1, at], o[:], folds[:, n // 2 % 2, 0, at],
                                                ALU.subtract).then_inc(taken, 1)
                own(last, b)
                for t in range(TPB):
                    last = nc.vector.bn_aggr(mv1[:, t, :], st1[:, t, :])
                own(last, b)
                nc.vector.tensor_scalar(ve1[:], mv1[:, :, 1], EPS, None, ALU.add).then_inc(var1_ready, 1)
                dve.wait_ge(rstd1_ready, b + 1)
                own(nc.vector.tensor_tensor(varn[:], mv1[:, :, 1], rs1[:], ALU.mult), b)
                own(nc.vector.tensor_tensor(varn[:], varn[:], rs1[:], ALU.mult), b)
                nc.vector.tensor_scalar(varn[:], varn[:], EPS, None, ALU.add).then_inc(varn_ready, 1)
                for t in range(TPB):
                    nc.vector.tensor_scalar(xn1[:, t, :], x_tile(t), mv1[:, t, 0:1], rs1[:, t:t + 1],
                                            ALU.subtract, ALU.mult).then_inc(xn1_ready, 1)
                dve.wait_ge(r2_ready, b + 1)
                own(nc.vector.reciprocal(keep["r2i"][:, bass.ds(TPB * b, TPB)], keep["r2"][:, bass.ds(TPB * b, TPB)]), b)
                assert steps[0] == VN, steps[0]




def route(nc, io, keep, scr, psum):
    ctx = ExitStack()

    def sb(name, shape, dt=F32):
        return ctx.enter_context(nc.sbuf_tensor(name, shape, dt))

    def sem(name):
        return ctx.enter_context(nc.semaphore(name))

    T, S = psum["T"], psum["S"]
    CNT = psum["G"][0]
    ident = keep["ident"]
    wv1, wg1, wqk1, wo1, rout = keep["wv1"], keep["wg1"], keep["wqk1"], keep["wo1"], keep["rout"]
    cols, row = keep["cols1"], keep["rows1"]
    with ctx:
        raw = sb("raw1", [P, 3, EC, DIM])
        rawqk = sb("rawqk", [QK + E, DIM])
        posb = sb("posb", [P, 2 * MAXREL + 1])
        band = sb("band", [P, MAXREL + 1, P])
        spread = sb("spread", [P, DC, P])
        xt = sb("xt", [P, 2, TPB, DIM])
        xT = sb("xT", [P, 2, 2, DC, P])
        logit = sb("logit", [P, TILES, E])
        top = sb("top", [P, TILES, 8])
        topi = sb("topi", [P, TILES, 8], mybir.dt.uint32)
        before, ones, iota8, iotaT = (sb("before", [P, P]), sb("ones", [P, P]), sb("iota8", [P, E]),
                                      sb("iotaT", [P, SLOTS_T + 8]))
        first, second, both = (sb(n, [P, TILES, E]) for n in ("chosen1", "chosen2", "chosen"))
        idx = sb("idx", [P, TOPK, TILES])
        diff = sb("diff", [P, TILES])
        cum = sb("cum", [P, 2, TILES, E])
        pos = sb("pos", [P, TILES, E])
        tot = sb("tot", [P, TILES, E])
        te = sb("te", [P, 6, E])
        ti = sb("ti", [P, 2, E], I32)
        ge = sb("ge", [P, SLOTS_T + 8, E])
        slotf = sb("slotf", [P, TOPK, TILES])
        tilef = sb("tilef", [P, SLOTS_T + 8])

        w_in, r_in, c_in = sem("l1_weights_in"), sem("rows_in"), sem("route_consts_in")
        x_in = [sem(f"xn1_in{i}") for i in range(2)]
        wt_done, wt_taken, spread_ready, rowprod, folded = (sem("l1_transposed"), sem("l1_transposes_taken"),
            sem("ln1_bias_spread"), sem("l1_bias_products"), sem("l1_folded"))
        t_done, t_taken, l_done, l_taken = (sem("xn1_transposed"), sem("xn1_transposes_taken"), sem("logits_done"),
                                            sem("logits_taken"))
        chosen, counted, diff_ready, gates_ready = (sem("experts_chosen"), sem("choices_counted"), sem("diff_ready"),
                                                    sem("gates_ready"))
        v_step, v_held = sem("route_step"), sem("route_held")
        block = ctx.enter_context(nc.Block())
        xn1_b = scr["xn1"].rearrange("(b t p) d -> b p t d", p=P, t=TPB)

        @block.sync
        def _(sp):
            sp.dma_start(rawqk[0:QK, :], io["L1_attn_Wqk"]).then_inc(w_in, 16)
            sp.dma_start(rawqk[QK:QK + E, :], io["L1_ffn_Wg"]).then_inc(w_in, 16)
            sp.dma_start(raw[:, 0, :, :], io["L1_attn_Wv"].rearrange("(c p) n -> p c n", p=P)).then_inc(w_in, 16)
            sp.dma_start(raw[:, 1, :, :], io["L1_attn_Wg"].rearrange("(c p) n -> p c n", p=P)).then_inc(w_in, 16)
            sp.dma_start(raw[:, 2, :, :].rearrange("p e d -> p (e d)").rearrange("p (c n) -> p c n", c=DC),
                         io["L1_attn_Wo"].rearrange("(c p) n -> p c n", p=P)).then_inc(w_in, 16)
            sp.dma_start(cols[:], io["cols1"]).then_inc(r_in, 16)
            sp.dma_start(xt[:, 0, :, :], xn1_b[0]).then_inc(x_in[0], 16)
            for name, a in ROWS1.items():
                sp.dma_start(row[:, a[0]:a[0] + a[1]], io[name].to_broadcast([P, a[1]])).then_inc(r_in, 16)
            for n, t in (("before", before), ("ones", ones), ("iota8", iota8), ("iotaT", iotaT)):
                sp.dma_start(t[:], io[n]).then_inc(c_in, 16)
            sp.dma_start(band[:], io["band"]).then_inc(c_in, 16)
            sp.dma_start(keep["same"][:], io["same_group"]).then_inc(c_in, 16)
            sp.dma_start(keep["rope"][:], io["rope"]).then_inc(c_in, 16)
            sp.dma_start(posb[:], io["L1_attn_pos_emb"].to_broadcast([P, 2 * MAXREL + 1])).then_inc(c_in, 16)
            for b in range(1, BATCH):
                if b >= 2:
                    sp.wait_ge(t_taken, 4 * (b - 1))
                sp.dma_start(xt[:, b % 2, :, :], xn1_b[b]).then_inc(x_in[b % 2], 16)

        def logit_bank(n):
            return S[n // 2 % 2][:, n % 2 * 512:n % 2 * 512 + 2 * E]

        def logits_of(pe, n):
            pe.wait_ge(t_taken, n + 1)
            if n >= 4:
                pe.wait_ge(l_taken, n - 3)
            for t in range(2):
                for c in range(DC):
                    last = nc.tensor.matmul(logit_bank(n)[:, t * E:(t + 1) * E], xT[:, n % 2, t, c, :],
                                            rout[:, c, :], start=(c == 0), stop=(c == DC - 1))
            last.then_inc(l_done, 1)

        @block.tensor
        def _(pe):
            mm, tr = nc.tensor.matmul, nc.tensor.transpose
            pe.wait_ge(w_in, 80)
            for c in range(DC):
                last = tr(T[0][:, c * (QK + E):(c + 1) * (QK + E)], rawqk[:, c * P:(c + 1) * P], ident[0:QK + E, 0:QK + E])
            last.then_inc(wt_done, 1)
            n = 1
            for w in range(2):
                for c in range(DC):
                    if n >= 2:
                        pe.wait_ge(wt_taken, n - 1)
                    for e in range(EC):
                        last = tr(T[n % 2][:, e * P:(e + 1) * P], raw[:, w, e, c * P:(c + 1) * P], ident[:])
                    last.then_inc(wt_done, 1)
                    n += 1
            wo_raw = raw[:, 2, :, :].rearrange("p e d -> p (e d)")
            for e2 in range(2):
                pe.wait_ge(wt_taken, n - 1)
                for e in range(2):
                    for c in range(DC):
                        last = tr(T[n % 2][:, (DC * e + c) * P:(DC * e + c + 1) * P],
                                  wo_raw[:, c * H1 + (2 * e2 + e) * P:c * H1 + (2 * e2 + e + 1) * P], ident[:])
                last.then_inc(wt_done, 1)
                n += 1
            pe.wait_ge(wt_taken, n)
            pe.wait_ge(spread_ready, 1)
            for c in range(DC):
                mm(S[0][:, 0:H1], spread[:, c, :], wv1[:, c, :], start=(c == 0), stop=(c == DC - 1))
            for c in range(DC):
                mm(S[0][:, 512:512 + QK], spread[:, c, :], wqk1[:, c, :], start=(c == 0), stop=(c == DC - 1))
            for e in range(EC):
                for c in range(DC):
                    last = mm(S[1][:, e:e + 1], wg1[:, c, e * P:(e + 1) * P], cols[:, 2 + c:3 + c],
                              start=(c == 0), stop=(c == DC - 1))
            last.then_inc(rowprod, 1)
            pe.wait_ge(folded, 1)
            for b in range(BATCH):
                pe.wait_ge(x_in[b % 2], 16 * (b // 2 + 1))
                for q in range(4):
                    n = 4 * b + q
                    if n >= 2:
                        pe.wait_ge(t_taken, n - 1)
                    for t in range(2):
                        for c in range(DC):
                            last = tr(T[n % 2][:, (DC * t + c) * P:(DC * t + c + 1) * P],
                                      xt[:, b % 2, 2 * q + t, c * P:(c + 1) * P], ident[:])
                    last.then_inc(t_done, 1)
                    if n >= 1:
                        logits_of(pe, n - 1)
            logits_of(pe, 4 * BATCH - 1)
            pe.wait_ge(chosen, 1)
            pe.wait_ge(c_in, 64)
            bo = both[:].rearrange("p t e -> p (t e)")
            mm(CNT[:, 0:TILES * E], before[:], bo, start=True, stop=True)
            mm(CNT[:, TILES * E:2 * TILES * E], ones[:], bo, start=True, stop=True).then_inc(counted, 1)

        @block.scalar
        def _(act):
            def copy(o, i):
                return nc.scalar.activation(o, i, ACT.Copy)

            act.wait_ge(wt_done, 1)
            t0 = T[0][:, 0:DC * (QK + E)].rearrange("p (c n) -> p c n", c=DC)
            copy(wqk1[:], t0[:, :, 0:QK])
            copy(rout[:], t0[:, :, QK:QK + E]).then_inc(wt_taken, 1)
            n = 1
            for w in (wv1, wg1):
                for c in range(DC):
                    act.wait_ge(wt_done, n + 1)
                    copy(w[:, c, :], T[n % 2][:]).then_inc(wt_taken, 1)
                    n += 1
            for e2 in range(2):
                act.wait_ge(wt_done, n + 1)
                copy(wo1[:, 2 * e2:2 * e2 + 2, :].rearrange("p e d -> p (e d)"), T[n % 2][:]).then_inc(wt_taken, 1)
                n += 1
            for n in range(4 * BATCH):
                act.wait_ge(t_done, n + 1)
                if n >= 2:
                    act.wait_ge(l_done, n - 1)
                copy(xT[:, n % 2, :, :, :].rearrange("p t c q -> p (t c q)"), T[n % 2][:]).then_inc(t_taken, 1)
            act.wait_ge(diff_ready, 1)
            for k in range(TOPK):
                last = nc.scalar.activation(keep["gates"][:, k, :], diff[:], ACT.Sigmoid, scale=(1.0 if k == 0 else -1.0))
            last.then_inc(gates_ready, 1)

        @block.vector
        def _(dve):
            steps = [0]
            tt, ts = nc.vector.tensor_tensor, nc.vector.tensor_scalar

            def own(ins):
                steps[0] += 1
                ins.then_inc(v_step, 1)
                dve.wait_ge(v_step, steps[0])

            dve.wait_ge(r_in, 16 * (1 + len(ROWS1)))
            for c in range(DC):
                last = ts(spread[:, c, :], ident[:], 0.0, cols[:, 2 + c:3 + c], ALU.mult, ALU.add)
            last.then_inc(spread_ready, 1)
            dve.wait_ge(rowprod, 1)
            bv, bqk = ROWS1["L1_attn_bv"], ROWS1["L1_attn_bqk"]
            tt(row[:, bv[0]:bv[0] + bv[1]], row[:, bv[0]:bv[0] + bv[1]], S[0][:, 0:H1], ALU.add)
            tt(row[:, bqk[0]:bqk[0] + bqk[1]], row[:, bqk[0]:bqk[0] + bqk[1]], S[0][:, 512:512 + QK], ALU.add)
            tt(cols[:, 4:8], cols[:, 4:8], S[1][:, 0:EC], ALU.add).then_inc(folded, 1)
            for w in (wv1, wg1, wqk1):
                for c in range(DC):
                    last = ts(w[:, c, :], w[:, c, :], cols[:, c:c + 1], None, ALU.mult)
            own(last)
            dve.wait_ge(c_in, 16 * 8)
            own(ts(keep["bias"][:], band[:, 0, :], posb[:, 0:1], None, ALU.mult))
            for n in range(4 * BATCH):
                for k in (2 * n + 1, 2 * n + 2):
                    own(nc.vector.scalar_tensor_tensor(out=keep["bias"][:], in0=band[:, k, :], scalar=posb[:, k:k + 1],
                                                       in1=keep["bias"][:], op0=ALU.mult, op1=ALU.add))
                dve.wait_ge(l_done, n + 1)
                nc.vector.tensor_copy(logit[:, 2 * n:2 * n + 2, :].rearrange("p t e -> p (t e)"),
                                      logit_bank(n)).then_inc(l_taken, 1)
                dve.wait_ge(l_taken, n + 1)
                for t in (2 * n, 2 * n + 1):
                    last = nc.vector.max(top[:, t, :], logit[:, t, :])
                own(last)
                for t in (2 * n, 2 * n + 1):
                    last = nc.vector.max_index(topi[:, t, :], top[:, t, :], logit[:, t, :])
            own(last)
            tt(diff[:], top[:, :, 0], top[:, :, 1], ALU.subtract).then_inc(diff_ready, 1)
            for k in range(TOPK):
                last = nc.vector.tensor_copy(idx[:, k, :], topi[:, :, k])
            own(last)
            every = iota8[:].unsqueeze(1).to_broadcast([P, TILES, E])
            for k, m in enumerate((first, second)):
                last = tt(m[:], idx[:, k, :].unsqueeze(2).to_broadcast([P, TILES, E]), every, ALU.is_equal)
            own(last)
            tt(both[:], first[:], second[:], ALU.add).then_inc(chosen, 1)
            dve.wait_ge(counted, 1)
            tc = CNT[:, TILES * E:2 * TILES * E].rearrange("p (t e) -> p t e", e=E)
            nc.vector.tensor_copy(tot[:], tc)
            own(nc.vector.tensor_copy(cum[:, 0, :, :], tc))
            k, step = 0, 1
            while step < TILES:
                nc.vector.tensor_copy(cum[:, 1 - k, 0:step, :], cum[:, k, 0:step, :])
                own(tt(cum[:, 1 - k, step:, :], cum[:, k, step:, :], cum[:, k, 0:TILES - step, :], ALU.add))
                k, step = 1 - k, 2 * step
            own(ts(ti[:, 0, :], cum[:, k, TILES - 1, :], 127.0, None, ALU.add))
            own(ts(ti[:, 1, :], ti[:, 0, :], 7, None, ALU.arith_shift_right))
            nc.vector.tensor_copy(te[:, 5, :], ti[:, 1, :])
            own(nc.vector.tensor_copy(te[:, 0, :], ti[:, 1, :]))
            j, step = 0, 1
            while step < E:
                nc.vector.tensor_copy(te[:, 1 - j, 0:step], te[:, j, 0:step])
                own(tt(te[:, 1 - j, step:], te[:, j, step:], te[:, j, 0:E - step], ALU.add))
                j, step = 1 - j, 2 * step
            upto = te[:, j, :]
            nc.vector.tensor_copy(keep["expert_end"][:], upto)
            own(tt(ge[:], iotaT[:].unsqueeze(2).to_broadcast([P, SLOTS_T + 8, E]),
                   upto.unsqueeze(1).to_broadcast([P, SLOTS_T + 8, E]), ALU.is_ge))
            own(nc.vector.reduce_sum(tilef[:], ge[:], AX.X))
            own(ts(keep["tile_expert"][:], tilef[:], float(E - 1), None, ALU.min))
            own(tt(te[:, 2, :], upto, te[:, 5, :], ALU.subtract))
            own(ts(te[:, 3, :], te[:, 2, :], float(P), None, ALU.mult))
            own(tt(pos[:], cum[:, k, :, :], tot[:], ALU.subtract))
            own(tt(pos[:], pos[:], CNT[:, 0:TILES * E].rearrange("p (t e) -> p t e", e=E), ALU.add))
            own(tt(pos[:], pos[:], te[:, 3, :].unsqueeze(1).to_broadcast([P, TILES, E]), ALU.add))
            for m in (first, second):
                last = tt(m[:], m[:], pos[:], ALU.mult)
            own(last)
            for q, m in enumerate((first, second)):
                last = nc.vector.reduce_sum(slotf[:, q, :], m[:], AX.X)
            own(last)
            own(nc.vector.tensor_copy(keep["slot"][:], slotf[:]))
            dve.wait_ge(gates_ready, 1)


VB = (46, 79)


GB = 6


def attention_units():
    order = [("UT", n) for n in range(4)] + [("QK", 0)] + [("VV", t) for t in range(TPB)]
    order += [("HT", n) for n in range(4)] + [("LK", 0), ("AT", 0), ("AT", 1)]
    for n in range(4):
        order += [("GA", n), ("OO", n)]
    order += [("GA", 4), ("GA", 5)] + [("YY", t) for t in range(4)] + [("OO", 4), ("OO", 5)]
    order += [("GA", 6), ("OO", 6), ("GA", 7), ("OO", 7)] + [("YY", t) for t in range(4, 8)]
    return order


class Products:

    def __init__(self, order, taker, banks, done, taken):
        self.order = [u for u in order if u[0] in taker]
        assert len(self.order) % banks == 0
        self.n, self.banks, self.done, self.sems = len(self.order), banks, done, taken
        self.at = {u: i for i, u in enumerate(self.order)}
        self.who = {u: taker[u[0]] for u in self.order}
        self.count = {e: sum(w == e for w in self.who.values()) for e in taken}

    def bank(self, u):
        return self.at[u] % self.banks

    def is_done(self, b, u):
        return self.done, self.n * b + self.at[u] + 1

    def is_taken(self, b, u):
        e = self.who[u]
        k = sum(self.who[w] == e for w in self.order[:self.at[u]])
        return self.sems[e], self.count[e] * (b + 1) + k + 1

    def is_free(self, b, u):
        i = self.at[u] - self.banks
        return self.is_taken(b, self.order[i]) if i >= 0 else self.is_taken(b - 1, self.order[i])


def attention(nc, io, keep, scr, psum, b0, out):
    ctx = ExitStack()
    tag = f"_{b0}"
    last_half = b0 > 0

    def sb(name, shape, dt=F32):
        return ctx.enter_context(nc.sbuf_tensor(name + tag, shape, dt))

    def sem(name):
        return ctx.enter_context(nc.semaphore(name + tag))

    NB = 2
    ORDER = attention_units()
    T_AT, T_N = numbered(ORDER, lambda u: 1 if u[0] in ("UT", "HT") else 0)
    T = psum["T"]
    banks = [psum["G"][0][:], psum["G"][1][:]] + [w[:, k:k + 512] for w in psum["S"] for k in (0, 512)]
    ident, wv1, wg1, wqk1, wo1 = (keep[n] for n in ("ident", "wv1", "wg1", "wqk1", "wo1"))
    cols, rows, rope = keep["cols1"], keep["rows1"], keep["rope"]

    def row(name):
        at, n = ROWS1[name]
        return rows[:, at:at + n]

    with ctx:
        u = sb("u", [P, TPB, DIM])
        x = sb("x1b", [P, TPB, DIM])
        uT = sb("uT", [P, DC, SEQ])
        qk = sb("qk", [P, TPB, QK])
        heads = sb("heads", [P, TPB, 4, QK])
        headT = sb("headT", [P, 2, SEQ])
        v = sb("v1", [P, TPB, H1])
        lkv = sb("lkv", [P, H1])
        att = sb("att", [P, TPB, P])
        attw = sb("attw", [P, 4, P])
        gT = sb("gT", [P, 2, 512])
        oT = heads[:].rearrange("p t h d -> p (t h d)").rearrange("p (e n) -> p e n", e=EC)
        y = sb("y1", [P, 2, DIM])
        sty = sb("sty", [P, 2, 6])
        mvy = sb("mvy", [P, 2, 2])
        vey = sb("vey", [P, 2])
        rsy = sb("rsy", [P, 2])
        half = sb("half1", [P, 1])
        if last_half:
            zx = sb("first_half", [P, TPB, DIM])
            got = sb("expert_results", [P, TILES, TOPK, DIM])
        else:
            ring = sb("ring", [P, 4, DIM])

        xn_in, x_in, stored = sem("xn_in"), sem("x1_in"), sem("stored")
        u_ready, t_done, t_taken, g_done = sem("u_ready"), sem("transposed"), sem("transposes_taken"), sem("products_done")
        by_act, by_dve = sem("products_taken_by_scalar"), sem("products_taken_by_vector")
        qk_ready, v_ready = sem("qk_ready"), sem("v_ready")
        rotated, att_ready = sem("heads_rotated"), sem("att_ready")
        var_ready, rstd_ready, x_ready = sem("var_ready"), sem("rstd_ready"), sem("x_ready")
        v_step, v_held, half_ready = sem("vector_step"), sem("vector_held"), sem("half_ready")
        pe_held, zeros_ready = sem("tensor_held"), sem("zeros_ready")
        z_in, z_stored, z_ready = sem("first_half_in"), sem("first_half_stored"), sem("first_half_ready")
        moved = [sem(f"rows_moved{i}") for i in range(4)]
        ring_in = [sem(f"ring_in{i}") for i in range(4)]
        block = ctx.enter_context(nc.Block())
        pr = Products(ORDER, {"QK": "dve", "VV": "dve", "LK": "act", "AT": "dve", "GA": "act", "OO": "dve", "YY": "dve"},
                      GB, g_done, {"act": by_act, "dve": by_dve})
        xn1_b = scr["xn1"].rearrange("(b t p) d -> b p t d", p=P, t=TPB)
        x1_b = scr["x1"].rearrange("(b t p) d -> b p t d", p=P, t=TPB)
        x2_b = scr["x2"].rearrange("(b t p) d -> b p t d", p=P, t=TPB)
        out_b = out.rearrange("b (t p) d -> b p t d", p=P)

        @block.sync
        def _(sp):
            sp.sem_inc(stored, 16)
            if last_half:
                sp.sem_inc(z_stored, 16)
            with sp.Fori(0, NB) as b:
                if last_half:
                    sp.wait_ge(z_stored, 16 * b + 16)
                    sp.dma_start(zx[:], x2_b[bass.ds(b, 1)].rearrange("o p t d -> p (o t) d")).then_inc(z_in, 16)
                sp.wait_ge(rotated, b + 1)
                sp.dma_start(u[:], xn1_b[bass.ds(b + b0, 1)].rearrange("o p t d -> p (o t) d")).then_inc(xn_in, 16)
                sp.wait_ge(stored, 16 * b + 16)
                sp.dma_start(x[:], x1_b[bass.ds(b + b0, 1)].rearrange("o p t d -> p (o t) d")).then_inc(x_in, 16)
                if last_half:
                    sp.wait_ge(z_ready, b + 1)
                    sp.dma_start(out_b[bass.ds(b, 1)].rearrange("o p t d -> p (o t) d"), zx[:]).then_inc(z_stored, 16)
                sp.wait_ge(x_ready, b + 1)
                to = out_b if last_half else x2_b
                sp.dma_start(to[bass.ds(b + b0 if last_half else b, 1)].rearrange("o p t d -> p (o t) d"),
                             x[:]).then_inc(stored, 16)
            sp.wait_ge(stored, 16 * NB + 16)
            if last_half:
                sp.wait_ge(z_stored, 16 * NB + 16)

        @block.gpsimd
        def _(pool):
            def index(k, t):
                return bass.IndirectOffsetOnAxis(ap=keep["slot"][:, k, t:t + 1], axis=0)

            def load(t):
                pool.dma_start(ring[:, t % 4, :], scr["xn1"][t * P:(t + 1) * P, :]).then_inc(ring_in[t % 4], 16)

            def scatter(t):
                pool.wait_ge(ring_in[t % 4], 16 * (t // 4 + 1))
                for k in range(TOPK):
                    nc.gpsimd.indirect_dma_start(out=scr["xs"], out_offset=index(k, t), in_=ring[:, t % 4, :],
                                                 in_offset=None, bounds_check=SLOTS - 1).then_inc(moved[t % 4], 16)

            def gather(t):
                for k in range(TOPK):
                    nc.gpsimd.indirect_dma_start(out=got[:, t, k, :], out_offset=None, in_=scr["ys"],
                                                 in_offset=index(k, t), bounds_check=SLOTS - 1).then_inc(moved[t // TPB // 2], 16)

            nc.gpsimd.memset(half[:], -0.5).then_inc(half_ready, 1)
            pool.wait_ge(half_ready, 1)
            if not last_half:
                for e in range(2):
                    load_expert(pool, io, keep, scr, e)
                for t in range(4):
                    load(t)
            for b in range(NB):
                if last_half:
                    for t in [TPB * b + t for t in range(TPB)] + [TPB * (b + b0) + t for t in range(TPB)]:
                        gather(t)
                else:
                    for t in range(2 * TPB * b, 2 * TPB * (b + 1)):
                        scatter(t)
                        if 2 <= t and t + 2 < TILES:
                            pool.wait_ge(moved[(t - 2) % 4], 32 * ((t - 2) // 4 + 1))
                            load(t + 2)
                for t in range(TPB):
                    pool.wait_ge(var_ready, TPB * b + t + 1)
                    nc.gpsimd.tensor_tensor(rsy[:, t % 2:t % 2 + 1], vey[:, t % 2:t % 2 + 1], half[:], ALU.pow
                                            ).then_inc(rstd_ready, 1)
            for q in range(2 if last_half else 4):
                pool.wait_ge(moved[q], 32 * TPB * (2 if last_half else 1))

        @block.tensor
        def _(pe):
            mm, tr = nc.tensor.matmul, nc.tensor.transpose
            with pe.Fori(0, NB) as b:
                def t_bank(un):
                    n = T_AT[un]
                    hold(pe, pe_held, t_taken, T_N * b + n + 1)
                    return T[n % 2]

                def taken_t(un):
                    return t_taken, T_N * b + T_AT[un] + 1 + 2

                for un in ORDER:
                    kind, n = un
                    if un in pr.at:
                        pe.wait_ge(*pr.is_free(b, un))
                        o = banks[pr.bank(un)]
                    if kind == "UT":
                        pe.wait_ge(u_ready, TPB * b + 2 * n + 2)
                        o = t_bank(un)
                        for c in range(DC):
                            for t in range(2):
                                last = tr(o[:, (2 * c + t) * P:(2 * c + t + 1) * P], u[:, 2 * n + t, c * P:(c + 1) * P], ident[:])
                        last.then_inc(t_done, 1)
                        continue
                    if kind == "HT":
                        if n == 0:
                            pe.wait_ge(rotated, b + 1 + 1)
                        o = t_bank(un)
                        for t in range(4):
                            pair = heads[:, 4 * (n % 2) + t, 2 * (n // 2):2 * (n // 2) + 2, :].rearrange("p h d -> p (h d)")
                            last = tr(o[:, t * P:(t + 1) * P], pair, ident[:])
                        last.then_inc(t_done, 1)
                        continue
                    if kind == "QK":
                        pe.wait_ge(*taken_t(("UT", 3)))
                        for t in range(TPB):
                            for c in range(DC):
                                last = mm(o[:, t * QK:(t + 1) * QK], uT[:, c, t * P:(t + 1) * P], wqk1[:, c, :],
                                          start=(c == 0), stop=(c == DC - 1))
                    elif kind == "VV":
                        for c in range(DC):
                            last = mm(o, uT[:, c, n * P:(n + 1) * P], wv1[:, c, :], start=(c == 0), stop=(c == DC - 1))
                    elif kind == "LK":
                        pe.wait_ge(v_ready, TPB * b + TPB)
                        for t in range(TPB):
                            last = mm(o, heads[:, t, 2:4, :].rearrange("p h d -> p (h d)"), v[:, t, :],
                                      start=(t == 0), stop=(t == TPB - 1))
                    elif kind == "AT":
                        if n == 0:
                            pe.wait_ge(*taken_t(("HT", 3)))
                            pe.wait_ge(zeros_ready, 1)
                        for t in range(4):
                            at = slice((4 * n + t) * P, (4 * n + t + 1) * P)
                            last = mm(o[:, t * P:(t + 1) * P], headT[:, 1, at], headT[:, 0, at], start=True, stop=True)
                    elif kind == "GA":
                        h, e = n // EC, n % EC
                        for c in range(DC):
                            last = mm(o, wg1[:, c, e * P:(e + 1) * P], uT[:, c, h * 512:(h + 1) * 512],
                                      start=(c == 0), stop=(c == DC - 1))
                    elif kind == "OO":
                        h, e = n // EC, n % EC
                        if n == 0:
                            pe.wait_ge(*pr.is_taken(b, ("LK", 0)))
                            pe.wait_ge(att_ready, 2 * b + 2)
                        mm(o, lkv[:, e * P:(e + 1) * P], headT[:, 0, h * 512:(h + 1) * 512], start=True, stop=False)
                        for t in range(4):
                            last = mm(o[:, t * P:(t + 1) * P], v[:, 4 * h + t, e * P:(e + 1) * P], att[:, 4 * h + t, :],
                                      start=False, stop=(t == 3))
                    elif kind == "YY":
                        pe.wait_ge(*pr.is_taken(b, ("OO", 3 if n < 4 else 7)))
                        for e in range(EC):
                            last = mm(o[:, 0:DIM], oT[:, e, (n % 4) * P:(n % 4 + 1) * P], wo1[:, e, :],
                                      start=(e == 0), stop=(e == EC - 1))
                    last.then_inc(g_done, 1)

        @block.scalar
        def _(act):
            def copy(o, i, scale=1.0):
                return nc.scalar.activation(o, i, ACT.Copy, scale=scale)

            act.sem_inc(t_taken, 2)
            act.sem_inc(by_act, pr.count["act"])
            with act.Fori(0, NB) as b:
                for un in ORDER:
                    kind, n = un
                    if kind in ("UT", "HT"):
                        k = T_AT[un]
                        act.wait_ge(t_done, T_N * b + k + 1)
                        o = T[k % 2]
                        if kind == "UT":
                            copy(uT[:, :, 2 * n * P:(2 * n + 2) * P], o[:].rearrange("p (c t) -> p c t", c=DC)).then_inc(t_taken, 1)
                        else:
                            rows_of = P if n < 2 else QK
                            copy(headT[0:rows_of, n // 2, (n % 2) * 512:(n % 2 + 1) * 512], o[0:rows_of, :]).then_inc(t_taken, 1)
                    elif kind == "QK":
                        act.wait_ge(*pr.is_taken(b, un))
                        nc.scalar.activation(qk[:], qk[:], ACT.Silu).then_inc(qk_ready, 1)
                    elif kind == "VV":
                        act.wait_ge(*pr.is_taken(b, un))
                        nc.scalar.activation(v[:, n, :], v[:, n, :], ACT.Silu).then_inc(v_ready, 1)
                    elif kind == "LK":
                        act.wait_ge(*pr.is_done(b, un))
                        copy(lkv[QK:, :], banks[pr.bank(un)][QK:, :], 1.0 / SEQ).then_inc(by_act, 1)
                    elif kind == "GA":
                        act.wait_ge(*pr.is_done(b, un))
                        if n >= 2:
                            act.wait_ge(*pr.is_taken(b, ("OO", n - 2)))
                        nc.scalar.activation(gT[:, n % 2, :], banks[pr.bank(un)], ACT.Silu,
                                             bias=cols[:, 4 + n % EC:5 + n % EC]).then_inc(by_act, 1)

        @block.vector
        def _(dve):
            steps = [0]
            tt, ts, stt = nc.vector.tensor_tensor, nc.vector.tensor_scalar, nc.vector.scalar_tensor_tensor
            V_N = VB[last_half]

            def own(ins):
                steps[0] += 1
                ins.then_inc(v_step, 1)
                hold(dve, v_held, v_step, V_N * b + steps[0])

            nc.vector.memset(headT[QK:, 1, :], 0.0)
            nc.vector.memset(lkv[0:QK, :], 0.0).then_inc(zeros_ready, 1)
            dve.sem_inc(by_dve, pr.count["dve"])
            dve.sem_inc(rotated, 1)
            with dve.Fori(0, NB) as b:
                def finish(t):
                    i = t % 2
                    dve.wait_ge(rstd_ready, TPB * b + t + 1)
                    own(ts(y[:, i, :], y[:, i, :], mvy[:, i, 0:1], rsy[:, i:i + 1], ALU.subtract, ALU.mult))
                    own(tt(y[:, i, :], y[:, i, :], row("L1_attn_ln2_w"), ALU.mult))
                    return tt(x[:, t, :], x[:, t, :], y[:, i, :], ALU.add)

                def add_experts(target, tile):
                    for t in range(TPB):
                        for k in range(TOPK):
                            g = got[:, bass.ds(tile + t, 1), k, :].rearrange("p o d -> p (o d)")
                            own(stt(out=target[:, t, :], in0=g, scalar=keep["gates"][:, k, bass.ds(tile + t, 1)],
                                    in1=target[:, t, :], op0=ALU.mult, op1=ALU.add))

                dve.wait_ge(xn_in, 16 * b + 16)
                for t in range(TPB):
                    ts(u[:, t, :], u[:, t, :], keep["r2"][:, bass.ds(TPB * (b + b0) + t, 1)], None,
                       ALU.mult).then_inc(u_ready, 1)
                for un in ORDER:
                    kind, n = un
                    if un in pr.at and pr.who[un] == "dve":
                        dve.wait_ge(*pr.is_done(b, un))
                        o = banks[pr.bank(un)]
                    if kind == "QK":
                        tt(qk[:], o.rearrange("p (t d) -> p t d", d=QK),
                           row("L1_attn_bqk").unsqueeze(1).to_broadcast([P, TPB, QK]), ALU.add).then_inc(by_dve, 1)
                    elif kind == "VV":
                        tt(v[:, n, :], o, row("L1_attn_bv"), ALU.add).then_inc(by_dve, 1)
                        if n == 1:
                            shape = [P, TPB, 4, QK]
                            dve.wait_ge(qk_ready, b + 1)
                            gam = row("L1_attn_gamma").rearrange("p (h d) -> p h d", d=QK).unsqueeze(1).to_broadcast(shape)
                            own(tt(heads[:], qk[:].unsqueeze(2).to_broadcast(shape), gam, ALU.mult))
                        if n == 2:
                            bet = row("L1_attn_beta").rearrange("p (h d) -> p h d", d=QK).unsqueeze(1).to_broadcast(shape)
                            own(tt(heads[:], heads[:], bet, ALU.add))
                        hq = QK // 2
                        tmp = u[:].rearrange("p t (h d) -> p t h d", d=QK)
                        if n == 3:
                            dve.wait_ge(t_taken, T_N * b + T_AT[("UT", 3)] + 1 + 2)
                            for d0, d1 in ((0, hq), (hq, 0)):
                                sn = rope[:, 1, :, d0:d0 + hq].unsqueeze(2).to_broadcast([P, TPB, 4, hq])
                                last = tt(tmp[:, :, :, d0:d0 + hq], heads[:, :, :, d1:d1 + hq], sn, ALU.mult)
                            own(last)
                        if n == 4:
                            own(tt(heads[:], heads[:], rope[:, 0, :, :].unsqueeze(2).to_broadcast(shape), ALU.mult))
                        if n == 5:
                            tt(heads[:], heads[:], tmp, ALU.add).then_inc(rotated, 1)
                        if n == 6:
                            hold(dve, v_held, x_in, 16 * b + 16)
                            own(tt(x[:], x[:], row("L1_attn_ln2_b").unsqueeze(1).to_broadcast([P, TPB, DIM]), ALU.add))
                    elif kind == "AT":
                        biased = keep["bias"][:].unsqueeze(1).to_broadcast([P, 4, P])
                        same = keep["same"][:].unsqueeze(1).to_broadcast([P, 4, P])
                        if n:
                            dve.wait_ge(att_ready, 2 * b + n)
                        stt(out=attw[:], in0=o.rearrange("p (t i) -> p t i", i=P), scalar=1.0 / GROUP, in1=biased,
                            op0=ALU.mult, op1=ALU.add).then_inc(by_dve, 1)
                        dve.wait_ge(*pr.is_taken(b, un))
                        own(stt(out=attw[:], in0=attw[:], scalar=0.0, in1=same, op0=ALU.max, op1=ALU.mult))
                        tt(att[:, 4 * n:4 * n + 4, :], attw[:], attw[:], ALU.mult).then_inc(att_ready, 1)
                    elif kind == "OO":
                        dve.wait_ge(*pr.is_taken(b, ("GA", n)))
                        tt(oT[:, n % EC, :], o, gT[:, n % 2, :], ALU.mult).then_inc(by_dve, 1)
                    elif kind == "YY":
                        i = n % 2
                        tt(y[:, i, :], o[:, 0:DIM], row("L1_attn_bo"), ALU.add).then_inc(by_dve, 1)
                        hold(dve, v_held, *pr.is_taken(b, un))
                        own(nc.vector.bn_stats(sty[:, i, :], y[:, i, :]))
                        own(nc.vector.bn_aggr(mvy[:, i, :], sty[:, i, :]))
                        if n == TPB - 1 and last_half:
                            hold(dve, v_held, moved[1], 32 * TPB * (b + 1))
                        ts(vey[:, i:i + 1], mvy[:, i, 1:2], EPS, None, ALU.add).then_inc(var_ready, 1)
                        if n:
                            own(finish(n - 1))
                        if n == 3 and last_half:
                            dve.wait_ge(z_in, 16 * b + 16)
                            hold(dve, v_held, moved[0], 32 * TPB * (b + 1))
                            add_experts(zx, TPB * b)
                            dve.sem_inc(z_ready, 1)
                last = finish(TPB - 1)
                if last_half:
                    own(last)
                    add_experts(x, TPB * (b + b0))
                    dve.sem_inc(x_ready, 1)
                else:
                    last.then_inc(x_ready, 1)
                assert steps[0] == V_N, steps[0]


def load_expert(pool, io, keep, scr, e):
    arrived = keep["expert_in"][e % 2]
    pool.dma_start(keep["experts"][:, e % 2, :, :].bitcast(F32), scr["experts"][e]).then_inc(arrived, 16)
    pool.dma_start(keep["expert_bias"][:, e % 2, :],
                   io["expert_bias"][e:e + 1, :].to_broadcast([P, BIASES])).then_inc(arrived, 16)


def moe(nc, io, keep, scr, psum):
    ctx = ExitStack()

    def sb(name, shape, dt=F32):
        return ctx.enter_context(nc.sbuf_tensor(name, shape, dt))

    def sem(name):
        return ctx.enter_context(nc.semaphore(name))

    B = psum["T"] + psum["G"]
    W = [w[:, k:k + 512] for w in psum["S"] for k in (0, 512)]
    T = B[0:2]
    YB = [B[2][:, 0:DIM], B[3][:, 0:DIM]]
    H = [(W[0], W[1]), (W[2], W[3])]
    ident, experts, table = keep["ident"], keep["experts"], keep["tile_expert"]
    brow = keep["expert_bias"]
    RING = 8
    with ctx:
        xs = sb("xs_ring", [P, RING, DIM])
        xT = sb("xsT", [P, 2, 2, DC, P], F32R)
        h1 = sb("h1", [P, 2, HID])
        h3 = sb("h3", [P, 2, HID])
        g = sb("g", [P, 2, HID])
        gT = sb("gsT", [P, 2, 2, HC, P], F32R)
        y = sb("ys_ring", [P, RING, DIM])
        expert_ready, loader_held = sem("expert_ready"), sem("loader_held")
        x_high, g_high = sem("slots_high_ready"), sem("gated_high_ready")
        x_in = [sem(f"slots_in{i}") for i in range(RING)]
        y_out = [sem(f"slots_out{i}") for i in range(RING)]
        xt_done, xt_taken = sem("slots_transposed"), sem("slots_transposes_taken")
        h_done, h1_ready, h_taken, s_ready, g_ready = (sem("hidden_done"), sem("h1_biased"), sem("hidden_taken"),
                                                       sem("silu_ready"), sem("gated"))
        gt_done, gt_taken = sem("gated_transposed"), sem("gated_transposes_taken")
        y_done, y_taken = sem("expert_out_done"), sem("expert_out_taken")
        block = ctx.enter_context(nc.Block())
        xs_d = scr["xs"].rearrange("(s p) d -> s p d", p=P)
        ys_d = scr["ys"].rearrange("(s p) d -> s p d", p=P)
        ROUNDS = SLOTS_T // RING
        assert ROUNDS * RING == SLOTS_T

        def expert(eng, s):
            return eng.value_load(table[0:1, bass.ds(s, 1)], min_val=0, max_val=E - 1)

        def every_tile(eng, step):
            with eng.Fori(0, ROUNDS - 1) as r:
                for k in range(RING):
                    step(RING * r + k, r, k, False)
            for k in range(RING):
                step(RING * (ROUNDS - 1) + k, ROUNDS - 1, k, True)

        @block.sync
        def _(sp):
            for k in range(RING):
                sp.dma_start(xs[:, k, :], xs_d[k]).then_inc(x_in[k], 16)
            for k in range(RING):
                sp.sem_inc(y_out[k], 16)

            def step(s, r, k, last):
                if not last:
                    sp.wait_ge(xt_done, s + 1)
                    sp.dma_start(xs[:, k, :], xs_d[bass.ds(s + RING, 1)].rearrange("o p d -> p (o d)")).then_inc(x_in[k], 16)
                sp.wait_ge(y_taken, s + 1 + 2)
                sp.dma_start(ys_d[bass.ds(s, 1)].rearrange("o p d -> p (o d)"), y[:, k, :]).then_inc(y_out[k], 16)

            every_tile(sp, step)
            for k in range(RING):
                sp.wait_ge(y_out[k], 16 * ROUNDS + 16)

        @block.gpsimd
        def _(pool):
            for e in range(E):
                if e >= 2:
                    end = pool.value_load(keep["expert_end"][0:1, e - 2:e - 1], min_val=0, max_val=SLOTS_T)
                    hold(pool, loader_held, y_taken, end + 2)
                    load_expert(pool, io, keep, scr, e)
                pool.wait_ge(keep["expert_in"][e % 2], 32 * (e // 2 + 1))
                pool.sem_inc(expert_ready, 1)

        @block.tensor
        def _(pe):
            mm, tr = nc.tensor.matmul, nc.tensor.transpose

            def rows(s, r, k):
                pe.wait_ge(x_in[k], 16 * (r + 1))
                pe.wait_ge(xt_taken, s + 1)
                for c in range(DC):
                    last = tr(T[0][:, c * P:(c + 1) * P], xs[:, k, c * P:(c + 1) * P], ident[:])
                last.then_inc(xt_done, 1)

            def times(o, parts, e, at, n, first, last):
                for q, (i, w) in enumerate(((0, 0), (0, 1), (1, 0))):
                    moving = experts[:, bass.ds(e % 2, 1), w, at:at + n].rearrange("p o n -> p (o n)")
                    ins = mm(o, parts[i], moving, start=(first and q == 0), stop=(last and q == 2))
                return ins

            def hidden(s, k, e, m):
                if m == 0:
                    pe.wait_ge(xt_taken, s + 1 + 1)
                    pe.wait_ge(h_taken, s + 1)
                    pe.wait_ge(expert_ready, e + 1)
                for c in range(DC):
                    last = times(H[k % 2][m], [xT[:, k % 2, i, c, :] for i in range(2)], e, (DC * m + c) * HID, HID,
                                 c == 0, c == DC - 1)
                last.then_inc(h_done, 1)

            current = [None]
            rows(0, 0, 0)
            rows(1, 0, 1)
            first = expert(pe, 0)
            hidden(0, 0, first, 0)
            hidden(0, 0, first, 1)

            def step(s, r, k, last):
                following = not last or k + 1 < RING
                if not last or k + 2 < RING:
                    rows(s + 2, r + (k + 2) // RING, (k + 2) % RING)
                e = expert(pe, s) if k == 0 else current[0]
                if following:
                    current[0] = expert(pe, s + 1)
                pe.wait_ge(g_ready, s + 1)
                pe.wait_ge(gt_taken, s + 1)
                for c in range(HC):
                    ins = tr(T[1][:, c * P:(c + 1) * P], g[:, k % 2, c * P:(c + 1) * P], ident[:])
                ins.then_inc(gt_done, 1)
                if following:
                    hidden(s + 1, k + 1, current[0], 0)
                    hidden(s + 1, k + 1, current[0], 1)
                pe.wait_ge(gt_taken, s + 1 + 1)
                pe.wait_ge(y_taken, s + 1)
                for c in range(HC):
                    ins = times(YB[k % 2], [gT[:, k % 2, i, c, :] for i in range(2)], e, 2 * DC * HID + c * DIM, DIM,
                                c == 0, c == HC - 1)
                ins.then_inc(y_done, 1)

            every_tile(pe, step)

        @block.scalar
        def _(act):
            def copy(o, i):
                return nc.scalar.activation(o, i, ACT.Copy)

            def rows(s, k):
                act.wait_ge(xt_done, s + 1)
                copy(xT[:, k % 2, 0, :, :].rearrange("p c q -> p (c q)"), T[0][:, 0:DIM]).then_inc(x_high, 1)

            def silu(s, k):
                act.wait_ge(h1_ready, s + 1)
                nc.scalar.activation(h1[:, k % 2, :], h1[:, k % 2, :], ACT.Silu).then_inc(s_ready, 1)

            rows(0, 0)
            rows(1, 1)
            silu(0, 0)

            def step(s, r, k, last):
                if not last or k + 2 < RING:
                    rows(s + 2, k)
                act.wait_ge(gt_done, s + 1)
                copy(gT[:, k % 2, 0, :, :].rearrange("p c q -> p (c q)"), T[1][:]).then_inc(g_high, 1)
                if not last or k + 1 < RING:
                    silu(s + 1, k + 1)

            every_tile(act, step)

        @block.vector
        def _(dve):
            tt = nc.vector.tensor_tensor

            def bias(e, at, n):
                return brow[:, bass.ds(e % 2, 1), at:at + n].rearrange("p o n -> p (o n)")

            def low(parts, bank, high, taken, s):
                dve.wait_ge(high, s + 1)
                flat = [parts[i].rearrange("p c q -> p (c q)") for i in range(2)]
                tt(flat[1], bank, flat[0], ALU.subtract).then_inc(taken, 1)

            def rows(s, k):
                low([xT[:, k % 2, i, :, :] for i in range(2)], T[0][:, 0:DIM], x_high, xt_taken, s)

            def h1_bias(s, k):
                e = expert(dve, s)
                dve.wait_ge(expert_ready, e + 1)
                dve.wait_ge(h_done, 2 * s + 1)
                tt(h1[:, k % 2, :], H[k % 2][0], bias(e, 0, HID), ALU.add).then_inc(h1_ready, 1)
                return e

            def gate(s, k, e):
                i = k % 2
                dve.wait_ge(h_done, 2 * s + 2)
                tt(h3[:, i, :], H[i][1], bias(e, HID, HID), ALU.add).then_inc(h_taken, 1)
                dve.wait_ge(h_taken, s + 1 + 2)
                dve.wait_ge(s_ready, s + 1)
                tt(g[:, i, :], h1[:, i, :], h3[:, i, :], ALU.mult).then_inc(g_ready, 1)

            dve.sem_inc(h_taken, 2)
            dve.sem_inc(y_taken, 2)
            dve.sem_inc(xt_taken, 1)
            dve.sem_inc(gt_taken, 1)
            rows(0, 0)
            rows(1, 1)
            gate(0, 0, h1_bias(0, 0))

            def step(s, r, k, last):
                following = not last or k + 1 < RING
                if not last or k + 2 < RING:
                    rows(s + 2, k)
                low([gT[:, k % 2, i, :, :] for i in range(2)], T[1][:], g_high, gt_taken, s)
                if following:
                    e1 = h1_bias(s + 1, k + 1)
                    gate(s + 1, k + 1, e1)
                e = expert(dve, s)
                dve.wait_ge(y_done, s + 1)
                dve.wait_ge(y_out[k], 16 * r + 16)
                tt(y[:, k, :], YB[k % 2], bias(e, 2 * HID, DIM), ALU.add).then_inc(y_taken, 1)

            every_tile(dve, step)


def constants():
    i = np.arange(P)
    distance = np.minimum(np.abs(i[:, None] - i[None, :]), MAXREL)
    same = i[:, None] // GROUP == i[None, :] // GROUP
    position = np.arange(SEQ, dtype=np.float32)
    half = QK // 2
    angle = position[:, None] * (10000.0 ** (-np.arange(half, dtype=np.float32) / half)).astype(np.float32)[None, :]
    cos, sin = np.cos(angle), np.sin(angle)
    rope = np.stack([np.concatenate([cos, cos], 1), np.concatenate([-sin, sin], 1)])
    f = np.float32
    return {
        "ident": np.eye(P, dtype=f),
        "causal": np.where(i[None, :] <= i[:, None], 0.0, MASKED).astype(f),
        "before": (i[:, None] < i[None, :]).astype(f),
        "ones": np.ones((P, P), f),
        "iota8": np.broadcast_to(np.arange(E, dtype=f), (P, E)),
        "iotaT": np.broadcast_to(np.arange(SLOTS_T + 8, dtype=f), (P, SLOTS_T + 8)),
        "band": ((distance[:, None, :] == np.arange(MAXREL + 1)[None, :, None]) & same[:, None, :]).astype(f),
        "same_group": same.astype(f),
        "rope": rope.reshape(2, TPB, P, QK).transpose(2, 0, 1, 3).astype(f),
    }


_INS = [
    "L0_attn_x", "L0_attn_Wq", "L0_attn_Wk", "L0_attn_Wv", "L0_attn_Wfc", "L0_attn_bfc",
    "L0_attn_gamma", "L0_attn_beta", "L0_ffn_W1", "L0_ffn_b1", "L0_ffn_W2", "L0_ffn_b2",
    "L1_attn_ln1_w", "L1_attn_ln1_b", "L1_attn_Wqk", "L1_attn_bqk", "L1_attn_Wv", "L1_attn_bv",
    "L1_attn_Wg", "L1_attn_bg", "L1_attn_Wo", "L1_attn_bo", "L1_attn_ln2_w", "L1_attn_ln2_b",
    "L1_attn_gamma", "L1_attn_beta", "L1_attn_pos_emb", "L1_ffn_Wg", "L1_ffn_W1", "L1_ffn_b1",
    "L1_ffn_A1", "L1_ffn_B1", "L1_ffn_W2", "L1_ffn_b2", "L1_ffn_A2", "L1_ffn_B2", "L1_ffn_W3",
    "L1_ffn_b3", "L1_ffn_A3", "L1_ffn_B3",
]
_OUTS = [((BATCH, SEQ, DIM), "float32")]


def kernel(**inputs):
    import concourse.bacc as _bacc
    from concourse.bass_utils import run_bass_kernel_spmd as _run

    nc = _bacc.Bacc("TRN2", target_bir_lowering=False, num_devices=1)
    arrays, io = {}, {}
    data = {n: np.asarray(inputs[n]) for n in _INS}
    laid = {"cols0": np.concatenate([data[n].reshape(-1, P) for n in ("L0_attn_gamma", "L0_attn_beta", "L0_ffn_b1")]).T,
            "cols1": np.concatenate([data[n].reshape(-1, P) for n in ("L1_attn_ln1_w", "L1_attn_ln1_b", "L1_attn_bg")]).T,
            "expert_bias": np.concatenate([data[n] for n in ("L1_ffn_b1", "L1_ffn_b3", "L1_ffn_b2")], 1)}
    for n in ("L0_attn_bfc", "L0_ffn_b2", "L1_attn_pos_emb", *ROWS1):
        data[n] = data[n].reshape(1, -1)
    for n, a in {**data, **laid, **constants()}.items():
        a = np.ascontiguousarray(a)
        arrays[f"in_{n}"] = a
        io[n] = nc.dram_tensor(f"in_{n}", a.shape, mybir.dt.from_np(a.dtype), kind="ExternalInput").ap()
    out = nc.dram_tensor("out_0_dram", (BATCH, SEQ, DIM), F32, kind="ExternalOutput").ap()
    build(nc, io, out)
    r = _run(nc, [arrays], core_ids=[0])
    return r.results[0]["out_0_dram"]
```

```python
import numpy as np
import concourse.bass as bass
from concourse import mybir
from contextlib import ExitStack

F32 = mybir.dt.float32
I32 = mybir.dt.int32
F32R = mybir.dt.float32r
ALU = mybir.AluOpType
ACT = mybir.ActivationFunctionType
AX = mybir.AxisListType

P = 128
BATCH, SEQ, DIM = 4, 1024, 256
TOKENS = BATCH * SEQ
TPB = SEQ // P
TILES = TOKENS // P
DC = DIM // P
INTER = 1024
IC = INTER // P
E, HID, R, TOPK = 8, 512, 16, 2
HC = HID // P
EXPERT = 3 * DC * HID
BIASES = 2 * HID + DIM
PIECE = 32
STACK = 3 * PIECE
QK, H1, GROUP, MAXREL = 64, 512, 64, 32
EC = H1 // P
SLOTS_T = TOKENS * TOPK // P + E
SLOTS = SLOTS_T * P
EPS = 1e-5
MASKED = -3.0e38


ROWS1 = {}
ROWS1_N = 0
for _name, _length in (("L1_attn_bv", H1), ("L1_attn_bqk", QK), ("L1_attn_bo", DIM), ("L1_attn_ln2_w", DIM),
                       ("L1_attn_ln2_b", DIM), ("L1_attn_gamma", 4 * QK), ("L1_attn_beta", 4 * QK)):
    ROWS1[_name] = (ROWS1_N, _length)
    ROWS1_N += _length


LAYER0_UNITS = """
    XT:0 XT:1 VV:0 XT:2 VV:1 XT:3 VV:2 PT:0 PT:2 VV:3 PT:1 PT:3 S:0 S:1 ET:0
    TP:0 W1:0 W1:1 S:2 W1:2 W1:3 EP:0 EP:1 AV:0
    TP:1 ET:1 W1:4 W1:5 EL:0 EL:1 S:3 W1:6 W1:7 LT:0 EP:2 EP:3 AV:1 EL:2 FC:0 ET:2
    TP:2 W2:0 EL:3 W2:1 EP:4 LT:1 EP:5 AV:2 S:4 EL:4 FC:1 ET:3
    TP:3 W2:2 S:5 LT:2 EL:5 EP:6 W2:3 FC:2 EP:7 AV:3 ET:4 EL:6 W1:8
    TP:4 EL:7 S:6 W1:9 LT:3 EP:8 EP:9 AV:4 ET:5 FC:3 W1:10
    TP:5 EL:8 EL:9 S:7 W1:11 LT:4 EP:10 AV:5
    TP:6 EL:10 W1:12 W1:13 FC:4 EP:11 LT:5 AV:6 EL:11 W1:14 FC:5
    TP:7 W1:15 LT:6 AV:7 FC:6 W2:4 W2:5 LT:7 W2:6 W2:7 FC:7
"""


def units_of_batch():
    return [(kind, int(n)) for kind, n in (u.split(":") for u in LAYER0_UNITS.split())]


def hold(engine, passed, semaphore, value):
    engine.wait_ge(semaphore, value)
    engine.sem_inc(passed, 1)


def t_uses(unit):
    kind, n = unit
    if kind == "TP":
        return n // 4 + 1
    return 1 if kind in ("XT", "LT", "ET", "EP") else 0


def high_parts(unit):
    kind, n = unit
    if kind == "TP":
        return n // 4 + 1
    return 1 if kind in ("XT", "PT", "VV", "LT", "EL") else 0


def normed_rows(order):
    out = []
    for at, (kind, n) in enumerate(order):
        if kind == "AV":
            out.append(("attn", n))
        elif kind in ("W2", "FC") and ("FC" if kind == "W2" else "W2", n) in order[:at]:
            out.append(("x1", n))
    return out


def g_uses(unit):
    return 1 if unit[0] in ("PT", "VV", "AV", "FC", "W1", "W2", "EP") else 0


def numbered(order, uses):
    at, out = 0, {}
    for u in order:
        out[u] = at
        at += uses(u)
    return out, at


def build(nc, io, out):
    ctx = ExitStack()

    def sb(name, shape, dt=F32, at=ctx):
        return at.enter_context(nc.sbuf_tensor(name, shape, dt))

    def sem(name):
        return ctx.enter_context(nc.semaphore(name))

    with ctx:
        bank = [ctx.enter_context(nc.psum_tensor(f"bank{i}", [P, 512], F32)) for i in range(4, 8)]
        wide = [ctx.enter_context(nc.psum_tensor(f"wide{i}", [P, 1024], F32)) for i in range(2)]
        psum = {"T": bank[0:2], "G": bank[2:4], "S": wide}
        keep = {
            "held": {e: sem(f"{e}_held") for e in ("tensor", "vector", "gpsimd")},
            "ident": sb("ident", [P, P]),
            "varn": sb("xn1_var", [P, TILES]),
        }
        scr = {
            "x1": nc.dram_tensor("x1_scratch", [TOKENS, DIM], F32).ap(),
            "xn1": nc.dram_tensor("xn1_scratch", [TOKENS, DIM], F32).ap(),
            "x2": nc.dram_tensor("x2_scratch", [TOKENS // 2, DIM], F32).ap(),
            "xs": nc.dram_tensor("slot_rows_scratch", [SLOTS, DIM], F32).ap(),
            "ys": nc.dram_tensor("slot_results_scratch", [SLOTS, DIM], F32).ap(),
            "experts": nc.dram_tensor("experts_scratch", [E, P, 2, EXPERT], F32).ap(),
        }
        layer0(nc, io, keep, scr, psum)
        keep.update({
            "r2": sb("r2", [P, TILES]),
            "wv1": sb("wv1", [P, DC, H1]), "wg1": sb("wg1", [P, DC, H1]), "wqk1": sb("wqk1", [P, DC, QK]),
            "wo1": sb("wo1", [P, EC, DIM]), "rout": sb("router", [P, DC, E]),
            "cols1": sb("cols1", [P, 8]),
            "rows1": sb("rows1", [P, ROWS1_N]),
            "same": sb("same_group", [P, P]), "bias": sb("distance_bias", [P, P]),
            "rope": sb("rope", [P, 2, TPB, QK]),
            "gates": sb("gates", [P, TOPK, TILES]), "slot": sb("slot", [P, TOPK, TILES], I32),
            "tile_rank": sb("tile_rank", [P, SLOTS_T], I32),
            "rank_expert": sb("rank_expert", [P, E], I32), "rank_end": sb("rank_end", [P, E], I32),
        })
        for half in (0, 2):
            keep[f"rows_in{half}"] = (sem(f"xn_in_{half}"), sem(f"x1_in_{half}"))
        keep["stored"] = sem("x2_stored")
        keep["u"] = sb("u", [P, TPB, DIM])
        keep["x"] = sb("x1b", [P, TPB, DIM])
        route(nc, io, keep, scr, psum)
        with ExitStack() as held:
            keep["experts"] = sb("expert_ring", [P, 2, 2, EXPERT], F32R, held)
            keep["expert_bias"] = sb("expert_bias", [P, 2, BIASES], F32, held)
            keep["expert_in"] = [held.enter_context(nc.semaphore(f"expert_in{i}")) for i in range(2)]
            attention(nc, io, keep, scr, psum, 0, out)
            moe(nc, io, keep, scr, psum)
        attention(nc, io, keep, scr, psum, 2, out)


VPRE, VN = 5, 68


def layer0(nc, io, keep, scr, psum):
    ctx = ExitStack()

    def sb(name, shape, dt=F32):
        return ctx.enter_context(nc.sbuf_tensor(name, shape, dt))

    def sem(name):
        return ctx.enter_context(nc.semaphore(name))

    ORDER = units_of_batch()
    T_AT, T_N = numbered(ORDER, t_uses)
    G_AT, G_N = numbered(ORDER, g_uses)
    H_AT, H_N = numbered(ORDER, high_parts)
    assert T_N % 2 == 0 and G_N % 2 == 0
    T, G, S = psum["T"], psum["G"], psum["S"]
    ident = keep["ident"]

    with ctx:
        wv = sb("wv", [P, 2, DC, DIM], F32R)
        wfc = sb("wfc", [P, 2, DC, DIM], F32R)
        w1 = sb("w1", [P, 2, DC, INTER], F32R)
        w2 = sb("w2", [P, 2, IC, DIM], F32R)
        wqk = sb("wqk_product", [P, 2, DC, DIM], F32R)
        cols = sb("cols", [P, 12])
        crow = sb("crow", [P, DIM])
        mask = sb("mask", [P, P])
        xb = sb("xb", [P, 2, TPB, DIM])
        xp = sb("xp", [P, 2, SEQ])
        xnT = sb("xnT", [P, 2, DC, SEQ], F32R)
        pT = sb("pT", [P, 2, DC, SEQ], F32R)
        v = sb("v", [P, 2, TPB, DIM], F32R)
        prT = sb("prT", [P, 2, TPB, P], F32R)
        hT = sb("hT", [P, 2, IC, 512], F32R)
        hid = sb("hid", [P, 2, 512])
        xn1 = sb("xn1", [P, TPB, DIM])
        res = sb("res", [P, DIM])
        lnT = sb("lnT", [P, 2, DIM], F32R)
        raw = sb("raw", [P, 2, 2 * HID])
        rawA = sb("rawA", [P, 2, HID])
        rawB = sb("rawB", [P, 2, HC, R])
        highB = sb("highB", [P, HC, R], F32R)
        partsB = sb("partsB", [P, 2, HC, STACK])
        partsA = sb("partsA", [P, 2, HID], F32R)
        partsBT = sb("partsBT", [P, HID], F32R)
        fold = sb("fold", [P, 2, 512])
        folds = sb("folded_matrix", [P, 2, 2 * HID], F32R)
        st = sb("st", [P, TPB, 6])
        mv = sb("mv", [P, TPB, 2])
        ve = sb("ve", [P, TPB])
        rs = sb("rs", [P, TPB])
        sta = sb("sta", [P, 2, 6])
        mva = sb("mva", [P, 2, 2])
        vea = sb("vea", [P, 2])
        rsa = sb("rsa", [P, 2])
        st1 = sb("st1", [P, 2, 6])
        mv1 = sb("mv1", [P, TPB, 2])
        ve1 = sb("ve1", [P, TPB])
        rs1 = sb("rs1", [P, TPB])
        varn = sb("varn", [P, TPB])
        half = sb("half", [P, TPB])
        mx = sb("mx", [P, 2])
        nmx = sb("nmx", [P, 2])
        rsum = sb("rsum", [P, 4])
        rinv = sb("rinv", [P, 2])

        prob = xp
        xn = xp[:].rearrange("p a (t d) -> p (a t) d", d=DIM)
        w10 = xb[:, 1, :, :].rearrange("p t d -> p (t d)").rearrange("p (c n) -> p c n", c=DC)
        w20 = xn1[:]
        wq0, wk0, wv0, wfc0 = (raw[:, k // 2, k % 2 * HID:(k % 2 + 1) * HID].rearrange("p (c n) -> p c n", c=DC)
                               for k in range(4))
        wqT, wkT = (fold[:, k, :].rearrange("p (c n) -> p c n", c=DC) for k in range(2))
        beta_rows = hid[:, 0, 0:DC * P].rearrange("p (c n) -> p c n", c=DC)
        rows = hid[:, 1, :].rearrange("p (c n) -> p c n", c=2)

        attn_w_in, ffn_w_in, const_in = sem("attn_weights_in"), sem("ffn_weights_in"), sem("consts_in")
        x_in, x1_stored, xn1_stored = sem("x_in"), sem("x1_stored"), sem("xn1_stored")
        matrix_in = [sem(f"matrix_in{i}") for i in range(2)]
        matrix_out, matrix_ready = sem("matrix_out"), sem("matrix_parts_ready")
        factors_ready = sem("factors_ready")
        p_step, p_held, v_held = sem("gpsimd_step"), keep["held"]["gpsimd"], keep["held"]["vector"]
        wT_done, wT_copied = sem("wqk_transposed"), sem("wqk_transposes_copied")
        pre_done, wqk_high, wqk_split = sem("pre_products_done"), sem("wqk_high"), sem("wqk_split")
        attn_split, ffn_high, ffn_split = sem("attn_weights_split"), sem("ffn_weights_high"), sem("ffn_weights_split")
        beta_spread, half_ready, zeroed = sem("beta_spread"), sem("half_ready"), sem("slots_zeroed")
        t_done, g_done = [[sem(f"{n}_done{i}") for i in range(2)] for n in ("transposes", "product")]
        t_taken, g_taken = [[sem(f"{n}_taken{i}") for i in range(2)] for n in ("transposes", "product")]
        high_ready, hid_low = sem("high_ready"), sem("hidden_low_ready")
        s_done, max_ready, probs_ready = sem("scores_done"), sem("max_ready"), sem("probs_ready")
        var_ready, rstd_ready, xn_ready, bias_added = (sem("var_ready"), sem("rstd_ready"), sem("xn_ready"),
                                                       sem("bias_added"))
        avar_ready, arstd_ready, ln_ready = sem("attn_var_ready"), sem("attn_rstd_ready"), sem("attn_normalised")
        var1_ready, rstd1_ready, xn1_ready = sem("var1_ready"), sem("rstd1_ready"), sem("xn1_ready")
        v_step = sem("vector_step")

        block = ctx.enter_context(nc.Block())
        x_b = io["L0_attn_x"].rearrange("b (t p) d -> b p t d", p=P)
        x1_b = scr["x1"].rearrange("(b t p) d -> b p t d", p=P, t=TPB)
        xn1_b = scr["xn1"].rearrange("(b t p) d -> b p t d", p=P, t=TPB)

        def t_use(b, u, k, extra):
            n = T_AT[u] + k
            return n % 2, (T_N // 2) * b + n // 2 + 1 + extra

        def g_use(b, u, extra):
            n = G_AT[u]
            return n % 2, (G_N // 2) * b + n // 2 + 1 + extra

        def is_done(b, u, k=0):
            i, n = g_use(b, u, 0) if u in g_units else t_use(b, u, k, 0)
            return (g_done if u in g_units else t_done)[i], n

        def taken_t(b, u, k=0):
            i, n = t_use(b, u, k, 1)
            return t_taken[i], n

        def taken_g(b, u):
            i, n = g_use(b, u, 1)
            return g_taken[i], n

        def is_high(b, u, k=0):
            return high_ready, H_N * b + H_AT[u] + k + 1

        g_units = {u for u in ORDER if g_uses(u) and not t_uses(u)}

        def x_half(b):
            return xb[:, bass.ds(b % 2, 1), :, :].rearrange("p o t d -> p (o t) d")

        def fold_part(n, part):
            return folds[:, part, (n % 2) * 512:(n % 2 + 1) * 512]

        @block.sync
        def _(sp):
            def load_matrix(b, j):
                e, m = 2 * b + j // 3, j % 3
                name = ("1", "3", "2")[m]
                k = DC if m == 2 else HC
                arrived = matrix_in[j % 2]
                sp.dma_start(raw[:, j % 2, :].rearrange("p (c n) -> p c n", c=k),
                             io["L1_ffn_W" + name][bass.ds(e, 1)].rearrange("e (c p) n -> p (e c) n", p=P)
                             ).then_inc(arrived, 16)
                for part in range(3):
                    sp.dma_start(rawA[PIECE * part:PIECE * part + R, j % 2, 0:DIM if m < 2 else HID],
                                 io["L1_ffn_A" + name][bass.ds(e, 1)].rearrange("e r n -> (e r) n")).then_inc(arrived, 16)
                sp.dma_start(rawB[:, j % 2, 0:k, :],
                             io["L1_ffn_B" + name][bass.ds(e, 1)].rearrange("e (c p) r -> p (e c) r", p=P)
                             ).then_inc(arrived, 16)

            def store_matrix(b, j):
                e, m = 2 * b + j // 3, j % 3
                sp.wait_ge(matrix_ready, 12 * b + 2 * j + 2 + 2)
                sp.dma_start(scr["experts"][bass.ds(e, 1), :, :, 2 * HID * m:2 * HID * (m + 1)].rearrange("e p h n -> (e p) h n"),
                             folds[:].bitcast(F32)).then_inc(matrix_out, 16)

            def store(b):
                sp.wait_ge(var1_ready, TPB * b + TPB)
                sp.dma_start(x1_b[bass.ds(b, 1)].rearrange("o p t d -> p (o t) d"), x_half(b)).then_inc(x1_stored, 16)
                sp.wait_ge(xn1_ready, TPB * b + TPB)
                sp.dma_start(xn1_b[bass.ds(b, 1)].rearrange("o p t d -> p (o t) d"), xn1[:]).then_inc(xn1_stored, 16)

            sp.dma_start(xb[:, 0, :, :], x_b[0]).then_inc(x_in, 16)
            sp.dma_start(ident[:], io["ident"]).then_inc(attn_w_in, 16)
            sp.dma_start(wq0, io["L0_attn_Wq"].rearrange("(c p) k -> p c k", p=P)).then_inc(attn_w_in, 16)
            sp.dma_start(wk0, io["L0_attn_Wk"].rearrange("(c p) k -> p c k", p=P)).then_inc(attn_w_in, 16)
            sp.dma_start(wv0, io["L0_attn_Wv"].rearrange("(c p) k -> p c k", p=P)).then_inc(const_in, 16)
            sp.dma_start(wfc0, io["L0_attn_Wfc"].rearrange("(c p) k -> p c k", p=P)).then_inc(const_in, 16)
            sp.dma_start(cols[:], io["cols0"]).then_inc(const_in, 16)
            sp.dma_start(rows[:, 0, :], io["L0_attn_bfc"].to_broadcast([P, DIM])).then_inc(const_in, 16)
            sp.dma_start(rows[:, 1, :], io["L0_ffn_b2"].to_broadcast([P, DIM])).then_inc(const_in, 16)
            sp.dma_start(mask[:], io["causal"]).then_inc(const_in, 16)
            sp.dma_start(w10, io["L0_ffn_W1"].rearrange("(c p) k -> p c k", p=P)).then_inc(ffn_w_in, 16)
            sp.dma_start(w20, io["L0_ffn_W2"].rearrange("(c p) k -> p c k", p=P)).then_inc(ffn_w_in, 16)
            for start_full in (x1_stored, xn1_stored, matrix_out):
                sp.sem_inc(start_full, 16)
            sp.wait_ge(half_ready, 3)
            sp.wait_ge(wT_done, 2)
            load_matrix(0, 0)
            sp.wait_ge(attn_split, 3)
            load_matrix(0, 1)

            def batch(b, last):
                if not last:
                    sp.wait_ge(var_ready, b + 1)
                    sp.wait_ge(x1_stored, 16 * b + 16)
                    sp.dma_start(x_half(b + 1), x_b[bass.ds(b + 1, 1)].rearrange("o p t d -> p (o t) d")).then_inc(x_in, 16)
                else:
                    sp.wait_ge(half_ready, 4)
                    sp.dma_start(scr["xs"].rearrange("(p s) d -> p (s d)", p=P).rearrange("p (k n) -> p k n", n=TPB * DIM),
                                 xb[:, BATCH % 2, :, :].rearrange("p t d -> p (t d)").unsqueeze(1).to_broadcast(
                                     [P, SLOTS_T // TPB, TPB * DIM])).then_inc(zeroed, 16)
                for j in range(6):
                    if not last or j < 4:
                        sp.wait_ge(*taken_g(b, ("EP", 2 * j + 1)))
                        load_matrix(b, j + 2)
                    store_matrix(b, j)
                store(b)

            sp.wait_ge(ffn_split, 2)
            with sp.Fori(0, BATCH - 1) as b:
                batch(b, False)
            batch(BATCH - 1, True)
            sp.wait_ge(matrix_out, 16 * (6 * BATCH + 1))
            sp.wait_ge(zeroed, 16)
            sp.wait_ge(x1_stored, 16 * BATCH + 16)
            sp.wait_ge(xn1_stored, 16 * BATCH + 16)

        @block.gpsimd
        def _(pool):
            tt = nc.gpsimd.tensor_tensor
            steps = [0]

            def factors(b, j):
                def own(ins):
                    steps[0] += 1
                    ins.then_inc(p_step, 1)
                    hold(pool, p_held, p_step, 18 * b + steps[0])

                i, k, w = j % 2, DC if j % 3 == 2 else HC, HID if j % 3 == 2 else DIM
                hold(pool, p_held, matrix_in[i], 80 * (3 * b + j // 2 + 1))
                nc.gpsimd.tensor_copy(partsA[:, i, 0:w], rawA[:, i, 0:w])
                own(nc.gpsimd.tensor_copy(highB[:, 0:k, :], rawB[:, i, 0:k, :]))
                pieces = partsB[:, i, 0:k, :].rearrange("p c (s w) -> p c s w", w=PIECE)
                nc.gpsimd.tensor_copy(pieces[:, :, 0:2, 0:R], highB[:, 0:k, :].unsqueeze(2).to_broadcast([P, k, 2, R]))
                own(tt(pieces[:, :, 2, 0:R], rawB[:, i, 0:k, :], highB[:, 0:k, :], ALU.subtract))
                low = slice(PIECE, 2 * PIECE)
                own(tt(partsA[low, i, 0:w], rawA[low, i, 0:w], partsA[low, i, 0:w], ALU.subtract))
                pool.sem_inc(factors_ready, 1)

            def rstd(b):
                pool.wait_ge(var_ready, b + 1)
                tt(rs[:], ve[:], half[:], ALU.pow).then_inc(rstd_ready, 1)

            nc.gpsimd.memset(half[:], -0.5).then_inc(half_ready, 1)
            nc.gpsimd.memset(rawA[:], 0.0).then_inc(half_ready, 1)
            nc.gpsimd.memset(partsB[:], 0.0).then_inc(half_ready, 1)
            pool.wait_ge(half_ready, 3)
            rstd(0)
            pool.wait_ge(ffn_high, 1)
            tt(w1[:, 1, :, :], w10, w1[:, 0, :, :], ALU.subtract).then_inc(ffn_split, 1)
            pool.wait_ge(ffn_high, 2)
            tt(w2[:, 1, :, :], w20, w2[:, 0, :, :], ALU.subtract).then_inc(ffn_split, 1)
            pool.wait_ge(ffn_split, 2)
            pool.wait_ge(attn_split, 3)

            def batch(b, last):
                steps[0] = 0
                factors(b, 0)
                factors(b, 1)
                for t in range(TPB):
                    pool.wait_ge(xn_ready, TPB * b + t + 1)
                    xs = xb[:, bass.ds(b % 2, 1), t, :].rearrange("p o d -> p (o d)")
                    tt(xs, xs, crow[:], ALU.add).then_inc(bias_added, 1)
                for kind, n in normed_rows(ORDER):
                    if kind == "attn":
                        pool.wait_ge(avar_ready, TPB * b + n + 1)
                        tt(rsa[:, n % 2:n % 2 + 1], vea[:, n % 2:n % 2 + 1], half[:, 0:1], ALU.pow).then_inc(arstd_ready, 1)
                        if n == 0 and last:
                            pool.wait_ge(x1_stored, 16 * BATCH)
                            nc.gpsimd.memset(xb[:, BATCH % 2, :, :], 0.0).then_inc(half_ready, 1)
                        if n == 5 and not last:
                            rstd(b + 1)
                        if n < 6:
                            for k in (2 * n, 2 * n + 1):
                                pool.wait_ge(*is_high(b, ("EL", k)))
                                tt(fold_part(k, 1), fold[:, k % 2, :], fold_part(k, 0), ALU.subtract).then_inc(matrix_ready, 1)
                        if n + 2 < 6:
                            factors(b, n + 2)
                    else:
                        pool.wait_ge(var1_ready, TPB * b + n + 1)
                        tt(rs1[:, n:n + 1], ve1[:, n:n + 1], half[:, 0:1], ALU.pow).then_inc(rstd1_ready, 1)

            pool.sem_inc(matrix_ready, 2)
            with pool.Fori(0, BATCH - 1) as b:
                batch(b, False)
            batch(BATCH - 1, True)

        @block.tensor
        def _(pe):
            mm, tr = nc.tensor.matmul, nc.tensor.transpose

            def times(o, stationary, moving, first, last):
                for q, (i, j) in enumerate(((0, 0), (0, 1), (1, 0))):
                    ins = mm(o, stationary(i), moving(j), start=(first and q == 0), stop=(last and q == 2))
                return ins

            pe.wait_ge(attn_w_in, 48)
            for n, w in enumerate((wq0, wk0)):
                for kc in range(DC):
                    for c in range(DC):
                        last = tr(S[n][:, (kc * DC + c) * P:(kc * DC + c + 1) * P], w[:, c, kc * P:(kc + 1) * P], ident[:])
                last.then_inc(wT_done, 1)
            pe.wait_ge(wT_copied, 2)
            for c in range(DC):
                for kc in range(DC):
                    last = mm(G[0][:, c * DIM:(c + 1) * DIM], wqT[:, kc, c * P:(c + 1) * P], wkT[:, kc, :],
                              start=(kc == 0), stop=(kc == DC - 1))
            last.then_inc(pre_done, 1)
            pe.wait_ge(const_in, 96)
            pe.wait_ge(beta_spread, 1)
            for c in range(DC):
                last = mm(G[1][:, 0:DIM], beta_rows[:, c, :], wfc0[:, c, :], start=(c == 0), stop=(c == DC - 1))
            last.then_inc(pre_done, 1)
            pe.wait_ge(wqk_split, 1)

            with pe.Fori(0, BATCH) as b:
                def t_bank(u, k=0):
                    i, n = t_use(b, u, k, 0)
                    pe.wait_ge(t_taken[i], n)
                    return T[i], t_done[i]

                def g_bank(u):
                    i, n = g_use(b, u, 0)
                    pe.wait_ge(g_taken[i], n)
                    return G[i], g_done[i]

                for u in ORDER:
                    kind, n = u
                    if kind == "XT":
                        pe.wait_ge(xn_ready, TPB * b + 2 * n + 2)
                        o, done = t_bank(u)
                        for c in range(DC):
                            for t in range(2):
                                last = tr(o[:, (2 * c + t) * P:(2 * c + t + 1) * P], xn[:, 2 * n + t, c * P:(c + 1) * P], ident[:])
                        last.then_inc(done, 1)
                    elif kind == "PT":
                        c2, h = n // 2, n % 2
                        pe.wait_ge(*taken_t(b, ("XT", 2 * h + 1)))
                        o, done = g_bank(u)
                        for c in range(DC):
                            last = times(o[:], lambda i: wqk[:, i, c, c2 * P:(c2 + 1) * P],
                                         lambda i: xnT[:, i, c, h * 512:(h + 1) * 512], c == 0, c == DC - 1)
                        last.then_inc(done, 1)
                    elif kind == "VV":
                        if n == 0:
                            pe.wait_ge(attn_split, 3)
                        pe.wait_ge(*taken_t(b, ("XT", n)))
                        o, done = g_bank(u)
                        for t in range(2):
                            for c in range(DC):
                                last = times(o[:, t * DIM:(t + 1) * DIM],
                                             lambda i: xnT[:, i, c, (2 * n + t) * P:(2 * n + t + 1) * P],
                                             lambda i: wv[:, i, c, :], c == 0, c == DC - 1)
                        last.then_inc(done, 1)
                    elif kind == "S":
                        pe.wait_ge(probs_ready, TPB * b + n + 1)
                        if n in (0, 4):
                            both = ("PT", n // 4), ("PT", 2 + n // 4)
                            pe.wait_ge(*taken_g(b, max(both, key=ORDER.index)))
                        keys = (n + 1) * P
                        for k0 in range(0, keys, 512):
                            k1 = min(max(keys, k0 + 2 * P), k0 + 512)
                            for c in range(DC):
                                last = times(S[n % 2][:, k0:k1], lambda i: pT[:, i, c, n * P:(n + 1) * P],
                                             lambda i: xnT[:, i, c, k0:k1], c == 0, c == DC - 1)
                        last.then_inc(s_done, 1)
                    elif kind == "TP":
                        pe.wait_ge(probs_ready, TPB * b + n + 1 + 2)
                        for k in range(n // 4 + 1):
                            o, done = t_bank(u, k)
                            for m in range(4 * k, min(n + 1, 4 * k + 4)):
                                last = tr(o[:, (m % 4) * P:(m % 4 + 1) * P], prob[:, n % 2, m * P:(m + 1) * P], ident[:])
                            last.then_inc(done, 1)
                    elif kind == "AV":
                        pe.wait_ge(*taken_t(b, ("TP", n), n // 4))
                        vv = ("VV", n // 2)
                        if n % 2 == 0 and G_AT[vv] % 2 != G_AT[u] % 2:
                            pe.wait_ge(*taken_g(b, vv))
                        o, done = g_bank(u)
                        for m in range(n + 1):
                            last = times(o[:, 0:DIM], lambda i: prT[:, i, m, :], lambda i: v[:, i, m, :], m == 0, m == n)
                        last.then_inc(done, 1)
                    elif kind == "LT":
                        pe.wait_ge(ln_ready, TPB * b + n + 1)
                        o, done = t_bank(u)
                        for c in range(DC):
                            last = tr(o[:, c * P:(c + 1) * P], res[:, c * P:(c + 1) * P], ident[:])
                        last.then_inc(done, 1)
                    elif kind == "FC":
                        pe.wait_ge(*taken_t(b, ("LT", n)))
                        o, done = g_bank(u)
                        for c in range(DC):
                            last = times(o[:, 0:DIM], lambda i: lnT[:, i, c * P:(c + 1) * P], lambda i: wfc[:, i, c, :],
                                         c == 0, c == DC - 1)
                        last.then_inc(done, 1)
                    elif kind == "W1":
                        h, i1 = n // IC, n % IC
                        if n == 0:
                            pe.wait_ge(ffn_split, 2)
                        o, done = g_bank(u)
                        for c in range(DC):
                            last = times(o[:], lambda i: w1[:, i, c, i1 * P:(i1 + 1) * P],
                                         lambda i: xnT[:, i, c, h * 512:(h + 1) * 512], c == 0, c == DC - 1)
                        last.then_inc(done, 1)
                    elif kind == "W2":
                        h, t = n // 4, n % 4
                        pe.wait_ge(hid_low, 2 * IC * b + IC * (h + 1) + 2)
                        o, done = g_bank(u)
                        for c in range(IC):
                            last = times(o[:, 0:DIM], lambda i: hT[:, i, c, t * P:(t + 1) * P], lambda i: w2[:, i, c, :],
                                         c == 0, c == IC - 1)
                        last.then_inc(done, 1)
                    elif kind == "ET":
                        pe.wait_ge(factors_ready, 6 * b + n + 1)
                        o, done = t_bank(u)
                        for c in range(DC if n % 3 == 2 else HC):
                            last = tr(o[0:STACK, c * P:(c + 1) * P], partsB[:, n % 2, c, :], ident[:])
                        last.then_inc(done, 1)
                    elif kind == "EP":
                        j, c = n // 2, n % 2
                        A, BT = partsA[0:STACK, j % 2, :], partsBT[0:STACK, :]
                        o, done = t_bank(u)
                        if j % 3 < 2:
                            for h in range(HC):
                                last = tr(o[:, h * P:(h + 1) * P],
                                          raw[:, j % 2, h * DIM + c * P:h * DIM + (c + 1) * P], ident[:])
                        else:
                            for h in range(2):
                                for d in range(DC):
                                    last = tr(o[:, (DC * h + d) * P:(DC * h + d + 1) * P],
                                              raw[:, j % 2, d * HID + (2 * c + h) * P:d * HID + (2 * c + h + 1) * P], ident[:])
                        last.then_inc(done, 1)
                        pe.wait_ge(*taken_t(b, ("ET", j)))
                        o, done = g_bank(u)
                        if j % 3 < 2:
                            last = mm(o[:], A[:, c * P:(c + 1) * P], BT, start=True, stop=True)
                        else:
                            for h in range(2):
                                last = mm(o[:, h * DIM:(h + 1) * DIM], A[:, (2 * c + h) * P:(2 * c + h + 1) * P],
                                          BT[:, 0:DIM], start=True, stop=True)
                        last.then_inc(done, 1)

        @block.scalar
        def _(act):
            def copy(o, i):
                return nc.scalar.activation(o, i, ACT.Copy)

            for n, w in enumerate((wqT, wkT)):
                act.wait_ge(wT_done, n + 1)
                copy(w, S[n][:, 0:512].rearrange("p (k d) -> p k d", k=DC)).then_inc(wT_copied, 1)
            act.wait_ge(pre_done, 1)
            copy(wqk[:, 0, :, :].rearrange("p c d -> p (c d)"), G[0][:]).then_inc(wqk_high, 1)
            act.wait_ge(ffn_w_in, 32)
            copy(w1[:, 0, :, :], w10).then_inc(ffn_high, 1)
            copy(w2[:, 0, :, :], w20).then_inc(ffn_high, 1)
            act.sem_inc(probs_ready, 2)
            for i in range(2):
                act.sem_inc(t_taken[i], 1)
                act.sem_inc(g_taken[i], 1)
            act.wait_ge(const_in, 96)
            with act.Fori(0, BATCH) as b:
                def bank(u, k=0, g=False):
                    i, n = g_use(b, u, 0) if g else t_use(b, u, k, 0)
                    act.wait_ge((g_done if g else t_done)[i], n)
                    return (G if g else T)[i]

                def exp(i):
                    act.wait_ge(max_ready, TPB * b + i + 1)
                    nc.scalar.activation(prob[:, i % 2, 0:(i + 1) * P], S[i % 2][:, 0:(i + 1) * P], ACT.Exp,
                                         bias=nmx[:, i % 2:i % 2 + 1], scale=1.0 / 16.0,
                                         accum_out=rsum[:, i % 4:i % 4 + 1]).then_inc(probs_ready, 1)

                for u in ORDER:
                    kind, n = u
                    if kind == "XT":
                        copy(xnT[:, 0, :, 2 * n * P:(2 * n + 2) * P],
                             bank(u)[:].rearrange("p (c t) -> p c t", c=DC)).then_inc(high_ready, 1)
                    elif kind == "PT":
                        copy(pT[:, 0, n // 2, (n % 2) * 512:(n % 2 + 1) * 512], bank(u, g=True)[:]).then_inc(high_ready, 1)
                    elif kind == "VV":
                        copy(v[:, 0, 2 * n:2 * n + 2, :].rearrange("p t d -> p (t d)"), bank(u, g=True)[:]).then_inc(high_ready, 1)
                    elif kind == "S" and n < 2:
                        exp(n)
                    elif kind == "AV" and n + 2 < TPB:
                        exp(n + 2)
                    elif kind == "TP":
                        for k in range(n // 4 + 1):
                            m0, m1 = 4 * k, min(n + 1, 4 * k + 4)
                            copy(prT[:, 0, m0:m1, :].rearrange("p m q -> p (m q)"),
                                 bank(u, k)[:, 0:(m1 - m0) * P]).then_inc(high_ready, 1)
                    elif kind == "LT":
                        copy(lnT[:, 0, :], bank(u)[:, 0:DIM]).then_inc(high_ready, 1)
                    elif kind == "W1":
                        o, bias = bank(u, g=True), cols[:, 4 + n % IC:5 + n % IC]
                        act.wait_ge(hid_low, 2 * IC * b + n + 1)
                        nc.scalar.activation(hT[:, 0, n % IC, :], o[:], ACT.Relu, bias=bias)
                        nc.scalar.activation(hid[:, n % 2, :], o[:], ACT.Relu, bias=bias).then_inc(taken_g(b, u)[0], 1)
                    elif kind == "ET":
                        w = DIM if n % 3 == 2 else HID
                        copy(partsBT[0:STACK, 0:w], bank(u)[0:STACK, 0:w]).then_inc(taken_t(b, u)[0], 1)
                    elif kind == "EP":
                        act.wait_ge(matrix_ready, 12 * b + n + 1)
                        copy(fold[:, n % 2, :], bank(u)[:]).then_inc(taken_t(b, u)[0], 1)
                    elif kind == "EL":
                        act.wait_ge(*taken_g(b, ("EP", n)))
                        if n % 2 == 0:
                            act.wait_ge(matrix_out, 16 * (6 * b + n // 2 + 1))
                        copy(fold_part(n, 0), fold[:, n % 2, :]).then_inc(high_ready, 1)

        @block.vector
        def _(dve):
            tt, ts = nc.vector.tensor_tensor, nc.vector.tensor_scalar
            steps = [0]

            def own(ins, b=None):
                steps[0] += 1
                ins.then_inc(v_step, 1)
                hold(dve, v_held, v_step, steps[0] if b is None else VPRE - 2 + VN * b + steps[0])

            def statistics(nb, tiles):
                for t in tiles:
                    last = nc.vector.bn_stats(st[:, t, :], xb[:, bass.ds(nb % 2, 1), t, :].rearrange("p o d -> p (o d)"))
                return last

            def variances(b, last):
                own(last, b)
                for t in range(TPB):
                    last = nc.vector.bn_aggr(mv[:, t, :], st[:, t, :])
                own(last, b)
                ts(ve[:], mv[:, :, 1], EPS, None, ALU.add).then_inc(var_ready, 1)

            def normalise(nb, tiles):
                dve.wait_ge(rstd_ready, nb + 1)
                for t in tiles:
                    ts(xn[:, t, :], xb[:, bass.ds(nb % 2, 1), t, :].rearrange("p o d -> p (o d)"), mv[:, t, 0:1],
                       rs[:, t:t + 1], ALU.subtract, ALU.mult).then_inc(xn_ready, 1)

            hold(dve, v_held, x_in, 16)
            variances(None, statistics(0, range(TPB)))
            normalise(0, range(TPB))
            dve.wait_ge(const_in, 96)
            dve.wait_ge(attn_w_in, 48)
            for c in range(DC):
                last = ts(beta_rows[:, c, :], ident[:], 0.0, cols[:, 2 + c:3 + c], ALU.mult, ALU.add)
            last.then_inc(beta_spread, 1)
            own(tt(crow[:], rows[:, 0, :], rows[:, 1, :], ALU.add))
            dve.wait_ge(wqk_high, 1)
            tt(wqk[:, 1, :, :].rearrange("p c d -> p (c d)"), G[0][:], wqk[:, 0, :, :].rearrange("p c d -> p (c d)"),
               ALU.subtract).then_inc(wqk_split, 1)
            dve.wait_ge(pre_done, 2)
            tt(crow[:], crow[:], G[1][:, 0:DIM], ALU.add).then_inc(attn_split, 1)
            for c in range(DC):
                last = ts(wfc0[:, c, :], wfc0[:, c, :], cols[:, c:c + 1], None, ALU.mult)
            nc.vector.tensor_copy(wv[:, 0, :, :], wv0)
            own(last)
            own(nc.vector.tensor_copy(wfc[:, 0, :, :], wfc0))
            tt(wv[:, 1, :, :], wv0, wv[:, 0, :, :], ALU.subtract).then_inc(attn_split, 1)
            tt(wfc[:, 1, :, :], wfc0, wfc[:, 0, :, :], ALU.subtract).then_inc(attn_split, 1)
            assert steps[0] == VPRE, steps[0]

            def normalise1(of, n):
                if n == 0:
                    hold(dve, v_held, xn1_stored, 16 * of + 16)
                dve.wait_ge(rstd1_ready, TPB * of + n + 1)
                ts(xn1[:, n, :], xb[:, bass.ds(of % 2, 1), n, :].rearrange("p o d -> p (o d)"), mv1[:, n, 0:1],
                   rs1[:, n:n + 1], ALU.subtract, ALU.mult).then_inc(xn1_ready, 1)

            def finish_xn1(b, of):
                normalise1(of, TPB - 1)
                own(tt(varn[:], mv1[:, :, 1], rs1[:], ALU.mult), b)
                own(tt(keep["varn"][:, bass.ds(TPB * of, TPB)], varn[:], rs1[:], ALU.mult), b)

            def batch(b, first_batch, last_batch):
                steps[0] = 2 if first_batch else 0

                def x_tile(t):
                    return xb[:, bass.ds(b % 2, 1), t, :].rearrange("p o d -> p (o d)")

                def low(parts, o, u, k=0, g=False):
                    dve.wait_ge(*is_high(b, u, k))
                    tt(parts(1), o, parts(0), ALU.subtract).then_inc(taken_g(b, u)[0] if g else taken_t(b, u, k)[0], 1)

                def g_full(u):
                    i, n = g_use(b, u, 0)
                    dve.wait_ge(g_done[i], n)
                    return G[i]

                def x1_whole(n):
                    own(nc.vector.bn_stats(st1[:, n % 2, :], x_tile(n)), b)
                    own(nc.vector.bn_aggr(mv1[:, n, :], st1[:, n % 2, :]), b)
                    ts(ve1[:, n:n + 1], mv1[:, n, 1:2], EPS, None, ALU.add).then_inc(var1_ready, 1)

                for u in ORDER:
                    kind, n = u
                    if kind == "XT":
                        low(lambda i: xnT[:, i, :, 2 * n * P:(2 * n + 2) * P],
                            T[t_use(b, u, 0, 0)[0]][:].rearrange("p (c t) -> p c t", c=DC), u)
                    elif kind == "PT":
                        low(lambda i: pT[:, i, n // 2, (n % 2) * 512:(n % 2 + 1) * 512], G[G_AT[u] % 2][:], u, g=True)
                    elif kind == "VV":
                        low(lambda i: v[:, i, 2 * n:2 * n + 2, :].rearrange("p t d -> p (t d)"), G[G_AT[u] % 2][:], u, g=True)
                    elif kind == "S":
                        i = n % 2
                        dve.wait_ge(s_done, TPB * b + n + 1)
                        diag = S[i][:, n * P:(n + 1) * P]
                        own(tt(diag, diag, mask[:], ALU.add), b)
                        own(nc.vector.reduce_max(mx[:, i:i + 1], S[i][:, 0:(n + 1) * P], AX.X), b)
                        ts(nmx[:, i:i + 1], mx[:, i:i + 1], -1.0 / 16.0, None, ALU.mult).then_inc(max_ready, 1)
                    elif kind == "TP":
                        for k in range(n // 4 + 1):
                            m0, m1 = 4 * k, min(n + 1, 4 * k + 4)
                            low(lambda i: prT[:, i, m0:m1, :].rearrange("p m q -> p (m q)"),
                                T[(T_AT[u] + k) % 2][:, 0:(m1 - m0) * P], u, k)
                    elif kind == "AV":
                        i = n % 2
                        o = g_full(u)
                        own(nc.vector.reciprocal(rinv[:, i:i + 1], rsum[:, n % 4:n % 4 + 1]), b)
                        nc.vector.scalar_tensor_tensor(out=res[:], in0=o[:, 0:DIM], scalar=rinv[:, i:i + 1],
                                                       in1=v[:, 0, n, :], op0=ALU.mult, op1=ALU.add).then_inc(taken_g(b, u)[0], 1)
                        hold(dve, v_held, *taken_g(b, u))
                        own(tt(res[:], res[:], v[:, 1, n, :], ALU.add), b)
                        own(nc.vector.bn_stats(sta[:, i, :], res[:]), b)
                        own(nc.vector.bn_aggr(mva[:, i, :], sta[:, i, :]), b)
                        ts(vea[:, i:i + 1], mva[:, i, 1:2], EPS, None, ALU.add).then_inc(avar_ready, 1)
                        dve.wait_ge(arstd_ready, TPB * b + n + 1)
                        ts(res[:], res[:], mva[:, i, 0:1], rsa[:, i:i + 1], ALU.subtract, ALU.mult).then_inc(ln_ready, 1)
                        if 2 <= n < 6 and not last_batch:
                            if n == 2:
                                hold(dve, v_held, x_in, 16 * b + 32)
                                hold(dve, v_held, xn_ready, TPB * b + TPB)
                            last = statistics(b + 1, (2 * n - 4, 2 * n - 3))
                            if n == 5:
                                variances(b, last)
                    elif kind == "LT":
                        low(lambda i: lnT[:, i, :], T[T_AT[u] % 2][:, 0:DIM], u)
                    elif kind in ("W2", "FC"):
                        o = g_full(u)
                        other = ("FC" if kind == "W2" else "W2", n)
                        second = ORDER.index(other) < ORDER.index(u)
                        if second:
                            dve.wait_ge(*taken_g(b, other))
                        else:
                            dve.wait_ge(bias_added, TPB * b + n + 1)
                        tt(x_tile(n), x_tile(n), o[:, 0:DIM], ALU.add).then_inc(taken_g(b, u)[0], 1)
                        if second:
                            hold(dve, v_held, *taken_g(b, u))
                            x1_whole(n)
                    elif kind == "W1":
                        dve.wait_ge(*taken_g(b, u))
                        tt(hT[:, 1, n % IC, :], hid[:, n % 2, :], hT[:, 0, n % IC, :], ALU.subtract).then_inc(hid_low, 1)
                    elif kind == "EP":
                        o = g_full(u)
                        dve.wait_ge(*taken_t(b, u))
                        tt(fold[:, n % 2, :], fold[:, n % 2, :], o[:], ALU.add).then_inc(taken_g(b, u)[0], 1)
                    if not last_batch and u == ("FC", 6):
                        hold(dve, v_held, *taken_t(b, ("TP", 7), 1))
                        normalise(b + 1, range(0, 4))
                    if not last_batch and u == ("W2", 4):
                        normalise(b + 1, range(4, TPB))
                    if u == ("W2", 5):
                        for t in range(4):
                            normalise1(b, t)
                    if u == ("W2", 6):
                        normalise1(b, 4)
                    if u == ("W2", 7):
                        normalise1(b, 5)
                        normalise1(b, 6)
                    if u == ("XT", 3) and not first_batch:
                        finish_xn1(b, b - 1)
                assert last_batch or steps[0] == VN, steps[0]
                if last_batch:
                    finish_xn1(b, b)

            dve.sem_inc(hid_low, 2)
            batch(0, True, False)
            with dve.Fori(1, BATCH - 1) as b:
                batch(b, False, False)
            batch(BATCH - 1, False, True)


def route(nc, io, keep, scr, psum):
    ctx = ExitStack()

    def sb(name, shape, dt=F32):
        return ctx.enter_context(nc.sbuf_tensor(name, shape, dt))

    def sem(name):
        return ctx.enter_context(nc.semaphore(name))

    T, S = psum["T"], psum["S"]
    CNT = psum["G"][0]
    ident = keep["ident"]
    wv1, wg1, wqk1, wo1, rout = keep["wv1"], keep["wg1"], keep["wqk1"], keep["wo1"], keep["rout"]
    cols, row = keep["cols1"], keep["rows1"]
    with ctx:
        raw = sb("raw1", [P, 3, EC, DIM])
        rawqk = sb("rawqk", [QK + E, DIM])
        posb = sb("posb", [P, 2 * MAXREL + 1])
        band = sb("band", [P, MAXREL + 1, P])
        spread = sb("spread", [P, DC, P])
        xt = sb("xt", [P, 2, TPB, DIM])
        xT = sb("xT", [P, 2, 2, DC, P])
        logit = sb("logit", [P, TILES, E])
        top = sb("top", [P, TILES, 8])
        topi = sb("topi", [P, TILES, 8], mybir.dt.uint32)
        before, ones, iota8, iotaT = (sb("before", [P, P]), sb("ones", [P, P]), sb("iota8", [P, E]),
                                      sb("iotaT", [P, SLOTS_T]))
        first, second, both = (sb(n, [P, TILES, E]) for n in ("chosen1", "chosen2", "chosen"))
        idx = sb("idx", [P, TOPK, TILES])
        diff = sb("diff", [P, TILES])
        cum = sb("cum", [P, 2, TILES, E])
        pos = sb("pos", [P, TILES, E])
        tot = sb("tot", [P, TILES, E])
        te = sb("te", [P, 6, E])
        ti = sb("ti", [P, 2, E], I32)
        ge = sb("ge", [P, SLOTS_T, E])
        upto_rank = sb("upto_rank", [P, E, SLOTS_T])
        rank = sb("rank", [P, 3, E])
        chosen_by = sb("chosen_by", [P, E, E])
        last_rank = sb("last_rank", [P, 1])
        slotf = sb("slotf", [P, TOPK, TILES])
        tilef = sb("tilef", [P, SLOTS_T])

        w_in, r_in, c_in = sem("l1_weights_in"), sem("rows_in"), sem("route_consts_in")
        x_in = [sem(f"xn1_in{i}") for i in range(2)]
        wt_done, wt_taken, spread_ready, rowprod, folded = (sem("l1_transposed"), sem("l1_transposes_taken"),
            sem("ln1_bias_spread"), sem("l1_bias_products"), sem("l1_folded"))
        t_done, t_taken, l_done, l_taken = (sem("xn1_transposed"), sem("xn1_transposes_taken"), sem("logits_done"),
                                            sem("logits_taken"))
        chosen, counted, diff_ready, gates_ready = (sem("experts_chosen"), sem("choices_counted"), sem("diff_ready"),
                                                    sem("gates_ready"))
        v_step, varn_ready, r2_ready = sem("route_step"), sem("xn1_var_ready"), sem("r2_ready")
        half = sb("half2", [P, TILES])
        scaled, bias_ready = sem("band_scaled"), sem("distance_bias_ready")
        block = ctx.enter_context(nc.Block())
        xn1_b = scr["xn1"].rearrange("(b t p) d -> b p t d", p=P, t=TPB)

        @block.sync
        def _(sp):
            sp.dma_start(rawqk[0:QK, :], io["L1_attn_Wqk"]).then_inc(w_in, 16)
            sp.dma_start(rawqk[QK:QK + E, :], io["L1_ffn_Wg"]).then_inc(w_in, 16)
            sp.dma_start(raw[:, 0, :, :], io["L1_attn_Wv"].rearrange("(c p) n -> p c n", p=P)).then_inc(w_in, 16)
            sp.dma_start(raw[:, 1, :, :], io["L1_attn_Wg"].rearrange("(c p) n -> p c n", p=P)).then_inc(w_in, 16)
            sp.dma_start(raw[:, 2, :, :].rearrange("p e d -> p (e d)").rearrange("p (c n) -> p c n", c=DC),
                         io["L1_attn_Wo"].rearrange("(c p) n -> p c n", p=P)).then_inc(w_in, 16)
            sp.dma_start(cols[:], io["cols1"]).then_inc(r_in, 16)
            sp.dma_start(xt[:, 0, :, :], xn1_b[0]).then_inc(x_in[0], 16)
            for name, a in ROWS1.items():
                sp.dma_start(row[:, a[0]:a[0] + a[1]], io[name].to_broadcast([P, a[1]])).then_inc(r_in, 16)
            for n, t in (("before", before), ("ones", ones), ("iota8", iota8), ("iotaT", iotaT)):
                sp.dma_start(t[:], io[n]).then_inc(c_in, 16)
            sp.dma_start(band[:], io["band"]).then_inc(c_in, 16)
            sp.dma_start(keep["same"][:], io["same_group"]).then_inc(c_in, 16)
            sp.dma_start(keep["rope"][:], io["rope"]).then_inc(c_in, 16)
            sp.dma_start(posb[:], io["L1_attn_pos_emb"].to_broadcast([P, 2 * MAXREL + 1])).then_inc(c_in, 16)
            for b in range(1, BATCH):
                if b >= 2:
                    sp.wait_ge(t_taken, 4 * (b - 1))
                sp.dma_start(xt[:, b % 2, :, :], xn1_b[b]).then_inc(x_in[b % 2], 16)
            load_rows(sp, keep, scr, "u", 0, 0)
            load_rows(sp, keep, scr, "x", 0, 0)

        @block.gpsimd
        def _(pool):
            nc.gpsimd.memset(half[:], -0.5).then_inc(varn_ready, 1)
            pool.wait_ge(varn_ready, 2)
            nc.gpsimd.tensor_tensor(keep["r2"][:], keep["varn"][:], half[:], ALU.pow).then_inc(r2_ready, 1)
            ts, tt = nc.gpsimd.tensor_scalar, nc.gpsimd.tensor_tensor
            pool.wait_ge(c_in, 16 * 8)
            ts(band[:, 0, :], band[:, 0, :], posb[:, 0:1], None, ALU.mult)
            for k in range(1, MAXREL + 1):
                ts(band[:, k, :], band[:, k, :], posb[:, k:k + 1], None, ALU.mult).then_inc(scaled, 1)
            terms, k = MAXREL, 0
            while terms > 1:
                pool.wait_ge(scaled, MAXREL + k)
                terms, k = terms // 2, k + 1
                tt(band[:, 1:terms + 1, :], band[:, 1:terms + 1, :], band[:, terms + 1:2 * terms + 1, :], ALU.add).then_inc(scaled, 1)
            pool.wait_ge(scaled, MAXREL + k)
            tt(keep["bias"][:], band[:, 0, :], band[:, 1, :], ALU.add).then_inc(bias_ready, 1)

        def logit_bank(n):
            return S[n // 2 % 2][:, n % 2 * 512:n % 2 * 512 + 2 * E]

        def logits_of(pe, n):
            pe.wait_ge(t_taken, n + 1)
            if n >= 4:
                pe.wait_ge(l_taken, n - 3)
            for t in range(2):
                for c in range(DC):
                    last = nc.tensor.matmul(logit_bank(n)[:, t * E:(t + 1) * E], xT[:, n % 2, t, c, :],
                                            rout[:, c, :], start=(c == 0), stop=(c == DC - 1))
            last.then_inc(l_done, 1)

        @block.tensor
        def _(pe):
            mm, tr = nc.tensor.matmul, nc.tensor.transpose
            pe.wait_ge(w_in, 80)
            for c in range(DC):
                last = tr(T[0][:, c * (QK + E):(c + 1) * (QK + E)], rawqk[:, c * P:(c + 1) * P], ident[0:QK + E, 0:QK + E])
            last.then_inc(wt_done, 1)
            n = 1
            for w in range(2):
                for c in range(DC):
                    if n >= 2:
                        pe.wait_ge(wt_taken, n - 1)
                    for e in range(EC):
                        last = tr(T[n % 2][:, e * P:(e + 1) * P], raw[:, w, e, c * P:(c + 1) * P], ident[:])
                    last.then_inc(wt_done, 1)
                    n += 1
            wo_raw = raw[:, 2, :, :].rearrange("p e d -> p (e d)")
            for e2 in range(2):
                pe.wait_ge(wt_taken, n - 1)
                for e in range(2):
                    for c in range(DC):
                        last = tr(T[n % 2][:, (DC * e + c) * P:(DC * e + c + 1) * P],
                                  wo_raw[:, c * H1 + (2 * e2 + e) * P:c * H1 + (2 * e2 + e + 1) * P], ident[:])
                last.then_inc(wt_done, 1)
                n += 1
            pe.wait_ge(wt_taken, n)
            pe.wait_ge(spread_ready, 1)
            for c in range(DC):
                mm(S[0][:, 0:H1], spread[:, c, :], wv1[:, c, :], start=(c == 0), stop=(c == DC - 1))
            for c in range(DC):
                mm(S[0][:, 512:512 + QK], spread[:, c, :], wqk1[:, c, :], start=(c == 0), stop=(c == DC - 1))
            for e in range(EC):
                for c in range(DC):
                    last = mm(S[1][:, e:e + 1], wg1[:, c, e * P:(e + 1) * P], cols[:, 2 + c:3 + c],
                              start=(c == 0), stop=(c == DC - 1))
            last.then_inc(rowprod, 1)
            pe.wait_ge(folded, 1)
            for b in range(BATCH):
                pe.wait_ge(x_in[b % 2], 16 * (b // 2 + 1))
                for q in range(4):
                    n = 4 * b + q
                    if n >= 2:
                        pe.wait_ge(t_taken, n - 1)
                    for t in range(2):
                        for c in range(DC):
                            last = tr(T[n % 2][:, (DC * t + c) * P:(DC * t + c + 1) * P],
                                      xt[:, b % 2, 2 * q + t, c * P:(c + 1) * P], ident[:])
                    last.then_inc(t_done, 1)
                    if n >= 1:
                        logits_of(pe, n - 1)
            logits_of(pe, 4 * BATCH - 1)
            pe.wait_ge(chosen, 1)
            pe.wait_ge(c_in, 16 * 8)
            bo = both[:].rearrange("p t e -> p (t e)")
            mm(CNT[:, 0:TILES * E], before[:], bo, start=True, stop=True)
            mm(CNT[:, TILES * E:2 * TILES * E], ones[:], bo, start=True, stop=True).then_inc(counted, 1)

        @block.scalar
        def _(act):
            def copy(o, i):
                return nc.scalar.activation(o, i, ACT.Copy)

            act.wait_ge(wt_done, 1)
            t0 = T[0][:, 0:DC * (QK + E)].rearrange("p (c n) -> p c n", c=DC)
            copy(wqk1[:], t0[:, :, 0:QK])
            copy(rout[:], t0[:, :, QK:QK + E]).then_inc(wt_taken, 1)
            n = 1
            for w in (wv1, wg1):
                for c in range(DC):
                    act.wait_ge(wt_done, n + 1)
                    copy(w[:, c, :], T[n % 2][:]).then_inc(wt_taken, 1)
                    n += 1
            for e2 in range(2):
                act.wait_ge(wt_done, n + 1)
                copy(wo1[:, 2 * e2:2 * e2 + 2, :].rearrange("p e d -> p (e d)"), T[n % 2][:]).then_inc(wt_taken, 1)
                n += 1
            for n in range(4 * BATCH):
                act.wait_ge(t_done, n + 1)
                if n >= 2:
                    act.wait_ge(l_done, n - 1)
                copy(xT[:, n % 2, :, :, :].rearrange("p t c q -> p (t c q)"), T[n % 2][:]).then_inc(t_taken, 1)
            act.wait_ge(diff_ready, 1)
            for k in range(TOPK):
                last = nc.scalar.activation(keep["gates"][:, k, :], diff[:], ACT.Sigmoid, scale=(1.0 if k == 0 else -1.0))
            last.then_inc(gates_ready, 1)

        @block.vector
        def _(dve):
            steps = [0]
            tt, ts = nc.vector.tensor_tensor, nc.vector.tensor_scalar

            def own(ins):
                steps[0] += 1
                ins.then_inc(v_step, 1)
                dve.wait_ge(v_step, steps[0])

            ts(keep["varn"][:], keep["varn"][:], EPS, None, ALU.add).then_inc(varn_ready, 1)
            dve.wait_ge(r_in, 16 * (1 + len(ROWS1)))
            for c in range(DC):
                last = ts(spread[:, c, :], ident[:], 0.0, cols[:, 2 + c:3 + c], ALU.mult, ALU.add)
            last.then_inc(spread_ready, 1)
            dve.wait_ge(rowprod, 1)
            bv, bqk = ROWS1["L1_attn_bv"], ROWS1["L1_attn_bqk"]
            tt(row[:, bv[0]:bv[0] + bv[1]], row[:, bv[0]:bv[0] + bv[1]], S[0][:, 0:H1], ALU.add)
            tt(row[:, bqk[0]:bqk[0] + bqk[1]], row[:, bqk[0]:bqk[0] + bqk[1]], S[0][:, 512:512 + QK], ALU.add)
            tt(cols[:, 4:8], cols[:, 4:8], S[1][:, 0:EC], ALU.add).then_inc(folded, 1)
            for w in (wv1, wg1, wqk1):
                for c in range(DC):
                    last = ts(w[:, c, :], w[:, c, :], cols[:, c:c + 1], None, ALU.mult)
            own(last)
            for n in range(4 * BATCH):
                dve.wait_ge(l_done, n + 1)
                nc.vector.tensor_copy(logit[:, 2 * n:2 * n + 2, :].rearrange("p t e -> p (t e)"),
                                      logit_bank(n)).then_inc(l_taken, 1)
                dve.wait_ge(l_taken, n + 1)
                for t in (2 * n, 2 * n + 1):
                    last = nc.vector.max(top[:, t, :], logit[:, t, :])
                own(last)
                for t in (2 * n, 2 * n + 1):
                    last = nc.vector.max_index(topi[:, t, :], top[:, t, :], logit[:, t, :])
            own(last)
            dve.wait_ge(c_in, 16 * 8)
            tt(diff[:], top[:, :, 0], top[:, :, 1], ALU.subtract).then_inc(diff_ready, 1)
            for k in range(TOPK):
                last = nc.vector.tensor_copy(idx[:, k, :], topi[:, :, k])
            own(last)
            every = iota8[:].unsqueeze(1).to_broadcast([P, TILES, E])
            for k, m in enumerate((first, second)):
                last = tt(m[:], idx[:, k, :].unsqueeze(2).to_broadcast([P, TILES, E]), every, ALU.is_equal)
            own(last)
            tt(both[:], first[:], second[:], ALU.add).then_inc(chosen, 1)
            dve.wait_ge(counted, 1)
            tc = CNT[:, TILES * E:2 * TILES * E].rearrange("p (t e) -> p t e", e=E)
            nc.vector.tensor_copy(tot[:], tc)
            own(nc.vector.tensor_copy(cum[:, 0, :, :], tc))
            k, step = 0, 1
            while step < TILES:
                nc.vector.tensor_copy(cum[:, 1 - k, 0:step, :], cum[:, k, 0:step, :])
                own(tt(cum[:, 1 - k, step:, :], cum[:, k, step:, :], cum[:, k, 0:TILES - step, :], ALU.add))
                k, step = 1 - k, 2 * step
            own(ts(ti[:, 0, :], cum[:, k, TILES - 1, :], 127.0, None, ALU.add))
            own(ts(ti[:, 1, :], ti[:, 0, :], 7, None, ALU.arith_shift_right))
            nc.vector.tensor_copy(te[:, 5, :], ti[:, 1, :])
            own(nc.vector.tensor_copy(te[:, 0, :], ti[:, 1, :]))
            j, step = 0, 1
            while step < E:
                nc.vector.tensor_copy(te[:, 1 - j, 0:step], te[:, j, 0:step])
                own(tt(te[:, 1 - j, step:], te[:, j, step:], te[:, j, 0:E - step], ALU.add))
                j, step = 1 - j, 2 * step
            upto = te[:, j, :]
            own(ts(te[:, 4, :], te[:, 5, :], 0.0, None, ALU.is_gt))
            q, step = 0, 1
            own(nc.vector.tensor_copy(rank[:, 0, :], te[:, 4, :]))
            while step < E:
                nc.vector.tensor_copy(rank[:, 1 - q, 0:step], rank[:, q, 0:step])
                own(tt(rank[:, 1 - q, step:], rank[:, q, step:], rank[:, q, 0:E - step], ALU.add))
                q, step = 1 - q, 2 * step
            counts = rank[:, q, :]
            own(tt(chosen_by[:], iota8[:].unsqueeze(2).to_broadcast([P, E, E]),
                   counts.unsqueeze(1).to_broadcast([P, E, E]), ALU.is_ge))
            own(nc.vector.reduce_sum(rank[:, 2, :], chosen_by[:], AX.X))
            own(ts(keep["rank_expert"][:], rank[:, 2, :], float(E - 1), None, ALU.min))
            own(ts(last_rank[:], counts[:, E - 1:E], -1.0, None, ALU.add))
            own(tt(ge[:], iotaT[:].unsqueeze(2).to_broadcast([P, SLOTS_T, E]),
                   upto.unsqueeze(1).to_broadcast([P, SLOTS_T, E]), ALU.is_ge))
            own(tt(ge[:], ge[:], te[:, 4, :].unsqueeze(1).to_broadcast([P, SLOTS_T, E]), ALU.mult))
            own(nc.vector.reduce_sum(tilef[:], ge[:], AX.X))
            own(ts(tilef[:], tilef[:], last_rank[:, 0:1], None, ALU.min))
            own(nc.vector.tensor_copy(keep["tile_rank"][:], tilef[:]))
            own(tt(upto_rank[:], iota8[:].unsqueeze(2).to_broadcast([P, E, SLOTS_T]),
                   tilef[:].unsqueeze(1).to_broadcast([P, E, SLOTS_T]), ALU.is_ge))
            own(nc.vector.reduce_sum(rank[:, 2, :], upto_rank[:], AX.X))
            own(nc.vector.tensor_copy(keep["rank_end"][:], rank[:, 2, :]))
            own(tt(te[:, 2, :], upto, te[:, 5, :], ALU.subtract))
            own(ts(te[:, 3, :], te[:, 2, :], float(P), None, ALU.mult))
            own(tt(pos[:], cum[:, k, :, :], tot[:], ALU.subtract))
            own(tt(pos[:], pos[:], CNT[:, 0:TILES * E].rearrange("p (t e) -> p t e", e=E), ALU.add))
            own(tt(pos[:], pos[:], te[:, 3, :].unsqueeze(1).to_broadcast([P, TILES, E]), ALU.add))
            for m in (first, second):
                last = tt(m[:], m[:], pos[:], ALU.mult)
            own(last)
            for q, m in enumerate((first, second)):
                last = nc.vector.reduce_sum(slotf[:, q, :], m[:], AX.X)
            own(last)
            own(nc.vector.tensor_copy(keep["slot"][:], slotf[:]))
            dve.wait_ge(gates_ready, 1)
            dve.wait_ge(r2_ready, 1)
            dve.wait_ge(bias_ready, 1)


VB = (38, 54)


GB = 6


LAYER1_UNITS = """
    UT:0 UT:1 UT:2 UT:3 VV:0 QK:0 VV:1 VV:2 VV:3 GA:0 VV:4 GA:1 VV:5 GA:2 VV:6 GA:3 HT:0 HT:1 VV:7 HT:2
    HT:3 AT:0 AT:1 LK:0 OO:0 OO:1 OO:2 OO:3 GA:4 GA:5 YY:0 YY:1 YY:2 GA:6 YY:3 OO:4 OO:5 OO:6 GA:7 OO:7
    YY:4 YY:5 YY:6 YY:7
"""


def attention_units():
    return [(kind, int(n)) for kind, n in (u.split(":") for u in LAYER1_UNITS.split())]


class Products:

    def __init__(self, order, taker, banks, done, taken):
        self.order = [u for u in order if u[0] in taker]
        assert len(self.order) % banks == 0
        self.n, self.banks, self.done, self.sems = len(self.order), banks, done, taken
        self.at = {u: i for i, u in enumerate(self.order)}
        self.who = {u: taker[u[0]] for u in self.order}
        self.count = {e: sum(w == e for w in self.who.values()) for e in taken}

    def bank(self, u):
        return self.at[u] % self.banks

    def is_done(self, b, u):
        return self.done, self.n * b + self.at[u] + 1

    def is_taken(self, b, u):
        e = self.who[u]
        k = sum(self.who[w] == e for w in self.order[:self.at[u]])
        return self.sems[e], self.count[e] * (b + 1) + k + 1

    def is_free(self, b, u):
        i = self.at[u] - self.banks
        return self.is_taken(b, self.order[i]) if i >= 0 else self.is_taken(b - 1, self.order[i])


def load_rows(sp, keep, scr, what, half, b):
    rows = scr["xn1" if what == "u" else "x1"].rearrange("(b t p) d -> b p t d", p=P, t=TPB)
    sp.dma_start(keep[what][:], rows[bass.ds(half + b, 1)].rearrange("o p t d -> p (o t) d")
                 ).then_inc(keep[f"rows_in{half}"]["ux".index(what)], 16)


def attention(nc, io, keep, scr, psum, b0, out):
    ctx = ExitStack()
    tag = f"_{b0}"
    last_half = b0 > 0

    def sb(name, shape, dt=F32):
        return ctx.enter_context(nc.sbuf_tensor(name + tag, shape, dt))

    def sem(name):
        return ctx.enter_context(nc.semaphore(name + tag))

    NB = 2
    ORDER = attention_units()
    T_AT, T_N = numbered(ORDER, lambda u: 1 if u[0] in ("UT", "HT") else 0)
    T = psum["T"]
    banks = [psum["G"][0][:], psum["G"][1][:]] + [w[:, k:k + 512] for w in psum["S"] for k in (0, 512)]
    ident, wv1, wg1, wqk1, wo1 = (keep[n] for n in ("ident", "wv1", "wg1", "wqk1", "wo1"))
    cols, rows, rope = keep["cols1"], keep["rows1"], keep["rope"]

    def row(name):
        at, n = ROWS1[name]
        return rows[:, at:at + n]

    with ctx:
        u, x = keep["u"], keep["x"]
        uT = sb("uT", [P, DC, SEQ])
        qk = sb("qk", [P, TPB, QK])
        heads = sb("heads", [P, TPB, 4, QK])
        headT = sb("headT", [P, 2, SEQ])
        v = sb("v1", [P, TPB, H1])
        lkv = sb("lkv", [P, H1])
        att = sb("att", [P, TPB, P])
        attw = sb("attw", [P, 4, P])
        gT = sb("gT", [P, 4, 512])
        oT = heads[:].rearrange("p t h d -> p (t h d)").rearrange("p (e n) -> p e n", e=EC)
        y = sb("y1", [P, 2, DIM])
        sty = sb("sty", [P, 2, 6])
        mvy = sb("mvy", [P, 2, 2])
        vey = sb("vey", [P, 2])
        rsy = sb("rsy", [P, 2])
        half = sb("half1", [P, 1])
        ones = sb("ones1", [1, P])
        if last_half:
            zx = sb("first_half", [P, TPB, DIM])
            got = sb("expert_results", [P, TILES, TOPK, DIM])
        else:
            ring = sb("ring", [P, 4, DIM])

        (xn_in, x_in), stored = keep[f"rows_in{b0}"], sem("stored") if last_half else keep["stored"]
        u_ready, t_done, t_taken, g_done = sem("u_ready"), sem("transposed"), sem("transposes_taken"), sem("products_done")
        by_act, by_dve = sem("products_taken_by_scalar"), sem("products_taken_by_vector")
        qk_ready, v_ready = sem("qk_ready"), sem("v_ready")
        rotated, att_ready = sem("heads_rotated"), sem("att_ready")
        var_ready, rstd_ready, x_ready = sem("var_ready"), sem("rstd_ready"), sem("x_ready")
        v_step, v_held, half_ready = sem("vector_step"), keep["held"]["vector"], sem("half_ready")
        pe_held, zeros_ready = keep["held"]["tensor"], sem("zeros_ready")
        if last_half:
            x_biased, scaled, x_summed = sem("x_biased"), sem("results_scaled"), sem("experts_added")
            z_in, z_stored, z_ready = sem("first_half_in"), sem("first_half_stored"), sem("first_half_ready")
        else:
            ring_in = [sem(f"ring_in{i}") for i in range(4)]
        moved = [sem(f"rows_moved{i}") for i in range(2 if last_half else 4)]
        block = ctx.enter_context(nc.Block())
        pr = Products(ORDER, {"QK": "dve", "VV": "dve", "LK": "act", "AT": "dve", "GA": "act", "OO": "dve", "YY": "dve"},
                      GB, g_done, {"act": by_act, "dve": by_dve})
        x2_b = scr["x2"].rearrange("(b t p) d -> b p t d", p=P, t=TPB)
        out_b = out.rearrange("b (t p) d -> b p t d", p=P)

        @block.sync
        def _(sp):
            sp.sem_inc(stored, 16)
            if last_half:
                sp.sem_inc(z_stored, 16)

            def batch(b, last):
                if last_half:
                    sp.wait_ge(z_stored, 16 * b + 16)
                    sp.dma_start(zx[:], x2_b[bass.ds(b, 1)].rearrange("o p t d -> p (o t) d")).then_inc(z_in, 16)
                if not last:
                    sp.wait_ge(rotated, b + 1)
                    load_rows(sp, keep, scr, "u", b0, b + 1)
                if last_half:
                    sp.wait_ge(z_ready, b + 1)
                    sp.dma_start(out_b[bass.ds(b, 1)].rearrange("o p t d -> p (o t) d"), zx[:]).then_inc(z_stored, 16)
                sp.wait_ge(x_ready, b + 1)
                to = out_b if last_half else x2_b
                sp.dma_start(to[bass.ds(b + b0 if last_half else b, 1)].rearrange("o p t d -> p (o t) d"),
                             x[:]).then_inc(stored, 16)
                if not last:
                    sp.wait_ge(stored, 16 * b + 32)
                    load_rows(sp, keep, scr, "x", b0, b + 1)

            with sp.Fori(0, NB - 1) as b:
                batch(b, False)
            batch(NB - 1, True)
            if last_half:
                sp.wait_ge(stored, 16 * NB + 16)
                sp.wait_ge(z_stored, 16 * NB + 16)

        @block.gpsimd
        def _(pool):
            def index(k, t):
                return bass.IndirectOffsetOnAxis(ap=keep["slot"][:, k, t:t + 1], axis=0)

            def load(t):
                pool.dma_start(ring[:, t % 4, :], scr["xn1"][t * P:(t + 1) * P, :]).then_inc(ring_in[t % 4], 16)

            def scatter(t):
                pool.wait_ge(ring_in[t % 4], 16 * (t // 4 + 1))
                for k in range(TOPK):
                    nc.gpsimd.indirect_dma_start(out=scr["xs"], out_offset=index(k, t), in_=ring[:, t % 4, :],
                                                 in_offset=None, bounds_check=SLOTS - 1).then_inc(moved[t % 4], 16)

            def gather(t):
                for k in range(TOPK):
                    nc.gpsimd.indirect_dma_start(out=got[:, t, k, :], out_offset=None, in_=scr["ys"],
                                                 in_offset=index(k, t), bounds_check=SLOTS - 1).then_inc(moved[t // TPB // 2], 16)

            nc.gpsimd.memset(half[:], -0.5).then_inc(half_ready, 1)
            pool.wait_ge(half_ready, 1)
            if not last_half:
                for t in range(4):
                    load(t)
            for b in range(NB):
                if last_half:
                    for t in [TPB * b + t for t in range(TPB)] + [TPB * (b + b0) + t for t in range(TPB)]:
                        gather(t)
                else:
                    for t in range(2 * TPB * b, 2 * TPB * (b + 1)):
                        scatter(t)
                        if 2 <= t and t + 2 < TILES:
                            pool.wait_ge(moved[(t - 2) % 4], 32 * ((t - 2) // 4 + 1))
                            load(t + 2)
                    if b == NB - 1:
                        for j in range(2):
                            load_expert(pool, io, keep, scr, j)
                if last_half:
                    pool.wait_ge(x_biased, b + 1)
                    for k in range(TOPK):
                        for t in range(TPB):
                            if k:
                                pool.wait_ge(x_summed, TOPK * TPB * b + t + 1)
                            pool.wait_ge(scaled, TOPK * TPB * b + TPB * k + t + 1)
                            nc.gpsimd.tensor_tensor(x[:, t, :], x[:, t, :], got[:, TPB * (b + b0) + t, k, :],
                                                    ALU.add).then_inc(x_summed, 1)
                for t in range(TPB):
                    pool.wait_ge(var_ready, TPB * b + t + 1)
                    nc.gpsimd.tensor_tensor(rsy[:, t % 2:t % 2 + 1], vey[:, t % 2:t % 2 + 1], half[:], ALU.pow
                                            ).then_inc(rstd_ready, 1)
            for q in range(2 if last_half else 4):
                pool.wait_ge(moved[q], 32 * TPB * (2 if last_half else 1))

        @block.tensor
        def _(pe):
            mm, tr = nc.tensor.matmul, nc.tensor.transpose
            with pe.Fori(0, NB) as b:
                def t_bank(un):
                    n = T_AT[un]
                    hold(pe, pe_held, t_taken, T_N * b + n + 1)
                    return T[n % 2]

                def taken_t(un):
                    return t_taken, T_N * b + T_AT[un] + 1 + 2

                for un in ORDER:
                    kind, n = un
                    if un in pr.at:
                        pe.wait_ge(*pr.is_free(b, un))
                        o = banks[pr.bank(un)]
                    if kind == "UT":
                        pe.wait_ge(u_ready, TPB * b + 2 * n + 2)
                        o = t_bank(un)
                        for c in range(DC):
                            for t in range(2):
                                last = tr(o[:, (2 * c + t) * P:(2 * c + t + 1) * P], u[:, 2 * n + t, c * P:(c + 1) * P], ident[:])
                        last.then_inc(t_done, 1)
                        continue
                    if kind == "HT":
                        if n == 0:
                            pe.wait_ge(rotated, b + 1)
                        o = t_bank(un)
                        for t in range(4):
                            pair = heads[:, 4 * (n % 2) + t, 2 * (n // 2):2 * (n // 2) + 2, :].rearrange("p h d -> p (h d)")
                            last = tr(o[:, t * P:(t + 1) * P], pair, ident[:])
                        last.then_inc(t_done, 1)
                        continue
                    if kind == "QK":
                        pe.wait_ge(*taken_t(("UT", 3)))
                        for t in range(TPB):
                            for c in range(DC):
                                last = mm(o[:, t * QK:(t + 1) * QK], uT[:, c, t * P:(t + 1) * P], wqk1[:, c, :],
                                          start=(c == 0), stop=(c == DC - 1))
                    elif kind == "VV":
                        for c in range(DC):
                            last = mm(o, uT[:, c, n * P:(n + 1) * P], wv1[:, c, :], start=(c == 0), stop=(c == DC - 1))
                    elif kind == "LK":
                        pe.wait_ge(v_ready, TPB * b + TPB)
                        for t in range(TPB):
                            last = mm(o, heads[:, t, 2:4, :].rearrange("p h d -> p (h d)"), v[:, t, :],
                                      start=(t == 0), stop=(t == TPB - 1))
                    elif kind == "AT":
                        if n == 0:
                            pe.wait_ge(*taken_t(("HT", 3)))
                            pe.wait_ge(zeros_ready, 1)
                        for t in range(4):
                            at = slice((4 * n + t) * P, (4 * n + t + 1) * P)
                            last = mm(o[:, t * P:(t + 1) * P], headT[:, 1, at], headT[:, 0, at], start=True, stop=True)
                    elif kind == "GA":
                        h, e = n // EC, n % EC
                        for c in range(DC):
                            last = mm(o, wg1[:, c, e * P:(e + 1) * P], uT[:, c, h * 512:(h + 1) * 512],
                                      start=(c == 0), stop=(c == DC - 1))
                    elif kind == "OO":
                        h, e = n // EC, n % EC
                        if n == 0:
                            pe.wait_ge(*pr.is_taken(b, ("LK", 0)))
                            pe.wait_ge(att_ready, 2 * b + 2)
                        mm(o, lkv[:, e * P:(e + 1) * P], headT[:, 0, h * 512:(h + 1) * 512], start=True, stop=False)
                        for t in range(4):
                            last = mm(o[:, t * P:(t + 1) * P], v[:, 4 * h + t, e * P:(e + 1) * P], att[:, 4 * h + t, :],
                                      start=False, stop=(t == 3))
                    elif kind == "YY":
                        pe.wait_ge(*pr.is_taken(b, ("OO", 3 if n < 4 else 7)))
                        for e in range(EC):
                            mm(o[:, 0:DIM], oT[:, e, (n % 4) * P:(n % 4 + 1) * P], wo1[:, e, :],
                               start=(e == 0), stop=False)
                        last = mm(o[:, 0:DIM], ones[:], row("L1_attn_bo")[0:1, :], start=False, stop=True)
                    last.then_inc(g_done, 1)

        @block.scalar
        def _(act):
            def copy(o, i, scale=1.0):
                return nc.scalar.activation(o, i, ACT.Copy, scale=scale)

            act.sem_inc(t_taken, 2)
            act.sem_inc(by_act, pr.count["act"])
            with act.Fori(0, NB) as b:
                act.wait_ge(xn_in, 16 * b + 16)
                for t in range(TPB):
                    copy(u[:, t, :], u[:, t, :], keep["r2"][:, bass.ds(TPB * (b + b0) + t, 1)]).then_inc(u_ready, 1)
                for un in ORDER:
                    kind, n = un
                    if kind in ("UT", "HT"):
                        k = T_AT[un]
                        act.wait_ge(t_done, T_N * b + k + 1)
                        o = T[k % 2]
                        if kind == "UT":
                            copy(uT[:, :, 2 * n * P:(2 * n + 2) * P], o[:].rearrange("p (c t) -> p c t", c=DC)).then_inc(t_taken, 1)
                        else:
                            rows_of = P if n < 2 else QK
                            copy(headT[0:rows_of, n // 2, (n % 2) * 512:(n % 2 + 1) * 512], o[0:rows_of, :]).then_inc(t_taken, 1)
                    elif kind == "QK":
                        act.wait_ge(*pr.is_taken(b, un))
                        nc.scalar.activation(qk[:], qk[:], ACT.Silu).then_inc(qk_ready, 1)
                    elif kind == "VV":
                        act.wait_ge(*pr.is_taken(b, un))
                        nc.scalar.activation(v[:, n, :], v[:, n, :], ACT.Silu).then_inc(v_ready, 1)
                    elif kind == "LK":
                        act.wait_ge(*pr.is_done(b, un))
                        copy(lkv[QK:, :], banks[pr.bank(un)][QK:, :], 1.0 / SEQ).then_inc(by_act, 1)
                        if last_half:
                            act.wait_ge(moved[1], 32 * TPB * (b + 1))
                            for k in range(TOPK):
                                for t in range(TPB):
                                    tile = TPB * (b + b0) + t
                                    g = got[:, bass.ds(tile, 1), k, :].rearrange("p o d -> p (o d)")
                                    copy(g, g, keep["gates"][:, k, bass.ds(tile, 1)]).then_inc(scaled, 1)
                    elif kind == "GA":
                        act.wait_ge(*pr.is_done(b, un))
                        if n >= 4:
                            act.wait_ge(*pr.is_taken(b, ("OO", n - 4)))
                        nc.scalar.activation(gT[:, n % 4, :], banks[pr.bank(un)], ACT.Silu,
                                             bias=cols[:, 4 + n % EC:5 + n % EC]).then_inc(by_act, 1)

        @block.vector
        def _(dve):
            steps = [0]
            tt, ts, stt = nc.vector.tensor_tensor, nc.vector.tensor_scalar, nc.vector.scalar_tensor_tensor
            V_N = VB[last_half]

            def own(ins):
                steps[0] += 1
                ins.then_inc(v_step, 1)
                hold(dve, v_held, v_step, V_N * b + steps[0])

            nc.vector.memset(ones[:], 1.0)
            nc.vector.memset(headT[QK:, 1, :], 0.0)
            nc.vector.memset(lkv[0:QK, :], 0.0).then_inc(zeros_ready, 1)
            dve.sem_inc(by_dve, pr.count["dve"])
            with dve.Fori(0, NB) as b:
                def finish(t):
                    i = t % 2
                    dve.wait_ge(rstd_ready, TPB * b + t + 1)
                    ts(y[:, i, :], banks[pr.bank(("YY", t))][:, 0:DIM], mvy[:, i, 0:1], rsy[:, i:i + 1],
                       ALU.subtract, ALU.mult).then_inc(by_dve, 1)
                    hold(dve, v_held, *pr.is_taken(b, ("YY", t)))
                    own(tt(y[:, i, :], y[:, i, :], row("L1_attn_ln2_w"), ALU.mult))
                    if last_half:
                        hold(dve, v_held, x_summed, TOPK * TPB * b + TPB + t + 1)
                    return tt(x[:, t, :], x[:, t, :], y[:, i, :], ALU.add)

                def add_experts(target, tile, t):
                    for k in range(TOPK):
                        g = got[:, bass.ds(tile + t, 1), k, :].rearrange("p o d -> p (o d)")
                        own(stt(out=target[:, t, :], in0=g, scalar=keep["gates"][:, k, bass.ds(tile + t, 1)],
                                in1=target[:, t, :], op0=ALU.mult, op1=ALU.add))

                def experts_after(un):
                    kind, n = un
                    if kind == "LK":
                        dve.wait_ge(z_in, 16 * b + 16)
                        hold(dve, v_held, moved[0], 32 * TPB * (b + 1))
                        for t in range(4):
                            add_experts(zx, TPB * b, t)
                    elif un[0] == "OO" and n < 4:
                        add_experts(zx, TPB * b, 4 + n)
                        if n == 3:
                            dve.sem_inc(z_ready, 1)
                for un in ORDER:
                    kind, n = un
                    if un in pr.at and pr.who[un] == "dve":
                        dve.wait_ge(*pr.is_done(b, un))
                        o = banks[pr.bank(un)]
                    if kind == "QK":
                        tt(qk[:], o.rearrange("p (t d) -> p t d", d=QK),
                           row("L1_attn_bqk").unsqueeze(1).to_broadcast([P, TPB, QK]), ALU.add).then_inc(by_dve, 1)
                    elif kind == "VV":
                        tt(v[:, n, :], o, row("L1_attn_bv"), ALU.add).then_inc(by_dve, 1)
                        if n == 1:
                            shape = [P, TPB, 4, QK]
                            dve.wait_ge(qk_ready, b + 1)
                            gam = row("L1_attn_gamma").rearrange("p (h d) -> p h d", d=QK).unsqueeze(1).to_broadcast(shape)
                            own(tt(heads[:], qk[:].unsqueeze(2).to_broadcast(shape), gam, ALU.mult))
                        if n == 2:
                            bet = row("L1_attn_beta").rearrange("p (h d) -> p h d", d=QK).unsqueeze(1).to_broadcast(shape)
                            own(tt(heads[:], heads[:], bet, ALU.add))
                        hq = QK // 2
                        tmp = u[:].rearrange("p t (h d) -> p t h d", d=QK)
                        if n == 3:
                            dve.wait_ge(t_taken, T_N * b + T_AT[("UT", 3)] + 1 + 2)
                            for d0, d1 in ((0, hq), (hq, 0)):
                                sn = rope[:, 1, :, d0:d0 + hq].unsqueeze(2).to_broadcast([P, TPB, 4, hq])
                                last = tt(tmp[:, :, :, d0:d0 + hq], heads[:, :, :, d1:d1 + hq], sn, ALU.mult)
                            own(last)
                        if n == 4:
                            own(tt(heads[:], heads[:], rope[:, 0, :, :].unsqueeze(2).to_broadcast(shape), ALU.mult))
                        if n == 5:
                            tt(heads[:], heads[:], tmp, ALU.add).then_inc(rotated, 1)
                        if n == 6:
                            hold(dve, v_held, x_in, 16 * b + 16)
                            own(tt(x[:], x[:], row("L1_attn_ln2_b").unsqueeze(1).to_broadcast([P, TPB, DIM]), ALU.add))
                            if last_half:
                                dve.sem_inc(x_biased, 1)
                    elif kind == "AT":
                        biased = keep["bias"][:].unsqueeze(1).to_broadcast([P, 4, P])
                        same = keep["same"][:].unsqueeze(1).to_broadcast([P, 4, P])
                        if n:
                            dve.wait_ge(att_ready, 2 * b + n)
                        stt(out=attw[:], in0=o.rearrange("p (t i) -> p t i", i=P), scalar=1.0 / GROUP, in1=biased,
                            op0=ALU.mult, op1=ALU.add).then_inc(by_dve, 1)
                        dve.wait_ge(*pr.is_taken(b, un))
                        own(stt(out=attw[:], in0=attw[:], scalar=0.0, in1=same, op0=ALU.max, op1=ALU.mult))
                        tt(att[:, 4 * n:4 * n + 4, :], attw[:], attw[:], ALU.mult).then_inc(att_ready, 1)
                    elif kind == "OO":
                        dve.wait_ge(*pr.is_taken(b, ("GA", n)))
                        tt(oT[:, n % EC, :], o, gT[:, n % 4, :], ALU.mult).then_inc(by_dve, 1)
                    elif kind == "YY":
                        i = n % 2
                        own(nc.vector.bn_stats(sty[:, i, :], o[:, 0:DIM]))
                        own(nc.vector.bn_aggr(mvy[:, i, :], sty[:, i, :]))
                        ts(vey[:, i:i + 1], mvy[:, i, 1:2], EPS, None, ALU.add).then_inc(var_ready, 1)
                        if n not in (0, 4):
                            own(finish(n - 1))
                        if n == 3:
                            own(finish(n))
                    if last_half:
                        experts_after(un)
                finish(TPB - 1).then_inc(x_ready, 1)
                assert steps[0] == V_N, steps[0]


def load_expert(pool, io, keep, scr, j):
    arrived = keep["expert_in"][j % 2]
    e = pool.value_load(keep["rank_expert"][0:1, j:j + 1], min_val=0, max_val=E - 1)
    pool.dma_start(keep["experts"][:, j % 2, :, :].bitcast(F32),
                   scr["experts"][bass.ds(e, 1)].rearrange("e p h n -> (e p) h n")).then_inc(arrived, 16)
    pool.dma_start(keep["expert_bias"][:, j % 2, :],
                   io["expert_bias"][bass.ds(e, 1), :].to_broadcast([P, BIASES])).then_inc(arrived, 16)


def moe(nc, io, keep, scr, psum):
    ctx = ExitStack()

    def sb(name, shape, dt=F32):
        return ctx.enter_context(nc.sbuf_tensor(name, shape, dt))

    def sem(name):
        return ctx.enter_context(nc.semaphore(name))

    B = psum["T"] + psum["G"]
    W = [w[:, k:k + 512] for w in psum["S"] for k in (0, 512)]
    T = B[0:2]
    YB = [B[2][:, 0:DIM], B[3][:, 0:DIM]]
    H = [(W[0], W[1]), (W[2], W[3])]
    ident, experts, table = keep["ident"], keep["experts"], keep["tile_rank"]
    brow = keep["expert_bias"]
    ROUND = 8
    RING = 4
    TURNS = ROUND // RING
    with ctx:
        xs = sb("xs_ring", [P, ROUND, DIM])
        xT = sb("xsT", [P, 2, 2, DC, P], F32R)
        h1 = sb("h1", [P, 2, HID])
        h3 = sb("h3", [P, 2, HID])
        g = sb("g", [P, 2, HID])
        gT = sb("gsT", [P, 2, 2, HC, P], F32R)
        y = sb("ys_ring", [P, RING, DIM])
        expert_ready, loader_held = sem("expert_ready"), keep["held"]["gpsimd"]
        x_high, g_high = sem("slots_high_ready"), sem("gated_high_ready")
        x_in = [sem(f"slots_in{i}") for i in range(ROUND)]
        y_out = [sem(f"slots_out{i}") for i in range(RING)]
        xt_done, xt_taken = sem("slots_transposed"), sem("slots_transposes_taken")
        h_done, h1_ready, h_taken, s_ready, g_ready = (sem("hidden_done"), sem("h1_biased"), sem("hidden_taken"),
                                                       sem("silu_ready"), sem("gated"))
        gt_done, gt_taken = sem("gated_transposed"), sem("gated_transposes_taken")
        y_done, y_taken = sem("expert_out_done"), sem("expert_out_taken")
        block = ctx.enter_context(nc.Block())
        xs_d = scr["xs"].rearrange("(s p) d -> s p d", p=P)
        ys_d = scr["ys"].rearrange("(s p) d -> s p d", p=P)
        ROUNDS = SLOTS_T // ROUND
        assert ROUNDS * ROUND == SLOTS_T

        def expert(eng, s):
            return eng.value_load(table[0:1, bass.ds(s, 1)], min_val=0, max_val=E - 1)

        def every_tile(eng, step):
            with eng.Fori(0, ROUNDS - 1) as r:
                for k in range(ROUND):
                    step(ROUND * r + k, r, k, False)
            for k in range(ROUND):
                step(ROUND * (ROUNDS - 1) + k, ROUNDS - 1, k, True)

        @block.sync
        def _(sp):
            for k in range(ROUND):
                sp.dma_start(xs[:, k, :], xs_d[k]).then_inc(x_in[k], 16)
            load_rows(sp, keep, scr, "u", BATCH // 2, 0)
            sp.wait_ge(keep["stored"], 16 * BATCH // 2 + 16)
            load_rows(sp, keep, scr, "x", BATCH // 2, 0)
            for k in range(RING):
                sp.sem_inc(y_out[k], 16)

            def step(s, r, k, last):
                if not last:
                    sp.wait_ge(xt_done, s + 1)
                    sp.dma_start(xs[:, k, :], xs_d[bass.ds(s + ROUND, 1)].rearrange("o p d -> p (o d)")).then_inc(x_in[k], 16)
                sp.wait_ge(y_taken, s + 1 + 2)
                sp.dma_start(ys_d[bass.ds(s, 1)].rearrange("o p d -> p (o d)"), y[:, k % RING, :]).then_inc(y_out[k % RING], 16)

            every_tile(sp, step)
            for k in range(RING):
                sp.wait_ge(y_out[k], 16 * TURNS * ROUNDS + 16)

        @block.gpsimd
        def _(pool):
            for e in range(E):
                if e >= 2:
                    end = pool.value_load(keep["rank_end"][0:1, e - 2:e - 1], min_val=0, max_val=SLOTS_T)
                    hold(pool, loader_held, y_taken, end + 2)
                    load_expert(pool, io, keep, scr, e)
                pool.wait_ge(keep["expert_in"][e % 2], 32 * (e // 2 + 1))
                pool.sem_inc(expert_ready, 1)

        @block.tensor
        def _(pe):
            mm, tr = nc.tensor.matmul, nc.tensor.transpose

            def rows(s, r, k):
                pe.wait_ge(x_in[k], 16 * (r + 1))
                pe.wait_ge(xt_taken, s + 1)
                for c in range(DC):
                    last = tr(T[0][:, c * P:(c + 1) * P], xs[:, k, c * P:(c + 1) * P], ident[:])
                last.then_inc(xt_done, 1)

            def times(o, parts, e, at, n, first, last):
                for q, (i, w) in enumerate(((0, 0), (0, 1), (1, 0))):
                    moving = experts[:, bass.ds(e % 2, 1), w, at:at + n].rearrange("p o n -> p (o n)")
                    ins = mm(o, parts[i], moving, start=(first and q == 0), stop=(last and q == 2))
                return ins

            def hidden(s, k, e, m):
                if m == 0:
                    pe.wait_ge(xt_taken, s + 1 + 1)
                    pe.wait_ge(h_taken, s + 1)
                    pe.wait_ge(expert_ready, e + 1)
                for c in range(DC):
                    last = times(H[k % 2][m], [xT[:, k % 2, i, c, :] for i in range(2)], e, (DC * m + c) * HID, HID,
                                 c == 0, c == DC - 1)
                last.then_inc(h_done, 1)

            current = [None]
            rows(0, 0, 0)
            rows(1, 0, 1)
            first = expert(pe, 0)
            hidden(0, 0, first, 0)
            hidden(0, 0, first, 1)

            def step(s, r, k, last):
                following = not last or k + 1 < ROUND
                if not last or k + 2 < ROUND:
                    rows(s + 2, r + (k + 2) // ROUND, (k + 2) % ROUND)
                e = expert(pe, s) if k == 0 else current[0]
                if following:
                    current[0] = expert(pe, s + 1)
                pe.wait_ge(g_ready, s + 1)
                pe.wait_ge(gt_taken, s + 1)
                for c in range(HC):
                    ins = tr(T[1][:, c * P:(c + 1) * P], g[:, k % 2, c * P:(c + 1) * P], ident[:])
                ins.then_inc(gt_done, 1)
                if following:
                    hidden(s + 1, k + 1, current[0], 0)
                    hidden(s + 1, k + 1, current[0], 1)
                pe.wait_ge(gt_taken, s + 1 + 1)
                pe.wait_ge(y_taken, s + 1)
                for c in range(HC):
                    ins = times(YB[k % 2], [gT[:, k % 2, i, c, :] for i in range(2)], e, 2 * DC * HID + c * DIM, DIM,
                                c == 0, c == HC - 1)
                ins.then_inc(y_done, 1)

            every_tile(pe, step)

        @block.scalar
        def _(act):
            def copy(o, i):
                return nc.scalar.activation(o, i, ACT.Copy)

            def rows(s, k):
                act.wait_ge(xt_done, s + 1)
                copy(xT[:, k % 2, 0, :, :].rearrange("p c q -> p (c q)"), T[0][:, 0:DIM]).then_inc(x_high, 1)

            def silu(s, k):
                act.wait_ge(h1_ready, s + 1)
                nc.scalar.activation(h1[:, k % 2, :], h1[:, k % 2, :], ACT.Silu).then_inc(s_ready, 1)

            rows(0, 0)
            rows(1, 1)
            silu(0, 0)

            def step(s, r, k, last):
                if not last or k + 2 < ROUND:
                    rows(s + 2, k)
                act.wait_ge(gt_done, s + 1)
                copy(gT[:, k % 2, 0, :, :].rearrange("p c q -> p (c q)"), T[1][:]).then_inc(g_high, 1)
                if not last or k + 1 < ROUND:
                    silu(s + 1, k + 1)

            every_tile(act, step)

        @block.vector
        def _(dve):
            tt = nc.vector.tensor_tensor

            def bias(e, at, n):
                return brow[:, bass.ds(e % 2, 1), at:at + n].rearrange("p o n -> p (o n)")

            def low(parts, bank, high, taken, s):
                dve.wait_ge(high, s + 1)
                flat = [parts[i].rearrange("p c q -> p (c q)") for i in range(2)]
                tt(flat[1], bank, flat[0], ALU.subtract).then_inc(taken, 1)

            def rows(s, k):
                low([xT[:, k % 2, i, :, :] for i in range(2)], T[0][:, 0:DIM], x_high, xt_taken, s)

            def h1_bias(s, k):
                e = expert(dve, s)
                dve.wait_ge(expert_ready, e + 1)
                dve.wait_ge(h_done, 2 * s + 1)
                tt(h1[:, k % 2, :], H[k % 2][0], bias(e, 0, HID), ALU.add).then_inc(h1_ready, 1)
                return e

            def gate(s, k, e):
                i = k % 2
                dve.wait_ge(h_done, 2 * s + 2)
                tt(h3[:, i, :], H[i][1], bias(e, HID, HID), ALU.add).then_inc(h_taken, 1)
                dve.wait_ge(h_taken, s + 1 + 2)
                dve.wait_ge(s_ready, s + 1)
                tt(g[:, i, :], h1[:, i, :], h3[:, i, :], ALU.mult).then_inc(g_ready, 1)

            dve.sem_inc(h_taken, 2)
            dve.sem_inc(y_taken, 2)
            dve.sem_inc(xt_taken, 1)
            dve.sem_inc(gt_taken, 1)
            rows(0, 0)
            rows(1, 1)
            gate(0, 0, h1_bias(0, 0))

            def step(s, r, k, last):
                following = not last or k + 1 < ROUND
                if not last or k + 2 < ROUND:
                    rows(s + 2, k)
                low([gT[:, k % 2, i, :, :] for i in range(2)], T[1][:], g_high, gt_taken, s)
                if following:
                    e1 = h1_bias(s + 1, k + 1)
                    gate(s + 1, k + 1, e1)
                e = expert(dve, s)
                dve.wait_ge(y_done, s + 1)
                dve.wait_ge(y_out[k % RING], 16 * (TURNS * r + k // RING) + 16)
                tt(y[:, k % RING, :], YB[k % 2], bias(e, 2 * HID, DIM), ALU.add).then_inc(y_taken, 1)

            every_tile(dve, step)


def constants():
    i = np.arange(P)
    distance = np.minimum(np.abs(i[:, None] - i[None, :]), MAXREL)
    same = i[:, None] // GROUP == i[None, :] // GROUP
    position = np.arange(SEQ, dtype=np.float32)
    half = QK // 2
    angle = position[:, None] * (10000.0 ** (-np.arange(half, dtype=np.float32) / half)).astype(np.float32)[None, :]
    cos, sin = np.cos(angle), np.sin(angle)
    rope = np.stack([np.concatenate([cos, cos], 1), np.concatenate([-sin, sin], 1)])
    f = np.float32
    return {
        "ident": np.eye(P, dtype=f),
        "causal": np.where(i[None, :] <= i[:, None], 0.0, MASKED).astype(f),
        "before": (i[:, None] < i[None, :]).astype(f),
        "ones": np.ones((P, P), f),
        "iota8": np.broadcast_to(np.arange(E, dtype=f), (P, E)),
        "iotaT": np.broadcast_to(np.arange(SLOTS_T, dtype=f), (P, SLOTS_T)),
        "band": ((distance[:, None, :] == np.arange(MAXREL + 1)[None, :, None]) & same[:, None, :]).astype(f),
        "same_group": same.astype(f),
        "rope": rope.reshape(2, TPB, P, QK).transpose(2, 0, 1, 3).astype(f),
    }


_INS = [
    "L0_attn_x", "L0_attn_Wq", "L0_attn_Wk", "L0_attn_Wv", "L0_attn_Wfc", "L0_attn_bfc",
    "L0_attn_gamma", "L0_attn_beta", "L0_ffn_W1", "L0_ffn_b1", "L0_ffn_W2", "L0_ffn_b2",
    "L1_attn_ln1_w", "L1_attn_ln1_b", "L1_attn_Wqk", "L1_attn_bqk", "L1_attn_Wv", "L1_attn_bv",
    "L1_attn_Wg", "L1_attn_bg", "L1_attn_Wo", "L1_attn_bo", "L1_attn_ln2_w", "L1_attn_ln2_b",
    "L1_attn_gamma", "L1_attn_beta", "L1_attn_pos_emb", "L1_ffn_Wg", "L1_ffn_W1", "L1_ffn_b1",
    "L1_ffn_A1", "L1_ffn_B1", "L1_ffn_W2", "L1_ffn_b2", "L1_ffn_A2", "L1_ffn_B2", "L1_ffn_W3",
    "L1_ffn_b3", "L1_ffn_A3", "L1_ffn_B3",
]


def kernel(**inputs):
    import concourse.bacc as _bacc
    from concourse.bass_utils import run_bass_kernel_spmd as _run

    nc = _bacc.Bacc("TRN2", target_bir_lowering=False, num_devices=1)
    arrays, io = {}, {}
    data = {n: np.asarray(inputs[n]) for n in _INS}
    laid = {"cols0": np.concatenate([data[n].reshape(-1, P) for n in ("L0_attn_gamma", "L0_attn_beta", "L0_ffn_b1")]).T,
            "cols1": np.concatenate([data[n].reshape(-1, P) for n in ("L1_attn_ln1_w", "L1_attn_ln1_b", "L1_attn_bg")]).T,
            "expert_bias": np.concatenate([data[n] for n in ("L1_ffn_b1", "L1_ffn_b3", "L1_ffn_b2")], 1)}
    for n in ("L0_attn_bfc", "L0_ffn_b2", "L1_attn_pos_emb", *ROWS1):
        data[n] = data[n].reshape(1, -1)
    for n, a in {**data, **laid, **constants()}.items():
        a = np.ascontiguousarray(a)
        arrays[f"in_{n}"] = a
        io[n] = nc.dram_tensor(f"in_{n}", a.shape, mybir.dt.from_np(a.dtype), kind="ExternalInput").ap()
    out = nc.dram_tensor("out_0_dram", (BATCH, SEQ, DIM), F32, kind="ExternalOutput").ap()
    build(nc, io, out)
    r = _run(nc, [arrays], core_ids=[0])
    return r.results[0]["out_0_dram"]
```
